# Optimizing a Trainium2 kernel written in Bass

```python
import numpy as np
import jax
import jax.numpy as jnp

def _softmax(x, axis=-1):
    return jax.nn.softmax(x, axis=axis)

def _gelu(x):
    return jax.nn.gelu(x, approximate=True)

def _silu(x):
    return jax.nn.silu(x)

def _sigmoid(x):
    return jax.nn.sigmoid(x)

def _layernorm(x, axis=-1, eps=1e-05):
    m = jnp.mean(x, axis=axis, keepdims=True)
    v = jnp.var(x, axis=axis, keepdims=True)
    return (x - m) / jnp.sqrt(v + eps)

def _scatter_add(tgt, idx, src, axis=0):
    return tgt.at[idx].add(src)

def _segment_sum(src, seg, n):
    return jax.ops.segment_sum(src, seg, n)
kernel_name = 'mk_vit_tower_d1_tok_img512_r4_383f45'

def setup_inputs(seed: int=0):
    np.random.seed(seed)
    _w = jnp.asarray

    def _rec_inputs():
        import jax
        import jax.numpy as jnp
        _rk = jax.random.key(seed)
        x = -0.000147625 + 0.999875 * jax.random.normal(jax.random.fold_in(_rk, 1), (128, 3, 224, 224), jnp.float32)
        return x
    x = _rec_inputs()

    def _L0_tok_setup():
        import jax, jax.numpy as jnp
        import numpy as np
        N_PATCHES = 8
        PATCH = 28
        C = 3
        IN_D = C * PATCH * PATCH
        HID = 128
        SEQ = N_PATCHES * N_PATCHES + 1

        def _positional_embedding(seq_len, dim):
            i = np.arange(seq_len)[:, None].astype(np.float32)
            j = np.arange(dim)[None, :].astype(np.float32)
            ang = i / np.power(100000.0, j / dim)
            pe = np.where(j % 2 == 0, np.sin(ang), np.cos(ang))
            return jnp.asarray(pe, dtype=jnp.float32)
        key = jax.random.key(seed)
        k1, k2, k3, k4 = jax.random.split(key, 4)
        B = 64
        X = jax.random.normal(k1, (B, C, 224, 224), dtype=jnp.float32)
        bound = 1.0 / np.sqrt(IN_D)
        W = jax.random.uniform(k2, (HID, IN_D), minval=-bound, maxval=bound, dtype=jnp.float32)
        b = jax.random.uniform(k3, (HID,), minval=-bound, maxval=bound, dtype=jnp.float32)
        class_token = jax.random.uniform(k4, (1, HID), dtype=jnp.float32)
        pos_embed = _positional_embedding(SEQ, HID)
        return {'X': X, 'W': W, 'b': b, 'class_token': class_token, 'pos_embed': pos_embed}
    _L0_tok_all = _L0_tok_setup()
    _L0_tok_in = {k: v for k, v in _L0_tok_all.items() if k in ('W', 'b', 'class_token', 'pos_embed')}
    del _L0_tok_all

    def _L0_attn_setup():
        import jax, jax.numpy as jnp
        import numpy as np
        import math
        D_MODEL = 128
        D_STATE = 8
        D_CONV = 3
        EXPAND = 1
        D_INNER = EXPAND * D_MODEL
        D_HALF = D_INNER // 2
        DT_RANK = math.ceil(D_MODEL / 16)
        B_SZ, L_SEQ = (4, 1024)

        def _silu(x):
            return x * jax.nn.sigmoid(x)

        def _dwconv_same(x_bcl, w):
            return jax.lax.conv_general_dilated(x_bcl, w, window_strides=(1,), padding='SAME', feature_group_count=x_bcl.shape[1], dimension_numbers=('NCH', 'OIH', 'NCH'))

        def _selective_scan(u_bld, delta_bld, A_dn, B_bln, C_bln, D_d):
            dA = jnp.exp(delta_bld[..., None] * A_dn[None, None])
            dBu = delta_bld[..., None] * B_bln[:, :, None, :] * u_bld[..., None]
            b, l, d, n = dA.shape
            dA_t = jnp.moveaxis(dA, 1, 0)
            dBu_t = jnp.moveaxis(dBu, 1, 0)
            C_t = jnp.moveaxis(C_bln, 1, 0)

            def step(x, inp):
                dA_i, dBu_i, C_i = inp
                x = dA_i * x + dBu_i
                y = jnp.einsum('bdn,bn->bd', x, C_i)
                return (x, y)
            x0 = jnp.zeros((b, d, n), dtype=u_bld.dtype)
            _, ys = jax.lax.scan(step, x0, (dA_t, dBu_t, C_t))
            y_bld = jnp.moveaxis(ys, 0, 1)
            return y_bld + u_bld * D_d[None, None, :]
        key = jax.random.key(seed)
        ks = jax.random.split(key, 10)
        xy = jax.random.normal(ks[0], (B_SZ, L_SEQ, D_MODEL), dtype=jnp.float32)
        in_proj_w = jax.random.normal(ks[1], (D_INNER, D_MODEL), dtype=jnp.float32) * 0.02
        conv_v_w = jax.random.normal(ks[2], (D_HALF, 1, D_CONV), dtype=jnp.float32) * 0.1
        conv_hs_w = jax.random.normal(ks[3], (D_HALF, 1, D_CONV), dtype=jnp.float32) * 0.1
        hs_proj_w = jax.random.normal(ks[4], (DT_RANK + 2 * D_STATE, D_HALF), dtype=jnp.float32) * 0.02
        dt_init_std = DT_RANK ** (-0.5)
        dt_proj_w = jax.random.uniform(ks[5], (D_HALF, DT_RANK), dtype=jnp.float32, minval=-dt_init_std, maxval=dt_init_std)
        dt = jnp.exp(jax.random.uniform(ks[6], (D_HALF,), dtype=jnp.float32) * (math.log(0.1) - math.log(0.001)) + math.log(0.001))
        dt = jnp.clip(dt, 0.0001, None)
        dt_proj_b = dt + jnp.log(-jnp.expm1(-dt))
        A_log = jnp.log(jnp.broadcast_to(jnp.arange(1, D_STATE + 1, dtype=jnp.float32), (D_HALF, D_STATE)))
        D_param = jnp.ones((D_HALF,), dtype=jnp.float32)
        out_proj_w = jax.random.normal(ks[7], (D_MODEL, D_INNER), dtype=jnp.float32) * 0.02
        return {'xy': xy, 'in_proj_w': in_proj_w, 'conv_v_w': conv_v_w, 'conv_hs_w': conv_hs_w, 'hs_proj_w': hs_proj_w, 'dt_proj_w': dt_proj_w, 'dt_proj_b': dt_proj_b, 'A_log': A_log, 'D_param': D_param, 'out_proj_w': out_proj_w}
    _L0_attn_all = _L0_attn_setup()
    _L0_attn_in = {k: v for k, v in _L0_attn_all.items() if k in ('in_proj_w', 'conv_v_w', 'conv_hs_w', 'hs_proj_w', 'dt_proj_w', 'dt_proj_b', 'A_log', 'D_param', 'out_proj_w')}
    del _L0_attn_all

    def _L0_ffn_setup():
        import jax, jax.numpy as jnp
        import numpy as np
        EPS = 1e-09
        LN_EPS = 1e-05

        def _layernorm(x, gamma):
            x = x.astype(jnp.float32)
            mu = jnp.mean(x, axis=-1, keepdims=True)
            var = jnp.var(x, axis=-1, keepdims=True)
            return (x - mu) * jax.lax.rsqrt(var + LN_EPS) * gamma
        key = jax.random.key(seed)
        ks = jax.random.split(key, 5)
        b, n, d, e, h = (4, 256, 128, 6, 512)
        x = jax.random.normal(ks[0], (b, n, d), dtype=jnp.float32)
        w_gating = jax.random.normal(ks[1], (d, e), dtype=jnp.float32)
        std1 = 1.0 / np.sqrt(h)
        std2 = 1.0 / np.sqrt(d)
        w1 = jax.random.uniform(ks[2], (e, d, h), jnp.float32, -std1, std1)
        w2 = jax.random.uniform(ks[3], (e, h, d), jnp.float32, -std2, std2)
        gamma = jnp.ones((d,), dtype=jnp.float32)
        return {'x': x, 'w_gating': w_gating, 'gamma': gamma, 'w1': w1, 'w2': w2}
    _L0_ffn_all = _L0_ffn_setup()
    _L0_ffn_in = {k: v for k, v in _L0_ffn_all.items() if k in ('w_gating', 'gamma', 'w1', 'w2')}
    del _L0_ffn_all
    return {'x': x, 'L0_tok_W': _L0_tok_in['W'], 'L0_tok_b': _L0_tok_in['b'], 'L0_tok_class_token': _L0_tok_in['class_token'], 'L0_tok_pos_embed': _L0_tok_in['pos_embed'], 'L0_attn_in_proj_w': _L0_attn_in['in_proj_w'], 'L0_attn_conv_v_w': _L0_attn_in['conv_v_w'], 'L0_attn_conv_hs_w': _L0_attn_in['conv_hs_w'], 'L0_attn_hs_proj_w': _L0_attn_in['hs_proj_w'], 'L0_attn_dt_proj_w': _L0_attn_in['dt_proj_w'], 'L0_attn_dt_proj_b': _L0_attn_in['dt_proj_b'], 'L0_attn_A_log': _L0_attn_in['A_log'], 'L0_attn_D_param': _L0_attn_in['D_param'], 'L0_attn_out_proj_w': _L0_attn_in['out_proj_w'], 'L0_ffn_w_gating': _L0_ffn_in['w_gating'], 'L0_ffn_gamma': _L0_ffn_in['gamma'], 'L0_ffn_w1': _L0_ffn_in['w1'], 'L0_ffn_w2': _L0_ffn_in['w2']}

def reference(x, L0_tok_W, L0_tok_b, L0_tok_class_token, L0_tok_pos_embed, L0_attn_in_proj_w, L0_attn_conv_v_w, L0_attn_conv_hs_w, L0_attn_hs_proj_w, L0_attn_dt_proj_w, L0_attn_dt_proj_b, L0_attn_A_log, L0_attn_D_param, L0_attn_out_proj_w, L0_ffn_w_gating, L0_ffn_gamma, L0_ffn_w1, L0_ffn_w2):
    import jax
    import jax.numpy as jnp

    def _L0_tok_ref(X, W, b, class_token, pos_embed):
        import jax, jax.numpy as jnp
        import numpy as np
        N_PATCHES = 8
        PATCH = 28
        C = 3
        IN_D = C * PATCH * PATCH
        HID = 128
        SEQ = N_PATCHES * N_PATCHES + 1

        def _positional_embedding(seq_len, dim):
            i = np.arange(seq_len)[:, None].astype(np.float32)
            j = np.arange(dim)[None, :].astype(np.float32)
            ang = i / np.power(100000.0, j / dim)
            pe = np.where(j % 2 == 0, np.sin(ang), np.cos(ang))
            return jnp.asarray(pe, dtype=jnp.float32)
        B = X.shape[0]
        patches = X.reshape(B, C, N_PATCHES, PATCH, N_PATCHES, PATCH)
        patches = patches.transpose(0, 2, 4, 1, 3, 5).reshape(B, N_PATCHES * N_PATCHES, IN_D)
        tokens = jnp.einsum('bpi,hi->bph', patches, W) + b
        cls = jnp.broadcast_to(class_token[None, :, :], (B, 1, HID))
        tokens = jnp.concatenate([cls, tokens], axis=1)
        return tokens * pos_embed[None, :, :]

    def _L0_attn_ref(xy, in_proj_w, conv_v_w, conv_hs_w, hs_proj_w, dt_proj_w, dt_proj_b, A_log, D_param, out_proj_w):
        import jax, jax.numpy as jnp
        import numpy as np
        import math
        D_MODEL = 128
        D_STATE = 8
        D_CONV = 3
        EXPAND = 1
        D_INNER = EXPAND * D_MODEL
        D_HALF = D_INNER // 2
        DT_RANK = math.ceil(D_MODEL / 16)
        B_SZ, L_SEQ = (4, 1024)

        def _silu(x):
            return x * jax.nn.sigmoid(x)

        def _dwconv_same(x_bcl, w):
            return jax.lax.conv_general_dilated(x_bcl, w, window_strides=(1,), padding='SAME', feature_group_count=x_bcl.shape[1], dimension_numbers=('NCH', 'OIH', 'NCH'))

        def _selective_scan(u_bld, delta_bld, A_dn, B_bln, C_bln, D_d):
            dA = jnp.exp(delta_bld[..., None] * A_dn[None, None])
            dBu = delta_bld[..., None] * B_bln[:, :, None, :] * u_bld[..., None]
            b, l, d, n = dA.shape
            dA_t = jnp.moveaxis(dA, 1, 0)
            dBu_t = jnp.moveaxis(dBu, 1, 0)
            C_t = jnp.moveaxis(C_bln, 1, 0)

            def step(x, inp):
                dA_i, dBu_i, C_i = inp
                x = dA_i * x + dBu_i
                y = jnp.einsum('bdn,bn->bd', x, C_i)
                return (x, y)
            x0 = jnp.zeros((b, d, n), dtype=u_bld.dtype)
            _, ys = jax.lax.scan(step, x0, (dA_t, dBu_t, C_t))
            y_bld = jnp.moveaxis(ys, 0, 1)
            return y_bld + u_bld * D_d[None, None, :]
        b, l, _ = xy.shape
        xy_p = xy @ in_proj_w.T
        xy_p = jnp.swapaxes(xy_p, 1, 2)
        v, hs = jnp.split(xy_p, 2, axis=1)
        A = -jnp.exp(A_log)
        v = _silu(_dwconv_same(v, conv_v_w))
        hs = _silu(_dwconv_same(hs, conv_hs_w))
        hs_bld = jnp.swapaxes(hs, 1, 2)
        x_dbl = hs_bld @ hs_proj_w.T
        dt, Bm, Cm = jnp.split(x_dbl, [DT_RANK, DT_RANK + D_STATE], axis=-1)
        dt = dt @ dt_proj_w.T + dt_proj_b
        delta = jax.nn.softplus(dt + dt_proj_b)
        y = _selective_scan(hs_bld, delta, A, Bm, Cm, D_param)
        v_bld = jnp.swapaxes(v, 1, 2)
        z = jnp.concatenate([v_bld, y], axis=-1)
        return z @ out_proj_w.T

    def _L0_ffn_ref(x, w_gating, gamma, w1, w2):
        import jax, jax.numpy as jnp
        import numpy as np
        EPS = 1e-09
        LN_EPS = 1e-05

        def _layernorm(x, gamma):
            x = x.astype(jnp.float32)
            mu = jnp.mean(x, axis=-1, keepdims=True)
            var = jnp.var(x, axis=-1, keepdims=True)
            return (x - mu) * jax.lax.rsqrt(var + LN_EPS) * gamma
        b, n, d = x.shape
        E = w_gating.shape[-1]
        C = max(min(n, int(n * 6.0 / E)), 4)
        raw = jnp.einsum('bnd,de->bne', x, w_gating)
        probs = jax.nn.softmax(raw, axis=-1)
        gate1 = jnp.max(probs, axis=-1)
        idx1 = jnp.argmax(probs, axis=-1)
        mask1 = jax.nn.one_hot(idx1, E, dtype=jnp.float32)
        gates_wo1 = probs * (1.0 - mask1)
        gate2 = jnp.max(gates_wo1, axis=-1)
        denom = gate1 + gate2 + EPS
        gate1 = gate1 / denom
        pos1 = (jnp.cumsum(mask1, axis=-2) - mask1) * mask1
        mask1 = mask1 * (pos1 < float(C)).astype(jnp.float32)
        mask1_flat = jnp.sum(mask1, axis=-1)
        pos1_flat = jnp.sum(pos1, axis=-1).astype(jnp.int32)
        gate1 = gate1 * mask1_flat
        combine = gate1[..., None, None] * mask1_flat[..., None, None] * jax.nn.one_hot(idx1, E, dtype=jnp.float32)[..., None] * jax.nn.one_hot(pos1_flat, C, dtype=jnp.float32)[..., None, :]
        dispatch = (combine != 0).astype(jnp.float32)
        expert_in = jnp.einsum('bnd,bnec->ebcd', x, dispatch)
        xn = _layernorm(expert_in, gamma)
        hidden = jax.nn.gelu(jnp.einsum('ebcd,edh->ebch', xn, w1), approximate=False)
        expert_out = jnp.einsum('ebch,ehd->ebcd', hidden, w2)
        out = jnp.einsum('ebcd,bnec->bnd', expert_out, combine)
        return out
    h = _L0_tok_ref(x, L0_tok_W, L0_tok_b, L0_tok_class_token, L0_tok_pos_embed)
    h = h + _L0_attn_ref(_layernorm(h, axis=-1), L0_attn_in_proj_w, L0_attn_conv_v_w, L0_attn_conv_hs_w, L0_attn_hs_proj_w, L0_attn_dt_proj_w, L0_attn_dt_proj_b, L0_attn_A_log, L0_attn_D_param, L0_attn_out_proj_w)
    h = h + _L0_ffn_ref(_layernorm(h, axis=-1), L0_ffn_w_gating, L0_ffn_gamma, L0_ffn_w1, L0_ffn_w2)
    return h

_drawn_inputs = setup_inputs


def setup_inputs(seed=0):
    import zlib

    import numpy as np

    out = dict(_drawn_inputs(seed))
    spreads = {'L0_attn_D_param': (1.0, 0.6), 'L0_ffn_gamma': (1.0, 0.2)}
    factors = {'L0_attn_conv_hs_w': 2.941,
     'L0_attn_hs_proj_w': 8.0,
     'L0_attn_dt_proj_w': 8.0,
     'L0_attn_dt_proj_b': 8.0,
     'L0_attn_A_log': 8.0}
    for name, (base, spread) in spreads.items():
        noise = np.random.default_rng([zlib.crc32(name.encode()), seed]).standard_normal(out[name].shape)
        drawn = base * np.exp(spread * noise) if base else spread * noise
        out[name] = jnp.asarray(drawn.astype(out[name].dtype))
    for name, factor in factors.items():
        out[name] = (out[name] * factor).astype(out[name].dtype)
    return out
```

```python
import concourse.bass as bass
from concourse import mybir
from concourse.alu_op_type import AluOpType as ALU
from contextlib import ExitStack

F32 = mybir.dt.float32
I32 = mybir.dt.int32
ACT = mybir.ActivationFunctionType
AX = mybir.AxisListType
ds = bass.ds

B, C, IMG = 128, 3, 224
NP, PATCH = 8, 28
K = C * PATCH * PATCH
D = 128
L = NP * NP + 1
G = 2
GB = B // G
HB = GB // 2
NS = 8
CH = D // 2
E = 6
H = 512
CL = 8
CW = CL * GB
NC = (L - 1) // CL
KT = -(-K // 128)
KR = K - (KT - 1) * 128
SK = 3
SLOTS = (KT - 1) // SK
TT = 4
NT = 1 + NC * TT
NX = 40
LW = L * HB
XW = LW // 5
SD = 2
NSC = 32 // SD
SEQ = SD * NS
EPS = 1e-5
GATE_EPS = 1e-9

C_ID, C_TRI, C_ONE, C_E8, C_K128, C_J = 0, 128, 256, 384, 390, 423
C_N = C_J + NX


def tower(nc, x_main, x_rem, w_main, w_rem, tok_b, cls, pos, w_in, cw_v, cw_h, w_hs, w_dt, b_dt,
          a_log, d_par, w_out, w_gate, gamma, w1, w2, consts, out):
    ctx = ExitStack()
    with ctx:
        def sb(name, shape, dt=F32):
            return ctx.enter_context(nc.sbuf_tensor(name, shape, dt))

        def sem(name):
            return ctx.enter_context(nc.semaphore(name))

        ring = sb("ring", [128, SLOTS, SK * CW])
        ring_rem = sb("ring_rem", [KR, 2, CW])
        wt = sb("wt", [128, KT - 1, D])
        wt_rem = sb("wt_rem", [KR, D])
        cst = sb("cst", [128, C_N])
        col = sb("col", [128, 24])
        posT = sb("posT", [128, L])
        win = sb("win", [128, D])
        lhs_xd = sb("lhs_xd", [128, 128])
        lhs_dt = sb("lhs_dt", [128, 128])
        wo = sb("wo", [128, 4, D])
        wg = sb("wg", [128, E])
        atab = sb("atab", [128, 32 * NS])
        hT = sb("hT", [128, G * NC, CW])
        hC = sb("hC", [128, G, 128])
        stage = sb("stage", [128, CW])
        xn = sb("xn", [128, TT, D])
        h2s = sb("h2s", [128, TT, D])
        xnT = sb("xnT", [128, CW])
        bst = sb("bst", [128, TT, 6])
        mv = sb("mv", [128, TT, 2])
        ln = sb("ln", [128, 6, TT])
        mhalf = sb("mhalf", [128, TT])
        epsT = sb("epsT", [128, TT])
        vhc = sb("vhc", [128, 2, HB])
        vh = sb("vh", [128, 2, L + 2, HB])
        vz = sb("vz", [128, LW])
        uz = sb("uz", [128, LW])
        deltaT = sb("deltaT", [128, LW])
        duT = sb("duT", [128, LW])
        xdT = sb("xdT", [128, LW])
        yT = sb("yT", [128, LW])
        tA = sb("tA", [128, 2, SEQ * L])
        tB = sb("tB", [128, 2, SEQ * L])
        hid_a = sb("hid_a", [128, 2, H])
        hidT_a = sb("hidT_a", [128, 2, H])
        xeT_a = sb("xeT_a", [128, 2, 128])
        lg = sb("lg", [128, NT, E])
        rt = sb("rt", [128, 6, NT * E])
        r1 = sb("r1", [128, 8, NT])
        gate = sb("gate", [128, G, NT])
        slot = sb("slot", [128, G, NT], I32)
        tiles = sb("tiles", [128, 3, E])
        tcmp = sb("tcmp", [1, NX * E])
        tsum = sb("tsum", [1, NX])
        texp = sb("texp", [1, G, NX], I32)

        ps = [ctx.enter_context(nc.psum_tensor(f"ps{i}", [128, 512], F32)) for i in range(8)]
        psT = ps[0:2]
        psA, psB, psV = ps[2], ps[3], ps[4]
        psM = ps[5:7]
        psG = ps[7]

        h2d = nc.dram_tensor("h2_scratch", [G, 128, NT * D], F32).ap()
        xsd = nc.dram_tensor("expert_in_scratch", [G * NX * 128, D], F32).ap()
        ysd = nc.dram_tensor("expert_out_scratch", [G * NX * 128, D], F32).ap()

        flat_ring = ring[:, :, :].rearrange("p a b -> p (a b)")
        w1_sb = flat_ring[:, 0:E * H]
        w2_sb = flat_ring[:, E * H:2 * E * H]
        o = 2 * E * H
        xs_sb = flat_ring[:, o:o + 4 * D].rearrange("p (a b) -> p a b", a=4)
        ys_sb = flat_ring[:, o + 4 * D:o + 8 * D].rearrange("p (a b) -> p a b", a=4)
        hid = [hid_a[:, 0, :], hid_a[:, 1, :]]
        hidT = [hidT_a[:, 0, :], hidT_a[:, 1, :]]
        xeT = [xeT_a[:, 0, :], xeT_a[:, 1, :]]
        yg = deltaT[:, 0:TT * D].rearrange("p (t d) -> p t d", t=TT), deltaT[:, TT * D:2 * TT * D].rearrange("p (t d) -> p t d", t=TT)
        hr = duT[:, 0:TT * D].rearrange("p (t d) -> p t d", t=TT), duT[:, TT * D:2 * TT * D].rearrange("p (t d) -> p t d", t=TT)

        ident = cst[:, C_ID:C_ID + 128]
        ones_sq = cst[:, C_ONE:C_ONE + 128]
        tri = cst[:, C_TRI:C_TRI + 128]
        bcol, clscol, b2col, dcol, gcol, onecol, clsp = (col[:, i:i + 1] for i in (0, 1, 2, 3, 4, 5, 6))
        cwv, cwh = col[:, 8:11], col[:, 11:14]

        s_const = sem("s_const")
        s_const_a = sem("s_const_a")
        s_slot = [sem(f"s_slot{i}") for i in range(SLOTS)]
        s_rem = [sem(f"s_rem{i}") for i in range(2)]
        s_zero_set = sem("s_zero_set")
        s_zero = sem("s_zero")
        s_ew = sem("s_ew")
        s_init = sem("s_init")
        s_init_a = sem("s_init_a")
        s_ring_used = sem("s_ring_used")
        s_tok = sem("s_tok")
        s_tok_out = sem("s_tok_out")
        s_hT = sem("s_hT")
        s_tm = sem("s_tm")
        s_stat = sem("s_stat")
        s_rstd = sem("s_rstd")
        s_xn = sem("s_xn")
        s_cm = sem("s_cm")
        s_xnT = sem("s_xnT")
        s_vh = sem("s_vh")
        s_vh_out = sem("s_vh_out")
        s_conv = sem("s_conv")
        s_silu = sem("s_silu")
        s_pm = sem("s_pm")
        s_pm_out = sem("s_pm_out")
        s_sp = sem("s_sp")
        s_du = sem("s_du")
        s_expo = sem("s_expo")
        s_decay = sem("s_decay")
        s_scan = sem("s_scan")
        s_y = sem("s_y")
        s_op = sem("s_op")
        s_op_out = sem("s_op_out")
        s_h2 = sem("s_h2")
        s_h2_st = sem("s_h2_st")
        s_lg = sem("s_lg")
        s_lg_out = sem("s_lg_out")
        s_xnn = sem("s_xnn")
        s_mask = sem("s_mask")
        s_dl = sem("s_dl")
        s_ex = sem("s_ex")
        s_rank = sem("s_rank")
        s_route = sem("s_route")
        s_scat = sem("s_scat")
        s_xs = [sem(f"s_xs{i}") for i in range(2)]
        s_xp = sem("s_xp")
        s_xp_out = sem("s_xp_out")
        s_up = sem("s_up")
        s_hid = sem("s_hid")
        s_ht = sem("s_ht")
        s_ht_out = sem("s_ht_out")
        s_dn = sem("s_dn")
        s_dn_out = sem("s_dn_out")
        s_ys = [sem(f"s_ys{i}") for i in range(2)]
        s_gat = [sem(f"s_gat{i}") for i in range(2)]
        s_hr = [sem(f"s_hr{i}") for i in range(2)]
        s_fin = sem("s_fin")
        s_out = [sem(f"s_out{i}") for i in range(2)]

        block = ctx.enter_context(nc.Block())

        N_CONST = 16 + 10

        def over_chunks(eng, body, group_start):
            for g in range(G):
                group_start(g)
                body(NC * g, 0, g, 0)
                body(NC * g + 1, 1, g, 1)
                with eng.Fori(1, NC // 2) as i:
                    body(i * 2 + NC * g, 0, g, 2)
                    body(i * 2 + (NC * g + 1), 1, g, 2)

        def store_out(sp, m):
            g, j, q = m // 9, m % 9, m % 2
            sp.wait_ge(s_fin, m + 1)
            og = out[g * GB:(g + 1) * GB, :, :]
            if j == 0:
                sp.dma_start(og[:, 0, :], yg[q][0:GB, 0, :]).then_inc(s_out[q], 32)
                return
            l0 = 1 + CL * (j - 1)
            for par in range(2):
                dst = og[:, l0 + par:l0 + par + 2 * TT - 1:2, :]
                sp.dma_start(dst, yg[q][GB * par:GB * par + GB, :, :]).then_inc(s_out[q], 16)

        def gathers(m):
            return sum(1 if u % 9 == 0 else TT for u in range(m % 2, m + 1, 2))

        @block.sync
        def _(sp):
            n = 0

            def load(dst, src):
                sp.dma_start(dst, src).then_inc(s_const, 16)

            load(cst[:, :], consts)
            load(col[:, 0:1], tok_b)
            load(col[:, 1:2], cls)
            load(posT[:, :], pos)
            load(wt[:, :, :], w_main)
            load(wt_rem[:, :], w_rem)
            load(win[:, :], w_in)
            for half in range(2):
                p = slice(CH * half, CH * half + CH)
                load(cwv[p, :], cw_v)
                load(cwh[p, :], cw_h)
                load(col[p, 2:3], b_dt)
                load(col[p, 3:4], d_par)

            def chunk(c, h, g, first):
                for s in range(SLOTS):
                    if not (g == 0 and first == 0):
                        sp.wait_ge(s_ring_used, (SLOTS + 1) * (c - 1) + s + 1)
                    sp.dma_start(ring[:, s, :], x_main[ds(c, 1), s, :, :].rearrange("o p f -> (o p) f")).then_inc(s_slot[s], 16)
                if not (g == 0 and first < 2):
                    sp.wait_ge(s_ring_used, (SLOTS + 1) * (c - 1))
                sp.dma_start(ring_rem[:, h, :], x_rem[ds(c, 1), :, :].rearrange("o p f -> (o p) f")).then_inc(s_rem[h], 16)

            over_chunks(sp, chunk, lambda g: None)
            sp.wait_ge(s_ring_used, (SLOTS + 1) * G * NC)
            sp.dma_start(w1_sb.rearrange("p (e h) -> p e h", e=E), w1).then_inc(s_ew, 16)
            sp.dma_start(w2_sb.rearrange("p (e c d) -> p (e c) d", e=E, c=H // 128), w2).then_inc(s_ew, 16)

            for g in range(G):
                sp.wait_ge(s_h2, 9 * g + 1)
                sp.dma_start(h2d[g, 0:GB, 0:D], h2s[0:GB, 0, :]).then_inc(s_h2_st, 16)
                with sp.Fori(0, NC) as j:
                    sp.wait_ge(s_h2, j + (9 * g + 2))
                    sp.dma_start(h2d[g, :, ds(j * (TT * D) + D, TT * D)],
                                 h2s[:, :, :].rearrange("p t d -> p (t d)")).then_inc(s_h2_st, 16)
                xs_v = xsd[g * NX * 128:(g + 1) * NX * 128, :].rearrange("(n t p) d -> n p t d", t=2, p=128)
                ys_v = ysd[g * NX * 128:(g + 1) * NX * 128, :].rearrange("(n t p) d -> n p t d", t=2, p=128)
                sp.wait_ge(s_scat, 16 * NT * (g + 1))

                def load_pair(q, i):
                    sp.dma_start(xs_sb[:, 2 * q:2 * q + 2, :],
                                 xs_v[ds(i, 1), :, :, :].rearrange("o p t d -> (o p) t d")).then_inc(s_xs[q], 16)

                def store_pair(q, i):
                    sp.wait_ge(s_dn_out, i * 2 + (g * NX + 2))
                    sp.dma_start(ys_v[ds(i, 1), :, :, :].rearrange("o p t d -> (o p) t d"),
                                 ys_sb[:, 2 * q:2 * q + 2, :]).then_inc(s_ys[q], 16)

                load_pair(0, 0)
                load_pair(1, 1)
                with sp.Fori(0, NX // 4 - 1) as i:
                    for q in range(2):
                        sp.wait_ge(s_xp, i * 4 + (g * NX + 2 * q + 2))
                        load_pair(q, i * 2 + (2 + q))
                        store_pair(q, i * 2 + q)
                store_pair(0, NX // 2 - 2)
                store_pair(1, NX // 2 - 1)

            for g in range(G):
                og = out[g * GB:(g + 1) * GB, :, :]
                for j in range(9):
                    m = 9 * g + j
                    q = m % 2
                    if m == 0:
                        sp.wait_ge(s_h2_st, 16 * 18)
                    if m >= 2:
                        sp.wait_ge(s_fin, m - 1)
                        sp.wait_ge(s_out[q], 32 * (m // 2))
                    if j == 0:
                        sp.dma_start(hr[q][0:GB, 0, :], h2d[g, 0:GB, 0:D]).then_inc(s_hr[q], 16)
                    else:
                        sp.dma_start(hr[q].rearrange("p t d -> p (t d)"),
                                     h2d[g, :, (4 * j - 3) * D:(4 * j + 1) * D]).then_inc(s_hr[q], 16)
                    if m >= 1:
                        store_out(sp, m - 1)
            store_out(sp, 17)
            sp.wait_ge(s_out[0], 32 * 9)
            sp.wait_ge(s_out[1], 32 * 9)
            sp.wait_ge(s_ys[0], 16 * (NX // 4) * G)
            sp.wait_ge(s_ys[1], 16 * (NX // 4) * G)

        @block.tensor
        def _(pe):
            def tok_ktile(c, h, t):
                if t < KT - 1:
                    if t % SK == 0:
                        pe.wait_ge(s_slot[t // SK], 16 * (c + 1))
                    m = pe.matmul(psT[h][:, :], wt[:, t, :], ring[:, t // SK, (t % SK) * CW:(t % SK + 1) * CW],
                                  start=(t == 0), stop=False)
                    if t % SK == SK - 1:
                        m.then_inc(s_ring_used, 1)
                else:
                    pe.wait_ge(s_rem[h], 8 * c + (16 - 8 * h))
                    pe.matmul(psT[h][:, :], wt_rem[:, :], ring_rem[:, h, :], start=False, stop=True).then_inc(s_ring_used, 1)

            def to_tokens(src, widths, n):
                for t, w in enumerate(widths):
                    m = pe.transpose(psA[0:w, t * D:(t + 1) * D], src[:, t * 128:t * 128 + w], ident)
                m.then_inc(s_tm, 1)

            def to_channels(widths):
                for t, w in enumerate(widths):
                    m = pe.transpose(psB[:, t * 128:t * 128 + w], xn[0:w, t, :], ident[0:w, 0:w])
                m.then_inc(s_cm, 1)

            def in_proj(n, width):
                pe.wait_ge(s_xnT, n + 1)
                if not (type(n) is int and n == 0):
                    pe.wait_ge(s_vh_out, n)
                v = xnT[:, 0:width * GB].rearrange("p (l b) -> p l b", b=GB)
                for kind in range(2):
                    for half in range(2):
                        m = pe.matmul(psV[CH * half:CH * half + CH, kind * 256:kind * 256 + width * HB],
                                      win[:, CH * kind:CH * kind + CH], v[:, :, HB * half:HB * half + HB],
                                      start=True, stop=True)
                m.then_inc(s_vh, 1)

            def unit_1(n, c):
                pe.wait_ge(s_tok_out, c + 1)
                pe.wait_ge(s_xn, n)
                to_tokens(stage, [128] * TT, n)

            def unit_2(n):
                pe.wait_ge(s_xn, n + 1)
                pe.wait_ge(s_xnT, n)
                to_channels([128] * TT)

            def chunk(c, h, g, first):
                prev = not (g == 0 and first == 0)
                if g > 0 or first == 2:
                    pe.wait_ge(s_tok_out, c - 1)
                for t in range(KT):
                    if prev and t == 3:
                        unit_1(c, c - 1)
                    if prev and t == 9:
                        unit_2(c)
                    if prev and t == 15:
                        in_proj(c, CL)
                    tok_ktile(c, h, t)

            pe.wait_ge(s_const, 16 * 15)
            pe.wait_ge(s_init, 3)
            to_tokens(hC[:, 0, :], [128], 0)
            pe.wait_ge(s_xn, 1)
            to_channels([128])
            in_proj(0, 1)

            def scan_projections(g):
                pe.wait_ge(s_init_a, 1)
                pe.wait_ge(s_silu, g + 1)
                for i in range(10):
                    k = 10 * g + i
                    if k >= 2:
                        pe.wait_ge(s_pm_out, k - 1)
                    if i == 5:
                        pe.wait_ge(s_pm_out, k)
                    src, lhs = (uz, lhs_xd) if i < 5 else (yT, lhs_dt)
                    pe.matmul(psM[k % 2][:, 0:XW], lhs[:, :], src[:, (i % 5) * XW:(i % 5 + 1) * XW],
                              start=True, stop=True).then_inc(s_pm, 1)

            for g in range(G):
                chunk(NC * g, 0, g, 0)
                chunk(NC * g + 1, 1, g, 1)
                if g == 1:
                    scan_projections(0)
                with pe.Fori(1, NC // 2) as i:
                    chunk(i * 2 + NC * g, 0, g, 2)
                    chunk(i * 2 + (NC * g + 1), 1, g, 2)
            unit_1(16, 15)
            unit_2(16)
            in_proj(16, CL)

            def out_proj(g, m, widthl, l0):
                q = m % 2 if type(m) is int else None
                return q

            def out_unit(g, j, q, m, nl, off):
                if q == "first":
                    pass
                w = nl * HB
                bank = psT[q]
                pe.wait_ge(s_op_out, m - 1) if not (type(m) is int and m < 2) else None
                dst = bank[:, 0:nl * GB].rearrange("p (l b) -> p l b", b=GB)
                for half in range(2):
                    for i, src in enumerate((vz, uz)):
                        mm = pe.matmul(dst[:, :, HB * half:HB * half + HB], wo[:, 2 * half + i, :],
                                       src[:, ds(off, w)], start=(i == 0), stop=(i == 1))
                mm.then_inc(s_op, 1)
                n = m + 17
                pe.wait_ge(s_op_out, m + 1)
                pe.wait_ge(s_h2, m) if not (type(m) is int and m < 1) else pe.wait_ge(s_xn, 17)
                widths = [128] * TT if nl > 1 else [GB]
                to_tokens(stage, widths, n)
                pe.wait_ge(s_xn, n + 1)
                pe.wait_ge(s_xnT, n)
                to_channels(widths)
                pe.wait_ge(s_xnT, n + 1)
                pe.wait_ge(s_lg_out, m) if not (type(m) is int and m < 1) else None
                for t, wd in enumerate(widths):
                    mm = pe.matmul(psG[0:wd, t * 8:t * 8 + E], xnT[:, t * 128:t * 128 + wd], wg[:, :], start=True, stop=True)
                mm.then_inc(s_lg, 1)

            scan_projections(1) if False else None
            for g in range(G):
                if g == 1:
                    pass
                pe.wait_ge(s_y, g + 1)
                out_unit(g, 0, (9 * g) % 2, 9 * g, 1, 0)
                with pe.Fori(0, NC // 2) as i:
                    for k in range(2):
                        out_unit(g, None, (9 * g + 1 + k) % 2, i * 2 + (9 * g + 1 + k), CL, i * (2 * CL * HB) + (HB + k * CL * HB))
                pe.wait_ge(s_mask, g + 1)
                if g == 1:
                    pe.wait_ge(s_pm_out, 20)
                pe.matmul(psM[0][:, 0:NT * E], tri, rt[:, 0, :], start=True, stop=True)
                pe.matmul(psM[1][:, 0:NT * E], ones_sq, rt[:, 0, :], start=True, stop=True).then_inc(s_rank, 1)
                pe.wait_ge(s_ew, 32)
                pe.wait_ge(s_route, g + 1)

                def step(s, par, do):
                    a = s + g * NX
                    if do[0]:
                        if par % 2 == 0:
                            pe.wait_ge(s_xs[par // 2], 4 * a + (16 - 4 * par))
                        if not (type(a) is int and a < 2):
                            pe.wait_ge(s_xp_out, a - 1)
                        pe.transpose(ps[par % 2][:, 0:128], xs_sb[:, par, :], ident).then_inc(s_xp, 1)
                    if do[1]:
                        b = a - 1
                        q = (par + 1) % 2
                        e = pe.value_load(texp[0:1, g, ds(s - 1, 1)], min_val=0, max_val=(E - 1) * H)
                        pe.wait_ge(s_xp_out, b + 1)
                        if not (type(b) is int and b < 2):
                            pe.wait_ge(s_hid, b - 1)
                        pe.matmul(ps[2 + q][:, :], xeT[q], w1_sb[:, ds(e, H)], start=True, stop=True).then_inc(s_up, 1)
                    if do[2]:
                        b = a - 2
                        q = par % 2
                        pe.wait_ge(s_hid, b + 1)
                        if not (type(b) is int and b < 2):
                            pe.wait_ge(s_ht_out, b - 1)
                        for k in range(4):
                            mm = pe.transpose(ps[4 + q][:, k * 128:k * 128 + 128], hid[q][:, k * 128:k * 128 + 128], ident)
                        mm.then_inc(s_ht, 1)
                    if do[3]:
                        b = a - 3
                        q = (par + 1) % 2
                        e = pe.value_load(texp[0:1, g, ds(s - 3, 1)], min_val=0, max_val=(E - 1) * H)
                        pe.wait_ge(s_ht_out, b + 1)
                        if not (type(b) is int and b < 2):
                            pe.wait_ge(s_dn_out, b - 1)
                        for k in range(4):
                            mm = pe.matmul(ps[6 + q][:, 0:D], hidT[q][:, k * 128:k * 128 + 128],
                                           w2_sb[:, ds(e + k * D, D)], start=(k == 0), stop=(k == 3))
                        mm.then_inc(s_dn, 1)

                step(0, 0, (1, 0, 0, 0))
                step(1, 1, (1, 1, 0, 0))
                step(2, 2, (1, 1, 1, 0))
                step(3, 3, (1, 1, 1, 1))
                with pe.Fori(1, NX // 4) as i:
                    for k in range(4):
                        step(i * 4 + k, k, (1, 1, 1, 1))
                step(NX, 0, (0, 1, 1, 1))
                step(NX + 1, 1, (0, 0, 1, 1))
                step(NX + 2, 2, (0, 0, 0, 1))
                if g == 0:
                    pe.wait_ge(s_dn_out, NX)
                    scan_projections(1)

        @block.scalar
        def _(act):
            def ld(dst, src):
                act.dma_start(dst, src).then_inc(s_const_a, 16)

            act.wait_ge(s_init, 1)
            for half in range(2):
                for dh in range(2):
                    r = CH * half + 32 * dh
                    ld(lhs_xd[CH * half:CH * half + CH, r:r + 24], w_hs)
                    ld(atab[r:r + 32, :], a_log[dh:dh + 1, :].broadcast_to([32, 32 * NS]))
                ld(lhs_dt[CH * half:CH * half + 8, CH * half:CH * half + CH], w_dt)
                for i in range(2):
                    ld(wo[CH * half:CH * half + CH, 2 * half + i, :], w_out[CH * i:CH * i + CH, :])
            ld(wg[:, :], w_gate)
            ld(col[:, 4:5], gamma)
            act.wait_ge(s_zero_set, 1)
            zv = xsd.rearrange("(q p r) d -> q p (r d)", q=5, p=128)
            zsrc = tA[:, :, :].rearrange("p a b -> p (a b)")
            for q in range(5):
                act.dma_start(zv[q, :, 0:1024], zsrc[:, 0:1024]).then_inc(s_zero, 16)
                act.dma_start(zv[q, :, 1024:2048], zsrc[:, 0:1024]).then_inc(s_zero, 16)
            act.wait_ge(s_const_a, 16 * 16)
            act.wait_ge(s_const, 16 * 15)
            nc.scalar.activation(atab[:, :], atab[:, :], ACT.Exp)
            nc.scalar.drain()
            nc.scalar.mul(atab[:, :], atab[:, :], -1.0)
            nc.scalar.mul(b2col, b2col, 2.0).then_inc(s_init_a, 1)

            def norm(n, widths, src):
                act.wait_ge(s_rstd, n + 1)
                for t, w in enumerate(widths):
                    i = nc.scalar.activation(xn[0:w, t, :], src[0:w, t * D:(t + 1) * D], ACT.Identity,
                                             bias=ln[0:w, 3, t:t + 1], scale=ln[0:w, 2, t:t + 1])
                i.then_inc(s_xn, 1)

            def copy_cm(n, w):
                act.wait_ge(s_cm, n + 1)
                nc.scalar.activation(xnT[:, 0:w], psB[:, 0:w], ACT.Copy).then_inc(s_xnT, 1)

            def unit(n, dst, w):
                act.wait_ge(s_vh, n + 1)
                nc.scalar.activation(dst, psV[:, :].rearrange("p (k f) -> p k f", k=2)[:, :, 0:w], ACT.Copy).then_inc(s_vh_out, 1)

            norm(0, [128], psA)
            copy_cm(0, 128)
            unit(0, vhc[:, :, :], HB)
            nc.scalar.drain()

            vhf = vh[:, :, :, :].rearrange("p k l b -> p k (l b)")

            def put_class():
                nc.scalar.activation(vh[:, :, 1, :], vhc[:, :, :], ACT.Copy)

            def chunk(c, h, g, first):
                prev = not (g == 0 and first == 0)
                if prev:
                    norm(c, [128] * TT, psA)
                    copy_cm(c, CW)
                    if first == 0:
                        pos0 = (2 + CL * (NC - 1)) * HB
                    else:
                        if first == 1 and g == 1:
                            act.wait_ge(s_conv, 1)
                            put_class()
                        pos0 = (c - 1 - NC * g) * (CL * HB) + 2 * HB
                    unit(c, vhf[:, :, ds(pos0, CL * HB)], CL * HB)
                act.wait_ge(s_tok_out, c + 1)
                nc.scalar.activation(hT[:, ds(c, 1), :].rearrange("p o f -> p (o f)"), stage[:, :], ACT.Copy).then_inc(s_hT, 1)

            def scan_prep(g):
                act.wait_ge(s_conv, g + 1)
                nc.scalar.activation(vz[:, :], vz[:, :], ACT.Silu)
                nc.scalar.activation(uz[:, :], uz[:, :], ACT.Silu).then_inc(s_silu, 1)
                if g > 0:
                    act.wait_ge(s_y, g)
                zf = tA[:, :, :].rearrange("p a b -> p (a b)")
                ef = tB[:, :, :].rearrange("p a b -> p (a b)")
                if g == 0:
                    act.wait_ge(s_zero, 160)
                for i in range(10):
                    act.wait_ge(s_pm, 10 * g + i + 1)
                    sl = slice((i % 5) * XW, (i % 5 + 1) * XW)
                    if i < 5:
                        nc.scalar.activation(yT[:, sl], psM[(10 * g + i) % 2][:, 0:XW], ACT.Copy).then_inc(s_pm_out, 1)
                    else:
                        nc.scalar.activation(zf[:, sl], psM[(10 * g + i) % 2][:, 0:XW], ACT.Identity,
                                             bias=b2col).then_inc(s_pm_out, 1)
                nc.scalar.drain()
                nc.scalar.activation(ef, zf, ACT.Abs)
                nc.scalar.drain()
                nc.scalar.activation(ef, ef, ACT.Exp, scale=-1.0)
                nc.scalar.drain()
                nc.scalar.activation(deltaT[:, :], ef, ACT.Ln, bias=onecol).then_inc(s_sp, 1)

            def decay(ks, q):
                act.wait_ge(s_expo, ks + 1)
                v = tA[:, q, :].rearrange("p (s l) -> p s l", l=L)[:, :, 1:L]
                nc.scalar.activation(v, v, ACT.Exp).then_inc(s_decay, 1)

            nc.scalar.drain()
            put_class()
            chunk(0, 0, 0, 0)
            chunk(1, 1, 0, 1)
            with act.Fori(1, NC // 2) as i:
                chunk(i * 2, 0, 0, 2)
                chunk(i * 2 + 1, 1, 0, 2)
            chunk(NC, 0, 1, 0)
            chunk(NC + 1, 1, 1, 1)
            scan_prep(0)
            with act.Fori(NC // 2 + 1, NC) as i:
                for k in range(2):
                    chunk(i * 2 + k, k, 1, 2)
                    for q in range(2):
                        decay(i * 4 + (2 * k + q - 20), q)
            norm(16, [128] * TT, psA)
            copy_cm(16, CW)
            unit(16, vhf[:, :, (2 + CL * (NC - 1)) * HB:(2 + CL * NC) * HB], CL * HB)
            for ks in range(12, NSC):
                decay(ks, ks % 2)

            def out_unit(m, widths, w):
                n = m + 17
                act.wait_ge(s_tm, n + 1)
                if not (type(m) is int and m == 0):
                    act.wait_ge(s_h2_st, 16 * m)
                wd = widths[0]
                nc.scalar.activation(h2s[0:wd, 0:len(widths), :].rearrange("p t d -> p (t d)"),
                                     psA[0:wd, 0:len(widths) * D], ACT.Copy).then_inc(s_h2, 1)
                if not (type(m) is int and m == 0):
                    act.wait_ge(s_xnn, m)
                norm(n, widths, h2s[:, :, :].rearrange("p t d -> p (t d)"))
                copy_cm(n, w)

            for g in range(G):
                if g == 1:
                    scan_prep(1)
                    with act.Fori(0, NSC // 2) as k:
                        decay(k * 2 + NSC, 0)
                        decay(k * 2 + (NSC + 1), 1)
                out_unit(9 * g, [GB], GB)
                with act.Fori(0, NC) as j:
                    out_unit(j + (9 * g + 1), [128] * TT, CW)
                act.wait_ge(s_dl, g + 1)
                nc.scalar.activation(rt[:, 2, :], rt[:, 2, :], ACT.Exp).then_inc(s_ex, 1)

                def step(s, par, do):
                    a = s + g * NX
                    if do[0]:
                        act.wait_ge(s_xp, a + 1)
                        nc.scalar.activation(xeT[par % 2], ps[par % 2][:, 0:128], ACT.Copy, scale=gcol).then_inc(s_xp_out, 1)
                    if do[1]:
                        q = (par + 1) % 2
                        act.wait_ge(s_up, a)
                        nc.scalar.activation(hid[q], ps[2 + q][:, :], ACT.Gelu).then_inc(s_hid, 1)

                step(0, 0, (1, 0))
                step(1, 1, (1, 1))
                step(2, 2, (1, 1))
                step(3, 3, (1, 1))
                with act.Fori(1, NX // 4) as i:
                    for k in range(4):
                        step(i * 4 + k, k, (1, 1))
                step(NX, 0, (0, 1))

        @block.vector
        def _(dve):
            def dr():
                nc.vector.drain()

            nc.vector.memset(lhs_xd[:, :], 0.0)
            nc.vector.memset(lhs_dt[:, :], 0.0)
            nc.vector.memset(wo[:, :, :], 0.0)
            nc.vector.memset(onecol, 1.0)
            nc.vector.memset(epsT[:, :], EPS)
            dr()
            nc.vector.memset(mhalf[:, :], -0.5).then_inc(s_init, 1)
            nc.vector.memset(tA[:, :, :], 0.0).then_inc(s_zero_set, 1)
            nc.vector.memset(lg[:, :, :], 0.0)
            nc.vector.memset(vh[:, :, 0, :], 0.0)
            nc.vector.memset(vh[:, :, L + 1, :], 0.0)
            dve.wait_ge(s_const, 16 * 15)
            nc.vector.tensor_tensor(clsp, clscol, posT[:, 0:1], ALU.mult).then_inc(s_init, 1)
            dr()
            nc.vector.tensor_copy(hC[:, :, :].rearrange("p g f -> p (g f)"),
                                  clsp.broadcast_to([128, G * 128])).then_inc(s_init, 1)

            def stats(n, widths, src):
                for t, w in enumerate(widths):
                    nc.vector.bn_stats(bst[0:w, t, :], src[0:w, t * D:(t + 1) * D])
                dr()
                for t, w in enumerate(widths):
                    i = nc.vector.bn_aggr(mv[0:w, t, :], bst[0:w, t, :])
                i.then_inc(s_stat, 1)

            def chunk(c, h, g, first):
                prev = not (g == 0 and first == 0)
                if prev:
                    dve.wait_ge(s_tm, c + 1)
                    stats(c, [128] * TT, psA)
                    dve.wait_ge(s_hT, c)
                dve.wait_ge(s_ring_used, 7 * c + 7)
                pv = posT[:, ds(c * CL + (1 - g * NC * CL), CL)].rearrange("p (l o) -> p l o", o=1).broadcast_to([128, CL, GB])
                nc.vector.scalar_tensor_tensor(
                    out=stage[:, :].rearrange("p (l b) -> p l b", b=GB),
                    in0=psT[h][:, :].rearrange("p (l b) -> p l b", b=GB), scalar=bcol, in1=pv,
                    op0=ALU.add, op1=ALU.mult).then_inc(s_tok_out, 1)

            def conv(g):
                dve.wait_ge(s_vh_out, NC * g + NC + 1)
                for tap in range(3):
                    for kind, (dst, w) in enumerate(((vz, cwv), (uz, cwh))):
                        src = vh[:, kind, tap:tap + L, :].rearrange("p l b -> p (l b)")
                        if tap == 0:
                            i = nc.vector.tensor_scalar(dst[:, :], src, w[:, 0:1], None, ALU.mult)
                        else:
                            i = nc.vector.scalar_tensor_tensor(out=dst[:, :], in0=src, scalar=w[:, tap:tap + 1],
                                                               in1=dst[:, :], op0=ALU.mult, op1=ALU.add)
                    if tap < 2:
                        dr()
                i.then_inc(s_conv, 1)

            zf = tA[:, :, :].rearrange("p a b -> p (a b)")
            ef = tB[:, :, :].rearrange("p a b -> p (a b)")

            def scan_prep(g):
                dve.wait_ge(s_pm_out, 10 * g + 10)
                nc.vector.transpose(xdT[:, :], yT[:, :])
                dve.wait_ge(s_sp, g + 1)
                nc.vector.tensor_scalar(duT[:, :], ef, 1.0, -1.0, ALU.add, ALU.add)
                dr()
                nc.vector.tensor_tensor(duT[:, :], ef, duT[:, :], ALU.subtract)
                dr()
                nc.vector.tensor_tensor(duT[:, :], duT[:, :], deltaT[:, :], ALU.add)
                dr()
                nc.vector.scalar_tensor_tensor(out=zf, in0=zf, scalar=0.0, in1=duT[:, :], op0=ALU.max, op1=ALU.add)
                dr()
                nc.vector.transpose(deltaT[:, :], zf)
                nc.vector.tensor_tensor(ef, zf, uz[:, :], ALU.mult)
                dr()
                i = nc.vector.memset(tA[:, :, :].rearrange("p a (s l) -> p (a s) l", l=L)[:, :, 0:1], 0.0)
                if g == 0:
                    i.then_inc(s_scan, 2)
                nc.vector.transpose(duT[:, :], ef).then_inc(s_du, 1)
                dr()

            duv = duT[:, :].rearrange("p (l d) -> p d l", d=32)
            xdv = xdT[:, :].rearrange("p (l r) -> p r l", r=32)
            yv = yT[:, :].rearrange("p (l d) -> p d l", d=32)

            def scan(ks, q, d0):
                t4 = tB[:, q, :].rearrange("p (d n l) -> p d n l", d=SD, n=NS)
                du4 = duv[:, ds(d0, SD), :].rearrange("p d (o l) -> p d o l", o=1).broadcast_to([128, SD, NS, L])
                b4 = xdv[:, 8:16, :].rearrange("p (o n) l -> p o n l", o=1).broadcast_to([128, SD, NS, L])
                c4 = xdv[:, 16:24, :].rearrange("p (o n) l -> p o n l", o=1).broadcast_to([128, SD, NS, L])
                nc.vector.tensor_tensor(t4, du4, b4, ALU.mult)
                dr()
                dve.wait_ge(s_decay, ks + 1)
                nc.vector.tensor_tensor_scan(tB[:, q, :], tA[:, q, :], tB[:, q, :], 0.0, ALU.mult, ALU.add).then_inc(s_scan, 1)
                dr()
                nc.vector.tensor_tensor(t4, t4, c4, ALU.mult)
                dr()
                nc.vector.tensor_reduce(yv[:, ds(d0, SD), :], tB[:, q, :].rearrange("p (d n l) -> p d l n", d=SD, n=NS),
                                        AX.X, ALU.add)

            def scan_end(g):
                dr()
                nc.vector.transpose(zf, yT[:, :])
                dr()
                nc.vector.scalar_tensor_tensor(out=uz[:, :], in0=uz[:, :], scalar=dcol, in1=zf,
                                               op0=ALU.mult, op1=ALU.add).then_inc(s_y, 1)

            dve.wait_ge(s_tm, 1)
            stats(0, [128], psA)
            chunk(0, 0, 0, 0)
            chunk(1, 1, 0, 1)
            with dve.Fori(1, NC // 2) as i:
                chunk(i * 2, 0, 0, 2)
                chunk(i * 2 + 1, 1, 0, 2)
            chunk(NC, 0, 1, 0)
            conv(0)
            chunk(NC + 1, 1, 1, 1)
            dve.wait_ge(s_init_a, 1)
            scan_prep(0)
            with dve.Fori(NC // 2 + 1, NC) as i:
                for k in range(2):
                    chunk(i * 2 + k, k, 1, 2)
                    for q in range(2):
                        scan(i * 4 + (2 * k + q - 20), q, i * (4 * SD) + (2 * k + q - 20) * SD)
            dve.wait_ge(s_tm, 17)
            stats(16, [128] * TT, psA)
            for ks in range(12, NSC):
                scan(ks, ks % 2, ks * SD)
            scan_end(0)

            def out_unit(g, j, q, m, nl):
                w = nl * GB
                widths = [128] * TT if nl > 1 else [GB]
                dve.wait_ge(s_op, m + 1)
                if not (type(m) is int and m == 0):
                    dve.wait_ge(s_tm, m + 17)
                old = hC[:, g, 0:GB] if nl == 1 else hT[:, ds(j + NC * g, 1), :].rearrange("p o f -> p (o f)")
                nc.vector.tensor_tensor(stage[:, 0:w], psT[q][:, 0:w], old, ALU.add).then_inc(s_op_out, 1)
                dve.wait_ge(s_h2, m + 1)
                stats(m + 17, widths, h2s[:, :, :].rearrange("p t d -> p (t d)"))
                dve.wait_ge(s_xn, m + 18)
                for t, wd in enumerate(widths):
                    dst = hC[0:wd, g, :] if nl == 1 else hT[:, ds(j + NC * g, 1), t * D:(t + 1) * D].rearrange("p o f -> p (o f)")
                    i = nc.vector.tensor_scalar(dst, xn[0:wd, t, :], ln[0:wd, 5, t:t + 1], None, ALU.mult)
                i.then_inc(s_xnn, 1)
                dve.wait_ge(s_lg, m + 1)
                src = psG[0:widths[0], 0:8 * len(widths)].rearrange("p (t e) -> p t e", e=8)[:, :, 0:E]
                dst = lg[0:GB, 0:1, :] if nl == 1 else lg[:, ds(j * TT + 1, TT), :]
                nc.vector.tensor_copy(dst, src).then_inc(s_lg_out, 1)

            def v3(i):
                return rt[:, i, :].rearrange("p (t e) -> p t e", e=E)

            def over_e(ap):
                return ap.rearrange("p (t o) -> p t o", o=1).broadcast_to([128, NT, E])

            def route(g):
                e8 = cst[:, C_E8:C_E8 + E]
                e8b = e8.rearrange("p (o e) -> p o e", o=1).broadcast_to([128, NT, E])
                dr()
                nc.vector.tensor_reduce(r1[:, 0, :], lg[:, :, :], AX.X, ALU.max)
                dr()
                nc.vector.tensor_tensor(v3(1), lg[:, :, :], over_e(r1[:, 0, :]), ALU.is_ge)
                nc.vector.tensor_tensor(v3(2), lg[:, :, :], over_e(r1[:, 0, :]), ALU.subtract).then_inc(s_dl, 1)
                dr()
                nc.vector.scalar_tensor_tensor(out=v3(1), in0=v3(1), scalar=-8.0, in1=e8b, op0=ALU.mult, op1=ALU.add)
                dr()
                nc.vector.tensor_reduce(r1[:, 1, :], v3(1), AX.X, ALU.min)
                dr()
                nc.vector.tensor_tensor(v3(0), v3(1), over_e(r1[:, 1, :]), ALU.is_equal)
                dr()
                nc.vector.memset(rt[GB:128, 0, 0:E], 0.0).then_inc(s_mask, 1)
                dve.wait_ge(s_ex, g + 1)
                nc.vector.tensor_reduce(r1[:, 2, :], v3(2), AX.X, ALU.add)
                dr()
                nc.vector.reciprocal(r1[:, 3, :], r1[:, 2, :])
                nc.vector.tensor_scalar(v3(1), v3(0), -1.0, 1.0, ALU.mult, ALU.add)
                dr()
                nc.vector.tensor_tensor(v3(2), v3(2), over_e(r1[:, 3, :]), ALU.mult)
                dr()
                nc.vector.tensor_reduce(r1[:, 4, :], v3(2), AX.X, ALU.max)
                nc.vector.tensor_tensor(v3(1), v3(1), v3(2), ALU.mult)
                dr()
                nc.vector.tensor_reduce(r1[:, 5, :], v3(1), AX.X, ALU.max)
                dr()
                nc.vector.tensor_tensor(r1[:, 5, :], r1[:, 5, :], r1[:, 4, :], ALU.add)
                dr()
                nc.vector.tensor_scalar(r1[:, 5, :], r1[:, 5, :], GATE_EPS, None, ALU.add)
                dr()
                nc.vector.reciprocal(r1[:, 6, :], r1[:, 5, :])
                dr()
                nc.vector.tensor_tensor(gate[:, g, :], r1[:, 4, :], r1[:, 6, :], ALU.mult)
                dve.wait_ge(s_rank, g + 1)
                nc.vector.tensor_copy(rt[:, 3, :], psM[1][:, 0:NT * E])
                dr()
                for e in range(E):
                    nc.vector.tensor_tensor_scan(rt[:, 4, e * NT:(e + 1) * NT], ones_sq[:, 0:NT], v3(3)[:, :, e],
                                                 0.0, ALU.mult, ALU.add)
                dr()
                cum = rt[:, 4, :].rearrange("p (e t) -> p e t", e=E)
                nc.vector.tensor_tensor(rt[:, 5, :].rearrange("p (e t) -> p e t", e=E),
                                        cum[:, :, NT - 1:NT].broadcast_to([128, E, NT]),
                                        cst[:, C_K128:C_K128 + NT].rearrange("p (o t) -> p o t", o=1).broadcast_to([128, E, NT]),
                                        ALU.is_gt)
                dr()
                nc.vector.tensor_reduce(tiles[:, 0, :], rt[:, 5, :].rearrange("p (e t) -> p e t", e=E), AX.X, ALU.add)
                dr()
                nc.vector.tensor_tensor_scan(tiles[:, 1, :], ones_sq[:, 0:E], tiles[:, 0, :], 0.0, ALU.mult, ALU.add)
                dr()
                nc.vector.tensor_tensor(tiles[:, 2, :], tiles[:, 1, :], tiles[:, 0, :], ALU.subtract)
                nc.vector.tensor_tensor(v3(3), rt[:, 4, :].rearrange("p (e t) -> p t e", e=E), v3(3), ALU.subtract)
                jv = cst[0:1, C_J:C_J + NX].rearrange("p (j o) -> p j o", o=1).broadcast_to([1, NX, E])
                tv = tiles[0:1, 1, :].rearrange("p (o e) -> p o e", o=1).broadcast_to([1, NX, E])
                nc.vector.tensor_tensor(tcmp[:, :].rearrange("p (j e) -> p j e", e=E), tv, jv, ALU.is_le)
                dr()
                nc.vector.tensor_reduce(tsum[:, :], tcmp[:, :].rearrange("p (j e) -> p j e", e=E), AX.X, ALU.add)
                nc.vector.scalar_tensor_tensor(out=v3(5), in0=tiles[:, 2, :].rearrange("p (o e) -> p o e", o=1).broadcast_to([128, NT, E]),
                                               scalar=128.0, in1=v3(3), op0=ALU.mult, op1=ALU.add)
                dr()
                nc.vector.tensor_scalar(texp[:, g, :], tsum[:, :], float(E - 1), float(H), ALU.min, ALU.mult)
                nc.vector.tensor_tensor(v3(5), v3(5), psM[0][:, 0:NT * E].rearrange("p (t e) -> p t e", e=E), ALU.add)
                dr()
                nc.vector.tensor_tensor(v3(5), v3(5), v3(0), ALU.mult)
                dr()
                nc.vector.tensor_reduce(r1[:, 7, :], v3(5), AX.X, ALU.add)
                dr()
                nc.vector.tensor_scalar(slot[:, g, :], r1[:, 7, :], float(g * NX * 128), None, ALU.add).then_inc(s_route, 1)

            for g in range(G):
                if g == 1:
                    conv(1)
                    scan_prep(1)
                    with dve.Fori(0, NSC // 2) as k:
                        scan(k * 2 + NSC, 0, k * (2 * SD))
                        scan(k * 2 + (NSC + 1), 1, k * (2 * SD) + SD)
                    scan_end(1)
                out_unit(g, 0, (9 * g) % 2, 9 * g, 1)
                with dve.Fori(0, NC // 2) as i:
                    for k in range(2):
                        out_unit(g, i * 2 + k, (9 * g + 1 + k) % 2, i * 2 + (9 * g + 1 + k), CL)
                route(g)

                def step(s, par, do):
                    a = s + g * NX
                    if do[0]:
                        dve.wait_ge(s_ht, a - 1)
                        nc.vector.tensor_copy(hidT[par % 2], ps[4 + par % 2][:, :]).then_inc(s_ht_out, 1)
                    if do[1]:
                        q = (par + 1) % 2
                        b = a - 3
                        dve.wait_ge(s_dn, a - 2)
                        if not (type(b) is int and b < 4):
                            dve.wait_ge(s_ys[((par + 1) % 4) // 2], b * 4 - 4 * ((par + 1) % 4))
                        nc.vector.tensor_copy(ys_sb[:, (par + 1) % 4, :], ps[6 + q][:, 0:D]).then_inc(s_dn_out, 1)

                step(2, 2, (1, 0))
                step(3, 3, (1, 1))
                with dve.Fori(1, NX // 4) as i:
                    for k in range(4):
                        step(i * 4 + k, k, (1, 1))
                step(NX, 0, (1, 1))
                step(NX + 1, 1, (1, 1))
                step(NX + 2, 2, (0, 1))

            for m in range(18):
                g, j, q = m // 9, m % 9, m % 2
                dve.wait_ge(s_gat[q], 16 * gathers(m))
                dve.wait_ge(s_hr[q], 16 * (m // 2 + 1))
                w = GB if j == 0 else 128
                for t in range(1 if j == 0 else TT):
                    tile = 0 if j == 0 else TT * (j - 1) + 1 + t
                    i = nc.vector.scalar_tensor_tensor(out=yg[q][0:w, t, :], in0=yg[q][0:w, t, :], scalar=gate[0:w, g, tile:tile + 1],
                                                       in1=hr[q][0:w, t, :], op0=ALU.mult, op1=ALU.add)
                i.then_inc(s_fin, 1)

        @block.gpsimd
        def _(pool):
            def norm(n, nt, second):
                pool.wait_ge(s_stat, n + 1)
                v = slice(0, nt)
                nc.gpsimd.tensor_tensor(ln[:, 0, v], mv[:, v, 1], epsT[:, v], ALU.add)
                nc.gpsimd.tensor_scalar(ln[:, 1, v], mv[:, v, 0], -1.0, None, ALU.mult)
                nc.gpsimd.drain()
                nc.gpsimd.tensor_tensor(ln[:, 2, v], ln[:, 0, v], mhalf[:, v], ALU.pow)
                nc.gpsimd.drain()
                i = nc.gpsimd.tensor_tensor(ln[:, 3, v], ln[:, 1, v], ln[:, 2, v], ALU.mult)
                if second:
                    nc.gpsimd.tensor_tensor(ln[:, 4, v], ln[:, 2, v], ln[:, 2, v], ALU.mult)
                    nc.gpsimd.drain()
                    nc.gpsimd.tensor_tensor(ln[:, 4, v], ln[:, 4, v], mv[:, v, 1], ALU.mult)
                    nc.gpsimd.drain()
                    nc.gpsimd.tensor_scalar(ln[:, 4, v], ln[:, 4, v], EPS, None, ALU.add)
                    nc.gpsimd.drain()
                    i = nc.gpsimd.tensor_tensor(ln[:, 5, v], ln[:, 4, v], mhalf[:, v], ALU.pow)
                i.then_inc(s_rstd, 1)

            dv = deltaT[:, :].rearrange("p (l d) -> p d l", d=32)
            av = atab[:, :].rearrange("p (d n) -> p d n", n=NS)

            def expo(ks, q, d0):
                pool.wait_ge(s_scan, ks + 1)
                t4 = tA[:, q, :].rearrange("p (d n l) -> p d n l", d=SD, n=NS)
                for i in range(SD):
                    d1 = dv[:, ds(d0 + i, 1), 1:L].broadcast_to([128, NS, L - 1])
                    a1 = av[:, ds(d0 + i, 1), :].rearrange("p o n -> p n o").broadcast_to([128, NS, L - 1])
                    r = nc.gpsimd.tensor_tensor(t4[:, i, :, 1:L], d1, a1, ALU.mult)
                r.then_inc(s_expo, 1)

            pool.wait_ge(s_init, 1)
            norm(0, 1, False)
            norm(1, TT, False)
            with pool.Fori(2, NC) as n:
                norm(n, TT, False)
            norm(NC, TT, False)
            norm(NC + 1, TT, False)
            pool.wait_ge(s_du, 1)
            pool.wait_ge(s_init_a, 1)
            with pool.Fori(NC // 2 + 1, NC) as i:
                for k in range(2):
                    norm(i * 2 + k, TT, False)
                    for q in range(2):
                        expo(i * 4 + (2 * k + q - 20), q, i * (4 * SD) + (2 * k + q - 20) * SD)
            norm(2 * NC, TT, False)
            for ks in range(12, NSC):
                expo(ks, ks % 2, ks * SD)

            for g in range(G):
                if g == 1:
                    pool.wait_ge(s_du, 2)
                    with pool.Fori(0, NSC // 2) as k:
                        expo(k * 2 + NSC, 0, k * (2 * SD))
                        expo(k * 2 + (NSC + 1), 1, k * (2 * SD) + SD)
                norm(17 + 9 * g, 1, True)
                with pool.Fori(0, NC) as j:
                    norm(j + (18 + 9 * g), TT, True)
                pool.wait_ge(s_route, g + 1)
                pool.wait_ge(s_zero, 160)
                pool.wait_ge(s_xnn, 9 * g + 9)
                nc.gpsimd.indirect_dma_start(out=xsd, out_offset=bass.IndirectOffsetOnAxis(ap=slot[0:GB, g, 0:1], axis=0),
                                             in_=hC[0:GB, g, :], in_offset=None).then_inc(s_scat, 16)
                for t in range(1, NT):
                    src = hT[:, NC * g + (t - 1) // TT, ((t - 1) % TT) * D:((t - 1) % TT + 1) * D]
                    nc.gpsimd.indirect_dma_start(out=xsd, out_offset=bass.IndirectOffsetOnAxis(ap=slot[:, g, t:t + 1], axis=0),
                                                 in_=src, in_offset=None).then_inc(s_scat, 16)

            pool.wait_ge(s_ys[0], 16 * (NX // 4) * G)
            pool.wait_ge(s_ys[1], 16 * (NX // 4) * G)
            for m in range(18):
                g, j, q = m // 9, m % 9, m % 2
                if m >= 2:
                    pool.wait_ge(s_out[q], 32 * (m // 2))
                w = GB if j == 0 else 128
                for t in range(1 if j == 0 else TT):
                    tile = 0 if j == 0 else TT * (j - 1) + 1 + t
                    nc.gpsimd.indirect_dma_start(out=yg[q][0:w, t, :], out_offset=None, in_=ysd,
                                                 in_offset=bass.IndirectOffsetOnAxis(ap=slot[0:w, g, tile:tile + 1], axis=0)
                                                 ).then_inc(s_gat[q], 16)


def kernel(**inputs):
    import numpy as np
    import concourse.bacc as bacc
    from concourse.bass_utils import run_bass_kernel_spmd as run

    a = {k: np.asarray(v) for k, v in inputs.items()}

    def cc(v):
        return np.ascontiguousarray(v)

    x = a["x"].reshape(G, GB, C, NP, PATCH, NP, PATCH).transpose(2, 4, 6, 0, 3, 5, 1).reshape(K, B * (L - 1))
    top = (KT - 1) * 128
    x_main = x[:top].reshape(SLOTS, SK, 128, G * NC, CW).transpose(3, 0, 2, 1, 4).reshape(G * NC, SLOTS, 128, SK * CW)
    x_rem = x[top:].reshape(KR, G * NC, CW).transpose(1, 0, 2)
    w = a["L0_tok_W"].T
    consts = np.zeros((128, C_N), np.float32)
    consts[:, C_ID:C_ID + 128] = np.eye(128)
    consts[:, C_TRI:C_TRI + 128] = np.triu(np.ones((128, 128)), 1)
    consts[:, C_ONE:C_ONE + 128] = 1.0
    consts[:, C_E8:C_E8 + E] = np.arange(E)
    consts[:, C_K128:C_K128 + NT] = np.arange(NT) * 128.0
    consts[:, C_J:C_J + NX] = np.arange(NX)
    arrays = {
        "x_main": cc(x_main), "x_rem": cc(x_rem),
        "w_main": cc(w[:top].reshape(KT - 1, 128, D).transpose(1, 0, 2)), "w_rem": cc(w[top:]),
        "tok_b": cc(a["L0_tok_b"].reshape(D, 1)), "cls": cc(a["L0_tok_class_token"].reshape(D, 1)),
        "pos": cc(a["L0_tok_pos_embed"].T), "w_in": cc(a["L0_attn_in_proj_w"].T),
        "cw_v": cc(a["L0_attn_conv_v_w"].reshape(CH, 3)), "cw_h": cc(a["L0_attn_conv_hs_w"].reshape(CH, 3)),
        "w_hs": cc(a["L0_attn_hs_proj_w"].T), "w_dt": cc(a["L0_attn_dt_proj_w"].T),
        "b_dt": cc(a["L0_attn_dt_proj_b"].reshape(CH, 1)), "a_log": cc(a["L0_attn_A_log"].reshape(2, 32 * NS)),
        "d_par": cc(a["L0_attn_D_param"].reshape(CH, 1)), "w_out": cc(a["L0_attn_out_proj_w"].T),
        "w_gate": cc(a["L0_ffn_w_gating"]), "gamma": cc(a["L0_ffn_gamma"].reshape(D, 1)),
        "w1": cc(a["L0_ffn_w1"].transpose(1, 0, 2)),
        "w2": cc(a["L0_ffn_w2"].reshape(E * (H // 128), 128, D).transpose(1, 0, 2)),
        "consts": consts,
    }
    nc = bacc.Bacc("TRN2", target_bir_lowering=False, num_devices=1)
    args = [nc.dram_tensor(n, v.shape, mybir.dt.from_np(v.dtype), kind="ExternalInput").ap() for n, v in arrays.items()]
    res = nc.dram_tensor("tokens_out", (B, L, D), F32, kind="ExternalOutput").ap()
    tower(nc, *args, res)
    r = run(nc, [arrays], core_ids=[0])
    return r.results[0]["tokens_out"]
```

```python
import concourse.bass as bass
from concourse import mybir
from concourse.alu_op_type import AluOpType as ALU
from contextlib import ExitStack

F32 = mybir.dt.float32
I32 = mybir.dt.int32
ACT = mybir.ActivationFunctionType
AX = mybir.AxisListType
ds = bass.ds

B, C, IMG = 128, 3, 224
NP, PATCH = 8, 28
K = C * PATCH * PATCH
D = 128
L = NP * NP + 1
G = 2
GB = B // G
HB = GB // 2
NS = 8
CH = D // 2
E = 6
H = 512
CL = 8
CW = CL * GB
NC = (L - 1) // CL
KT = -(-K // 128)
KR = K - (KT - 1) * 128
SK = 3
SLOTS = (KT - 1) // SK
TT = 4
NT = 1 + NC * TT
NX = 40
LW = L * HB
XW = LW // 5
SD = 2
NSC = 32 // SD
SEQ = SD * NS
EPS = 1e-5
GATE_EPS = 1e-9

C_ID, C_TRI, C_ONE, C_E8, C_K128, C_J = 0, 128, 256, 384, 390, 423
C_TOK = C_J + NX
C_N = C_TOK + NT
RW = D + 2
NO_TOKEN = 1 << 20
T_TM, T_CM, T_IN = 5, 12, 17
NSP = 3
NU = 10


def tower(nc, x_main, x_rem, w_main, w_rem, tok_b, cls, pos, w_in, cw_v, cw_h, w_hs, w_dt, b_dt,
          a_log, d_par, w_out, w_gate, gamma, w1, w2, consts, out):
    ctx = ExitStack()
    with ctx:
        def sb(name, shape, dt=F32):
            return ctx.enter_context(nc.sbuf_tensor(name, shape, dt))

        def sem(name):
            return ctx.enter_context(nc.semaphore(name))

        ring = sb("ring", [128, SLOTS, SK * CW])
        ring_rem = sb("ring_rem", [KR, 2, CW])
        wt = sb("wt", [128, KT - 1, D])
        wt_rem = sb("wt_rem", [KR, D])
        cst = sb("cst", [128, C_N])
        col = sb("col", [128, 24])
        posT = sb("posT", [128, L])
        win = sb("win", [128, D])
        lhs_xd = sb("lhs_xd", [128, 128])
        lhs_dt = sb("lhs_dt", [128, 128])
        wo = sb("wo", [128, 4, D])
        wg = sb("wg", [128, E])
        atab = sb("atab", [128, 32 * NS])
        hT = sb("hT", [128, G * NC, TT, RW])
        hC = sb("hC", [128, G, RW])
        stage_a = sb("stage", [128, 2, CW])
        xn_a = sb("xn", [128, 2, TT, D])
        h2s_a = sb("h2s", [128, 2, TT, D])
        xnT_a = sb("xnT", [128, 2, CW])
        bst_a = sb("bst", [128, 2, TT, 6])
        mv_a = sb("mv", [128, 2, TT, 2])
        ln_a = sb("ln", [128, 2, 6, TT])
        stage, xn, h2s, xnT, bst, mv, ln = ([t[:, q] for q in range(2)] for t in (stage_a, xn_a, h2s_a, xnT_a, bst_a, mv_a, ln_a))
        mhalf = sb("mhalf", [128, TT])
        epsT = sb("epsT", [128, TT])
        vhc = sb("vhc", [128, 2, HB])
        vh = sb("vh", [128, 2, L + 2, HB])
        vz = sb("vz", [128, LW])
        uz = sb("uz", [128, LW])
        deltaT = sb("deltaT", [128, LW])
        duT = sb("duT", [128, LW])
        xdT = sb("xdT", [128, LW])
        yT = sb("yT", [128, LW])
        tA = sb("tA", [128, 2, SEQ * L])
        tB = sb("tB", [128, 2, SEQ * L])
        hid_a = sb("hid_a", [128, 2, H])
        hidT_a = sb("hidT_a", [128, 2, H])
        xeT_a = sb("xeT_a", [128, 2, 128])
        lg = sb("lg", [128, NT, E])
        rt = sb("rt", [128, 6, NT * E])
        r1 = sb("r1", [128, 8, NT])
        slot = sb("slot", [128, G, NT], I32)
        tiles = sb("tiles", [128, 3, E])
        tcmp = sb("tcmp", [1, NX * E])
        tsum = sb("tsum", [1, NX])
        texp = sb("texp", [1, G, NX], I32)

        ps = [ctx.enter_context(nc.psum_tensor(f"ps{i}", [128, 512], F32)) for i in range(8)]
        psT = ps[0:2]
        psA, psB, psV = ps[2], ps[3], ps[4]
        psM = ps[5:7]
        psG = ps[7]

        xsd = nc.dram_tensor("expert_scratch", [G * NX * 128, RW], F32).ap()

        flat_ring = ring[:, :, :].rearrange("p a b -> p (a b)")
        w1_sb = flat_ring[:, 0:E * H]
        w2_sb = flat_ring[:, E * H:2 * E * H]
        o = 2 * E * H
        assert o + NU * (RW + D) <= SLOTS * SK * CW
        xs_sb = flat_ring[:, o:o + NU * RW].rearrange("p (a b) -> p a b", a=NU)
        ys_sb = flat_ring[:, o + NU * RW:o + NU * (RW + D)].rearrange("p (a b) -> p a b", a=NU)
        hid = [hid_a[:, 0, :], hid_a[:, 1, :]]
        hidT = [hidT_a[:, 0, :], hidT_a[:, 1, :]]
        xeT = [xeT_a[:, 0, :], xeT_a[:, 1, :]]
        fill = yT[:, 0:1024].bitcast(I32)
        NZ = -(-G * NX * RW // 1024)

        ident = cst[:, C_ID:C_ID + 128]
        ones_sq = cst[:, C_ONE:C_ONE + 128]
        tri = cst[:, C_TRI:C_TRI + 128]
        bcol, clscol, b2col, dcol, gcol, onecol, clsp = (col[:, i:i + 1] for i in (0, 1, 2, 3, 4, 5, 6))
        cwv, cwh = col[:, 8:11], col[:, 11:14]

        s_const = sem("s_const")
        s_const_a = sem("s_const_a")
        s_wt = [sem(f"s_wt{i}") for i in range(SLOTS + 1)]
        s_slot = [sem(f"s_slot{i}") for i in range(SLOTS)]
        s_rem = [sem(f"s_rem{i}") for i in range(2)]
        s_zero_set = sem("s_zero_set")
        s_zero = sem("s_zero")
        s_ew = sem("s_ew")
        s_init = sem("s_init")
        s_init_a = sem("s_init_a")
        s_ring_used = sem("s_ring_used")
        s_tok = sem("s_tok")
        s_tok_out = sem("s_tok_out")
        s_hT = sem("s_hT")
        s_tm = sem("s_tm")
        s_stat = sem("s_stat")
        s_rstd = sem("s_rstd")
        s_xn = sem("s_xn")
        s_cm = sem("s_cm")
        s_xnT = sem("s_xnT")
        s_vh = sem("s_vh")
        s_vh_out = sem("s_vh_out")
        s_conv = sem("s_conv")
        s_silu = sem("s_silu")
        s_pm = sem("s_pm")
        s_pm_out = sem("s_pm_out")
        s_sp = sem("s_sp")
        s_du = sem("s_du")
        s_expo = sem("s_expo")
        s_decay = sem("s_decay")
        s_scan = sem("s_scan")
        s_y = sem("s_y")
        s_op = sem("s_op")
        s_op_out = sem("s_op_out")
        s_h2 = sem("s_h2")
        s_h2_st = [sem(f"s_h2_st{i}") for i in range(2)]
        s_lg = sem("s_lg")
        s_lg_out = sem("s_lg_out")
        s_xnn = sem("s_xnn")
        s_mask = sem("s_mask")
        s_dl = sem("s_dl")
        s_ex = sem("s_ex")
        s_rank = sem("s_rank")
        s_route = sem("s_route")
        s_scat = sem("s_scat")
        s_xs = [sem(f"s_xs{i}") for i in range(NU // 2)]
        s_xp = sem("s_xp")
        s_xp_out = sem("s_xp_out")
        s_up = sem("s_up")
        s_hid = sem("s_hid")
        s_ht = sem("s_ht")
        s_ht_out = sem("s_ht_out")
        s_dn = sem("s_dn")
        s_dn_out = sem("s_dn_out")
        s_add = [sem(f"s_add{i}") for i in range(NU // 2)]

        NCONST = 16 * 13

        block = ctx.enter_context(nc.Block())

        def over_chunks(eng, body, group_start):
            for g in range(G):
                group_start(g)
                body(NC * g, 0, g, 0)
                body(NC * g + 1, 1, g, 1)
                with eng.Fori(1, NC // 2) as i:
                    body(i * 2 + NC * g, 0, g, 2)
                    body(i * 2 + (NC * g + 1), 1, g, 2)

        def widths_of(j):
            return [GB] if j == 0 else [128] * TT

        @block.sync
        def _(sp):
            n = 0

            def load(dst, src):
                sp.dma_start(dst, src).then_inc(s_const, 16)

            def constants():
                load(cst[:, :], consts)
                load(col[:, 0:1], tok_b)
                load(col[:, 1:2], cls)
                load(posT[:, :], pos)
                load(win[:, :], w_in)
                for half in range(2):
                    p = slice(CH * half, CH * half + CH)
                    load(cwv[p, :], cw_v)
                    load(cwh[p, :], cw_h)
                    load(col[p, 2:3], b_dt)
                    load(col[p, 3:4], d_par)

            def chunk(c, h, g, first):
                for s in range(SLOTS):
                    if not (g == 0 and first == 0):
                        sp.wait_ge(s_ring_used, (SLOTS + 1) * (c - 1) + s + 1)
                    sp.dma_start(ring[:, s, :], x_main[ds(c, 1), s, :, :].rearrange("o p f -> (o p) f")).then_inc(s_slot[s], 16)
                    if g == 0 and first == 0 and s == 1:
                        constants()
                if not (g == 0 and first < 2):
                    sp.wait_ge(s_ring_used, (SLOTS + 1) * (c - 1))
                sp.dma_start(ring_rem[:, h, :], x_rem[ds(c, 1), :, :].rearrange("o p f -> (o p) f")).then_inc(s_rem[h], 16)

            over_chunks(sp, chunk, lambda g: None)
            sp.wait_ge(s_ring_used, (SLOTS + 1) * G * NC)
            sp.dma_start(w1_sb.rearrange("p (e h) -> p e h", e=E), w1).then_inc(s_ew, 16)
            sp.dma_start(w2_sb.rearrange("p (e c d) -> p (e c) d", e=E, c=H // 128), w2).then_inc(s_ew, 16)

            for g in range(G):
                og = out[g * GB:(g + 1) * GB, 1:L, :].rearrange("b (j t r) d -> j r b t d", t=TT, r=2)
                for j in range(9):
                    m = 9 * g + j
                    sp.wait_ge(s_h2, m + 1)
                    if j == 0:
                        sp.dma_start(out[g * GB:(g + 1) * GB, 0, :], h2s[m % 2][0:GB, 0, :]).then_inc(s_h2_st[m % 2], 32)
                    else:
                        for r in range(2):
                            sp.dma_start(og[j - 1, r], h2s[m % 2][GB * r:GB * r + GB, :, :]).then_inc(s_h2_st[m % 2], 16)
                xs_v = xsd[g * NX * 128:(g + 1) * NX * 128, :].rearrange("(n t p) d -> n p t d", t=2, p=128)
                sp.wait_ge(s_scat, 16 * NT * (g + 1))
                for q in range(NU // 2):
                    if g > 0:
                        sp.wait_ge(s_add[q], 32 * (NX // NU) * g)
                    sp.dma_start(xs_sb[:, 2 * q:2 * q + 2, :], xs_v[q]).then_inc(s_xs[q], 16)
                with sp.Fori(1, NX // NU) as i:
                    for q in range(NU // 2):
                        sp.wait_ge(s_add[q], i * 32 + 32 * (NX // NU) * g)
                        sp.dma_start(xs_sb[:, 2 * q:2 * q + 2, :],
                                     xs_v[ds(i * (NU // 2) + q, 1)].rearrange("o p t d -> (o p) t d")).then_inc(s_xs[q], 16)
            for q in range(NU // 2):
                sp.wait_ge(s_add[q], 32 * (NX // NU) * G)

        @block.tensor
        def _(pe):
            def tok_ktile(c, h, t):
                if t < KT - 1:
                    if t % SK == 0:
                        if type(c) is int and c == 0:
                            pe.wait_ge(s_wt[t // SK], 16)
                        pe.wait_ge(s_slot[t // SK], 16 * (c + 1))
                    m = pe.matmul(psT[h][:, :], wt[:, t, :], ring[:, t // SK, (t % SK) * CW:(t % SK + 1) * CW],
                                  start=(t == 0), stop=False)
                    if t % SK == SK - 1:
                        m.then_inc(s_ring_used, 1)
                else:
                    if type(c) is int and c == 0:
                        pe.wait_ge(s_wt[SLOTS], 16)
                    pe.wait_ge(s_rem[h], 8 * c + (16 - 8 * h))
                    pe.matmul(psT[h][:, :], wt_rem[:, :], ring_rem[:, h, :], start=False, stop=True).then_inc(s_ring_used, 1)

            def to_tokens(src, widths):
                for t, w in enumerate(widths):
                    m = pe.transpose(psA[0:w, t * D:(t + 1) * D], src[:, t * 128:t * 128 + w], ident)
                m.then_inc(s_tm, 1)

            def to_channels(widths, q):
                for t, w in enumerate(widths):
                    m = pe.transpose(psB[:, t * 128:t * 128 + w], xn[q][0:w, t, :], ident[0:w, 0:w])
                m.then_inc(s_cm, 1)

            def in_proj(n, width):
                pe.wait_ge(s_xnT, n + 1)
                if not (type(n) is int and n == 0):
                    pe.wait_ge(s_vh_out, n)
                v = xnT[0][:, 0:width * GB].rearrange("p (l b) -> p l b", b=GB)
                for kind in range(2):
                    for half in range(2):
                        m = pe.matmul(psV[CH * half:CH * half + CH, kind * 256:kind * 256 + width * HB],
                                      win[:, CH * kind:CH * kind + CH], v[:, :, HB * half:HB * half + HB],
                                      start=True, stop=True)
                m.then_inc(s_vh, 1)

            def unit_1(n, c):
                pe.wait_ge(s_tok_out, c + 1)
                pe.wait_ge(s_xn, n)
                to_tokens(stage[0], [128] * TT)

            def unit_2(n):
                pe.wait_ge(s_xn, n + 1)
                pe.wait_ge(s_xnT, n)
                to_channels([128] * TT, 0)

            def scan_projection(g, i):
                k = 10 * g + i
                if k >= 2:
                    pe.wait_ge(s_pm_out, k - 1)
                if i == 5:
                    pe.wait_ge(s_pm_out, k)
                src, lhs = (uz, lhs_xd) if i < 5 else (yT, lhs_dt)
                pe.matmul(psM[k % 2][:, 0:XW], lhs[:, :], src[:, (i % 5) * XW:(i % 5 + 1) * XW],
                          start=True, stop=True).then_inc(s_pm, 1)

            def chunk(c, h, g, first, between={}):
                if g > 0 or first >= 2:
                    pe.wait_ge(s_tok_out, c - 1)
                for t in range(KT):
                    if t == T_TM:
                        if g == 0 and first == 0:
                            pe.wait_ge(s_const, NCONST)
                            pe.wait_ge(s_init, 3)
                            to_tokens(hC[:, 0, :], [128])
                        else:
                            unit_1(c, c - 1)
                    if t == T_CM:
                        if g == 0 and first == 0:
                            pe.wait_ge(s_xn, 1)
                            to_channels([128], 0)
                        else:
                            unit_2(c)
                    if t == T_IN:
                        in_proj(c, 1 if g == 0 and first == 0 else CL)
                    if t in between:
                        scan_projection(0, between[t])
                    tok_ktile(c, h, t)

            chunk(0, 0, 0, 0)
            chunk(1, 1, 0, 1)
            with pe.Fori(1, NC // 2) as i:
                chunk(i * 2, 0, 0, 2)
                chunk(i * 2 + 1, 1, 0, 2)
            chunk(NC, 0, 1, 0)
            chunk(NC + 1, 1, 1, 1)
            pe.wait_ge(s_init_a, 1)
            pe.wait_ge(s_silu, 1)
            chunk(NC + 2, 0, 1, 2, {**{1 + k: k for k in range(5)}, **{7 + k: 5 + k for k in range(5)}})
            chunk(NC + 3, 1, 1, 3)
            with pe.Fori(NC // 2 + 2, NC) as i:
                chunk(i * 2, 0, 1, 4)
                chunk(i * 2 + 1, 1, 1, 4)
            unit_1(16, 15)
            unit_2(16)
            in_proj(16, CL)

            def out_step(g, i):
                m = 9 * g + i
                if i < 9:
                    nl, off = (1, 0) if i == 0 else (CL, (1 + CL * (i - 1)) * HB)
                    if m >= 2:
                        pe.wait_ge(s_op_out, m - 1)
                    dst = psT[m % 2][:, 0:nl * GB].rearrange("p (l b) -> p l b", b=GB)
                    for half in range(2):
                        for k, src in enumerate((vz, uz)):
                            mm = pe.matmul(dst[:, :, HB * half:HB * half + HB], wo[:, 2 * half + k, :],
                                           src[:, off:off + nl * HB], start=(k == 0), stop=(k == 1))
                    mm.then_inc(s_op, 1)
                if i >= 3:
                    u = m - 3
                    pe.wait_ge(s_xnT, u + 18)
                    if u >= 1:
                        pe.wait_ge(s_lg_out, u)
                    for t, wd in enumerate(widths_of(i - 3)):
                        mm = pe.matmul(psG[0:wd, t * 8:t * 8 + E], xnT[u % 2][:, t * 128:t * 128 + wd], wg[:, :],
                                       start=True, stop=True)
                    mm.then_inc(s_lg, 1)
                if 1 <= i < 10:
                    u = m - 1
                    pe.wait_ge(s_op_out, u + 1)
                    if u >= 1:
                        pe.wait_ge(s_h2, u)
                    to_tokens(stage[u % 2], widths_of(i - 1))
                if 2 <= i < 11:
                    u = m - 2
                    pe.wait_ge(s_xn, u + 18)
                    pe.wait_ge(s_xnT, u + 17)
                    to_channels(widths_of(i - 2), u % 2)

            def expert_step(g, s, k, do, experts):
                a = s + g * NX
                if do[0]:
                    if k % 2 == 0:
                        pe.wait_ge(s_xs[k // 2], (s - k) // NU * 16 + 16 * (NX // NU * g + 1) if type(s) is int
                                   else experts["pass"] * 16 + 16 * (NX // NU * g + 1))
                    if not (type(a) is int and a < 2):
                        pe.wait_ge(s_xp_out, a - 1)
                    pe.transpose(ps[k % 2][:, 0:128], xs_sb[:, k, 0:D], ident).then_inc(s_xp, 1)
                if do[1]:
                    b, q = a - 1, (k + 1) % 2
                    e = pe.value_load(texp[0:1, g, ds(s - 1, 1)], min_val=0, max_val=(E - 1) * H)
                    experts[(k - 1) % NU] = e
                    pe.wait_ge(s_xp_out, b + 1)
                    if not (type(b) is int and b < 2):
                        pe.wait_ge(s_hid, b - 1)
                    pe.matmul(ps[2 + q][:, :], xeT[q], w1_sb[:, ds(e, H)], start=True, stop=True).then_inc(s_up, 1)
                if do[2]:
                    b, q = a - 2, k % 2
                    pe.wait_ge(s_hid, b + 1)
                    if not (type(b) is int and b < 2):
                        pe.wait_ge(s_ht_out, b - 1)
                    for c in range(4):
                        mm = pe.transpose(ps[4 + q][:, c * 128:c * 128 + 128], hid[q][:, c * 128:c * 128 + 128], ident)
                    mm.then_inc(s_ht, 1)
                if do[3]:
                    b, q = a - 3, (k + 1) % 2
                    e = experts.get((k - 3) % NU)
                    if e is None:
                        e = pe.value_load(texp[0:1, g, ds(s - 3, 1)], min_val=0, max_val=(E - 1) * H)
                    pe.wait_ge(s_ht_out, b + 1)
                    if not (type(b) is int and b < 2):
                        pe.wait_ge(s_dn_out, b - 1)
                    for c in range(4):
                        mm = pe.matmul(ps[6 + q][:, 0:D], hidT[q][:, c * 128:c * 128 + 128],
                                       w2_sb[:, ds(e + c * D, D)], start=(c == 0), stop=(c == 3))
                    mm.then_inc(s_dn, 1)

            for g in range(G):
                if g == 1:
                    pe.wait_ge(s_dn_out, NX)
                pe.wait_ge(s_y, g + 1)
                for i in range(12):
                    out_step(g, i)
                pe.wait_ge(s_mask, g + 1)
                pe.matmul(psM[0][:, 0:NT * E], tri, rt[:, 0, :], start=True, stop=True)
                pe.matmul(psM[1][:, 0:NT * E], ones_sq, rt[:, 0, :], start=True, stop=True).then_inc(s_rank, 1)
                pe.wait_ge(s_ew, 32)
                pe.wait_ge(s_route, g + 1)
                if g == 0:
                    pe.wait_ge(s_silu, 2)
                    for i in range(10):
                        scan_projection(1, i)
                    pe.wait_ge(s_pm_out, 20)
                ex = {}
                for s in range(NU):
                    expert_step(g, s, s, (1, s >= 1, s >= 2, s >= 3), ex)
                with pe.Fori(1, NX // NU) as i:
                    ex = {"pass": i}
                    for k in range(NU):
                        expert_step(g, i * NU + k, k, (1, 1, 1, 1), ex)
                ex = {}
                for k in range(3):
                    expert_step(g, NX + k, k, (0, k < 1, k < 2, 1), ex)

        @block.scalar
        def _(act):
            def ld(dst, src):
                act.dma_start(dst, src).then_inc(s_const_a, 16)

            for t in range(SLOTS):
                act.dma_start(wt[:, SK * t:SK * t + SK, :], w_main[:, SK * t:SK * t + SK, :]).then_inc(s_wt[t], 16)
            act.dma_start(wt_rem[:, :], w_rem).then_inc(s_wt[SLOTS], 16)
            act.wait_ge(s_init, 1)
            for half in range(2):
                for dh in range(2):
                    r = CH * half + 32 * dh
                    ld(lhs_xd[CH * half:CH * half + CH, r:r + 24], w_hs)
                    ld(atab[r:r + 32, :], a_log[dh:dh + 1, :].broadcast_to([32, 32 * NS]))
                ld(lhs_dt[CH * half:CH * half + 8, CH * half:CH * half + CH], w_dt)
                for i in range(2):
                    ld(wo[CH * half:CH * half + CH, 2 * half + i, :], w_out[CH * i:CH * i + CH, :])
            ld(wg[:, :], w_gate)
            ld(col[:, 4:5], gamma)
            act.wait_ge(s_const_a, 16 * 16)
            act.wait_ge(s_const, NCONST)
            nc.scalar.activation(atab[:, :], atab[:, :], ACT.Exp)
            nc.scalar.drain()
            nc.scalar.mul(atab[:, :], atab[:, :], -1.0)
            nc.scalar.mul(b2col, b2col, 2.0).then_inc(s_init_a, 1)

            def norm(n, widths, src, q=0):
                act.wait_ge(s_rstd, n + 1)
                for t, w in enumerate(widths):
                    i = nc.scalar.activation(xn[q][0:w, t, :], src[0:w, t * D:(t + 1) * D], ACT.Identity,
                                             bias=ln[q][0:w, 3, t:t + 1], scale=ln[q][0:w, 2, t:t + 1])
                i.then_inc(s_xn, 1)

            def copy_cm(n, w, q=0):
                act.wait_ge(s_cm, n + 1)
                nc.scalar.activation(xnT[q][:, 0:w], psB[:, 0:w], ACT.Copy).then_inc(s_xnT, 1)

            def unit(n, dst, w):
                act.wait_ge(s_vh, n + 1)
                nc.scalar.activation(dst, psV[:, :].rearrange("p (k f) -> p k f", k=2)[:, :, 0:w], ACT.Copy).then_inc(s_vh_out, 1)

            norm(0, [128], psA)
            copy_cm(0, 128)
            unit(0, vhc[:, :, :], HB)
            nc.scalar.drain()

            vhf = vh[:, :, :, :].rearrange("p k l b -> p k (l b)")

            def put_class():
                nc.scalar.activation(vh[:, :, 1, :], vhc[:, :, :], ACT.Copy)

            def unit_of(c, g, first):
                if first == 0:
                    pos0 = (2 + CL * (NC - 1)) * HB
                else:
                    if first == 1 and g == 1:
                        act.wait_ge(s_conv, 1)
                        put_class()
                    pos0 = (c - 1 - NC * g) * (CL * HB) + 2 * HB
                unit(c, vhf[:, :, ds(pos0, CL * HB)], CL * HB)

            def chunk(c, h, g, first):
                if not (g == 0 and first == 0):
                    norm(c, [128] * TT, psA)
                    copy_cm(c, CW)
                    unit_of(c, g, first)
                copy_hT(c)

            def copy_hT(c):
                act.wait_ge(s_tok_out, c + 1)
                nc.scalar.activation(hT[:, ds(c, 1), :, 0:D].rearrange("p o t f -> p (o t) f"),
                                     stage[0].rearrange("p (t f) -> p t f", t=TT), ACT.Copy).then_inc(s_hT, 1)

            zf = tA[:, :, :].rearrange("p a b -> p (a b)")
            ef = tB[:, :, :].rearrange("p a b -> p (a b)")

            def silus(g):
                act.wait_ge(s_conv, g + 1)
                nc.scalar.activation(vz[:, :], vz[:, :], ACT.Silu)
                nc.scalar.activation(uz[:, :], uz[:, :], ACT.Silu).then_inc(s_silu, 1)

            def projections(g, i0):
                for i in range(i0, i0 + 5):
                    act.wait_ge(s_pm, 10 * g + i + 1)
                    sl = slice((i % 5) * XW, (i % 5 + 1) * XW)
                    if i < 5:
                        nc.scalar.activation(yT[:, sl], psM[(10 * g + i) % 2][:, 0:XW], ACT.Copy).then_inc(s_pm_out, 1)
                    else:
                        nc.scalar.activation(zf[:, sl], psM[(10 * g + i) % 2][:, 0:XW], ACT.Identity,
                                             bias=b2col).then_inc(s_pm_out, 1)

            def softplus(g):
                nc.scalar.drain()
                nc.scalar.activation(ef, zf, ACT.Abs)
                nc.scalar.drain()
                nc.scalar.activation(ef, ef, ACT.Exp, scale=-1.0)
                nc.scalar.drain()
                nc.scalar.activation(deltaT[:, :], ef, ACT.Ln, bias=onecol).then_inc(s_sp, 1)

            def decay(ks, q):
                act.wait_ge(s_expo, ks + 1)
                v = tA[:, q, :].rearrange("p (s l) -> p s l", l=L)[:, :, 1:L]
                nc.scalar.activation(v, v, ACT.Exp).then_inc(s_decay, 1)

            def fill_scratch():
                act.wait_ge(s_zero_set, 1)
                zv = xsd.bitcast(I32).rearrange("(p r) d -> p (r d)", p=128)
                FW = G * NX * RW
                for o1 in range(0, FW, 1024):
                    w = min(1024, FW - o1)
                    act.dma_start(zv[:, o1:o1 + w], fill[:, 0:w]).then_inc(s_zero, 16)

            nc.scalar.drain()
            put_class()
            chunk(0, 0, 0, 0)
            chunk(1, 1, 0, 1)
            with act.Fori(1, NC // 2) as i:
                chunk(i * 2, 0, 0, 2)
                chunk(i * 2 + 1, 1, 0, 2)
            fill_scratch()
            chunk(NC, 0, 1, 0)
            chunk(NC + 1, 1, 1, 1)
            silus(0)
            act.wait_ge(s_zero, 16 * NZ)
            c = NC + 2
            projections(0, 0)
            norm(c, [128] * TT, psA)
            projections(0, 5)
            copy_cm(c, CW)
            softplus(0)
            unit_of(c, 1, 2)
            copy_hT(c)
            chunk(NC + 3, 1, 1, 3)
            decay(0, 0)
            decay(1, 1)
            with act.Fori(NC // 2 + 2, NC) as i:
                for k in range(2):
                    c, ks = i * 2 + k, i * (2 * NSP) + (NSP * k + 2 - (NC // 2 + 2) * 2 * NSP)
                    norm(c, [128] * TT, psA)
                    copy_cm(c, CW)
                    decay(ks, (NSP * k) % 2)
                    unit_of(c, 1, 4)
                    decay(ks + 1, (NSP * k + 1) % 2)
                    copy_hT(c)
                    decay(ks + 2, (NSP * k) % 2)
            norm(16, [128] * TT, psA)
            copy_cm(16, CW)
            unit(16, vhf[:, :, (2 + CL * (NC - 1)) * HB:(2 + CL * NC) * HB], CL * HB)
            for ks in range(4 * NSP + 2, NSC):
                decay(ks, ks % 2)

            def out_step(g, i):
                m = 9 * g + i
                if 1 <= i < 10:
                    u, widths = m - 1, widths_of(i - 1)
                    act.wait_ge(s_tm, u + 18)
                    if u >= 2:
                        act.wait_ge(s_h2_st[u % 2], 32 * (u // 2))
                    nc.scalar.activation(h2s[u % 2][0:widths[0], 0:len(widths), :],
                                         psA[0:widths[0], 0:len(widths) * D].rearrange("p (t d) -> p t d", d=D),
                                         ACT.Copy).then_inc(s_h2, 1)
                if 2 <= i < 11:
                    u, widths = m - 2, widths_of(i - 2)
                    if u >= 2:
                        act.wait_ge(s_xnn, u - 1)
                    norm(u + 17, widths, h2s[u % 2].rearrange("p t d -> p (t d)"), u % 2)
                    copy_cm(u + 17, sum(widths), u % 2)

            def expert_step(g, s, k, do, ht):
                a = s + g * NX
                if do[0]:
                    act.wait_ge(s_xp, a + 1)
                    nc.scalar.activation(xeT[k % 2], ps[k % 2][:, 0:128], ACT.Copy, scale=gcol).then_inc(s_xp_out, 1)
                if do[1]:
                    q = (k + 1) % 2
                    act.wait_ge(s_up, a)
                    nc.scalar.activation(hid[q], ps[2 + q][:, :], ACT.Gelu).then_inc(s_hid, 1)
                if ht and do[2]:
                    act.wait_ge(s_ht, a - 1)
                    nc.scalar.activation(hidT[k % 2], ps[4 + k % 2][:, :], ACT.Copy).then_inc(s_ht_out, 1)

            for g in range(G):
                for i in range(12):
                    out_step(g, i)
                act.wait_ge(s_dl, g + 1)
                nc.scalar.activation(rt[:, 2, :], rt[:, 2, :], ACT.Exp).then_inc(s_ex, 1)
                if g == 0:
                    silus(1)
                    act.wait_ge(s_y, 1)
                    projections(1, 0)
                    projections(1, 5)
                    softplus(1)

                def half(g, s0, k0, flags):
                    for k in range(k0, k0 + NU // 2):
                        expert_step(g, s0 + (k - k0), k, flags(k), g == 0)

                decays = (lambda ks: (decay(ks, 0), decay(ks + 1, 1))) if g == 0 else (lambda ks: None)
                first = lambda k: (1, k >= 1, k >= 2)
                for h in range(2):
                    decays(NSC + 2 * h)
                    half(g, h * (NU // 2), h * (NU // 2), first)
                with act.Fori(1, NX // NU) as i:
                    for h in range(2):
                        decays(i * 4 + (NSC + 2 * h))
                        half(g, i * NU + h * (NU // 2), h * (NU // 2), lambda k: (1, 1, 1))
                for k in range(2):
                    expert_step(g, NX + k, k, (0, k < 1, 1), g == 0)

        @block.vector
        def _(dve):
            def dr():
                nc.vector.drain()

            nc.vector.memset(lhs_xd[:, :], 0.0)
            nc.vector.memset(lhs_dt[:, :], 0.0)
            nc.vector.memset(wo[:, :, :], 0.0)
            nc.vector.memset(onecol, 1.0)
            nc.vector.memset(epsT[:, :], EPS)
            dr()
            nc.vector.memset(mhalf[:, :], -0.5).then_inc(s_init, 1)
            nc.vector.memset(fill, NO_TOKEN).then_inc(s_zero_set, 1)
            nc.vector.memset(lg[:, :, :], 0.0)
            nc.vector.memset(vh[:, :, 0, :], 0.0)
            nc.vector.memset(vh[:, :, L + 1, :], 0.0)
            dve.wait_ge(s_const, NCONST)
            nc.vector.tensor_tensor(clsp, clscol, posT[:, 0:1], ALU.mult).then_inc(s_init, 1)
            dr()
            nc.vector.tensor_copy(hC[:, :, 0:128], col[:, 6:7].rearrange("p (o f) -> p o f", o=1).broadcast_to([128, G, 128])).then_inc(s_init, 1)

            def stats(n, widths, src, q=0):
                for t, w in enumerate(widths):
                    nc.vector.bn_stats(bst[q][0:w, t, :], src[0:w, t * D:(t + 1) * D])
                dr()
                for t, w in enumerate(widths):
                    i = nc.vector.bn_aggr(mv[q][0:w, t, :], bst[q][0:w, t, :])
                i.then_inc(s_stat, 1)

            def unit_stats(c):
                dve.wait_ge(s_tm, c + 1)
                stats(c, [128] * TT, psA)

            def chunk(c, h, g, first):
                if not (g == 0 and first == 0):
                    unit_stats(c)
                evacuate(c, h, g)

            def evacuate(c, h, g):
                if not (type(c) is int and c == 0):
                    dve.wait_ge(s_hT, c)
                dve.wait_ge(s_ring_used, 7 * c + 7)
                pv = posT[:, ds(c * CL + (1 - g * NC * CL), CL)].rearrange("p (l o) -> p l o", o=1).broadcast_to([128, CL, GB])
                nc.vector.scalar_tensor_tensor(
                    out=stage[0].rearrange("p (l b) -> p l b", b=GB),
                    in0=psT[h][:, :].rearrange("p (l b) -> p l b", b=GB), scalar=bcol, in1=pv,
                    op0=ALU.add, op1=ALU.mult).then_inc(s_tok_out, 1)

            def conv(g):
                dve.wait_ge(s_vh_out, NC * g + NC + 1)
                for tap in range(3):
                    for kind, (dst, w) in enumerate(((vz, cwv), (uz, cwh))):
                        src = vh[:, kind, tap:tap + L, :].rearrange("p l b -> p (l b)")
                        if tap == 0:
                            i = nc.vector.tensor_scalar(dst[:, :], src, w[:, 0:1], None, ALU.mult)
                        else:
                            i = nc.vector.scalar_tensor_tensor(out=dst[:, :], in0=src, scalar=w[:, tap:tap + 1],
                                                               in1=dst[:, :], op0=ALU.mult, op1=ALU.add)
                    if tap < 2:
                        dr()
                i.then_inc(s_conv, 1)

            zf = tA[:, :, :].rearrange("p a b -> p (a b)")
            ef = tB[:, :, :].rearrange("p a b -> p (a b)")

            def prep_xd(g):
                dve.wait_ge(s_pm_out, 10 * g + 5)
                nc.vector.transpose(xdT[:, :], yT[:, :])

            def scan_prep(g):
                dve.wait_ge(s_sp, g + 1)
                nc.vector.tensor_scalar(duT[:, :], ef, 1.0, -1.0, ALU.add, ALU.add)
                dr()
                nc.vector.tensor_tensor(duT[:, :], ef, duT[:, :], ALU.subtract)
                dr()
                nc.vector.tensor_tensor(duT[:, :], duT[:, :], deltaT[:, :], ALU.add)
                dr()
                nc.vector.scalar_tensor_tensor(out=zf, in0=zf, scalar=0.0, in1=duT[:, :], op0=ALU.max, op1=ALU.add)
                dr()
                nc.vector.transpose(deltaT[:, :], zf)
                nc.vector.tensor_tensor(ef, zf, uz[:, :], ALU.mult)
                dr()
                i = nc.vector.memset(tA[:, :, :].rearrange("p a (s l) -> p (a s) l", l=L)[:, :, 0:1], 0.0)
                if g == 0:
                    i.then_inc(s_scan, 2)
                nc.vector.transpose(duT[:, :], ef).then_inc(s_du, 1)
                dr()

            duv = duT[:, :].rearrange("p (l d) -> p d l", d=32)
            xdv = xdT[:, :].rearrange("p (l r) -> p r l", r=32)
            yv = yT[:, :].rearrange("p (l d) -> p d l", d=32)

            def scan(ks, q, d0):
                t4 = tB[:, q, :].rearrange("p (d n l) -> p d n l", d=SD, n=NS)
                du4 = duv[:, ds(d0, SD), :].rearrange("p d (o l) -> p d o l", o=1).broadcast_to([128, SD, NS, L])
                b4 = xdv[:, 8:16, :].rearrange("p (o n) l -> p o n l", o=1).broadcast_to([128, SD, NS, L])
                c4 = xdv[:, 16:24, :].rearrange("p (o n) l -> p o n l", o=1).broadcast_to([128, SD, NS, L])
                nc.vector.tensor_tensor(t4, du4, b4, ALU.mult)
                dr()
                dve.wait_ge(s_decay, ks + 1)
                nc.vector.tensor_tensor_scan(tB[:, q, :], tA[:, q, :], tB[:, q, :], 0.0, ALU.mult, ALU.add).then_inc(s_scan, 1)
                dr()
                nc.vector.tensor_tensor(t4, t4, c4, ALU.mult)
                dr()
                nc.vector.tensor_reduce(yv[:, ds(d0, SD), :], tB[:, q, :].rearrange("p (d n l) -> p d l n", d=SD, n=NS),
                                        AX.X, ALU.add)

            def scan_end(g):
                dr()
                nc.vector.transpose(zf, yT[:, :])
                dr()
                nc.vector.scalar_tensor_tensor(out=uz[:, :], in0=uz[:, :], scalar=dcol, in1=zf,
                                               op0=ALU.mult, op1=ALU.add).then_inc(s_y, 1)

            dve.wait_ge(s_tm, 1)
            stats(0, [128], psA)
            chunk(0, 0, 0, 0)
            chunk(1, 1, 0, 1)
            with dve.Fori(1, NC // 2) as i:
                chunk(i * 2, 0, 0, 2)
                chunk(i * 2 + 1, 1, 0, 2)
            chunk(NC, 0, 1, 0)
            unit_stats(NC + 1)
            conv(0)
            evacuate(NC + 1, 1, 1)
            unit_stats(NC + 2)
            dve.wait_ge(s_init_a, 1)
            prep_xd(0)
            evacuate(NC + 2, 0, 1)
            unit_stats(NC + 3)
            scan_prep(0)
            evacuate(NC + 3, 1, 1)
            with dve.Fori(NC // 2 + 2, NC) as i:
                for k in range(2):
                    unit_stats(i * 2 + k)
                    for j in range(NSP * k, NSP * k + NSP):
                        o1 = j - (NC // 2 + 2) * 2 * NSP
                        scan(i * (2 * NSP) + o1, j % 2, i * (2 * NSP * SD) + o1 * SD)
                    evacuate(i * 2 + k, k, 1)
            dve.wait_ge(s_tm, 17)
            stats(16, [128] * TT, psA)
            for ks in range(4 * NSP, NSC):
                scan(ks, ks % 2, ks * SD)
            scan_end(0)

            def out_step(g, i):
                m = 9 * g + i
                if i < 9:
                    w = sum(widths_of(i))
                    dve.wait_ge(s_op, m + 1)
                    if m >= 2:
                        dve.wait_ge(s_tm, m + 16)
                    if i == 0:
                        nc.vector.tensor_tensor(stage[m % 2][:, 0:w], psT[m % 2][:, 0:w], hC[:, g, 0:w], ALU.add).then_inc(s_op_out, 1)
                    else:
                        nc.vector.tensor_tensor(stage[m % 2].rearrange("p (t f) -> p t f", t=TT),
                                                psT[m % 2][:, :].rearrange("p (t f) -> p t f", t=TT),
                                                hT[:, NC * g + i - 1, :, 0:D], ALU.add).then_inc(s_op_out, 1)
                if 1 <= i < 10:
                    u = m - 1
                    dve.wait_ge(s_h2, u + 1)
                    stats(u + 17, widths_of(i - 1), h2s[u % 2].rearrange("p t d -> p (t d)"), u % 2)
                if 2 <= i < 11:
                    u = m - 2
                    dve.wait_ge(s_xn, u + 18)
                    for t, wd in enumerate(widths_of(i - 2)):
                        dst = hC[0:wd, g, 0:D] if i == 2 else hT[:, NC * g + i - 3, t, 0:D]
                        r = nc.vector.tensor_scalar(dst, xn[u % 2][0:wd, t, :], ln[u % 2][0:wd, 5, t:t + 1], None, ALU.mult)
                    r.then_inc(s_xnn, 1)
                if i >= 3:
                    u, wd = m - 3, widths_of(i - 3)
                    dve.wait_ge(s_lg, u + 1)
                    src = psG[0:wd[0], 0:8 * len(wd)].rearrange("p (t e) -> p t e", e=8)[:, :, 0:E]
                    t0 = 0 if i == 3 else 1 + TT * (i - 4)
                    nc.vector.tensor_copy(lg[0:wd[0], t0:t0 + len(wd), :], src).then_inc(s_lg_out, 1)

            def v3(i):
                return rt[:, i, :].rearrange("p (t e) -> p t e", e=E)

            def over_e(ap):
                return ap.rearrange("p (t o) -> p t o", o=1).broadcast_to([128, NT, E])

            def route(g):
                e8 = cst[:, C_E8:C_E8 + E]
                e8b = e8.rearrange("p (o e) -> p o e", o=1).broadcast_to([128, NT, E])
                dr()
                nc.vector.tensor_reduce(r1[:, 0, :], lg[:, :, :], AX.X, ALU.max)
                dr()
                nc.vector.tensor_tensor(v3(1), lg[:, :, :], over_e(r1[:, 0, :]), ALU.is_ge)
                nc.vector.tensor_tensor(v3(2), lg[:, :, :], over_e(r1[:, 0, :]), ALU.subtract).then_inc(s_dl, 1)
                dr()
                nc.vector.scalar_tensor_tensor(out=v3(1), in0=v3(1), scalar=-8.0, in1=e8b, op0=ALU.mult, op1=ALU.add)
                dr()
                nc.vector.tensor_reduce(r1[:, 1, :], v3(1), AX.X, ALU.min)
                dr()
                nc.vector.tensor_tensor(v3(0), v3(1), over_e(r1[:, 1, :]), ALU.is_equal)
                dr()
                nc.vector.memset(rt[GB:128, 0, 0:E], 0.0).then_inc(s_mask, 1)
                dve.wait_ge(s_ex, g + 1)
                nc.vector.tensor_reduce(r1[:, 2, :], v3(2), AX.X, ALU.add)
                dr()
                nc.vector.reciprocal(r1[:, 3, :], r1[:, 2, :])
                nc.vector.tensor_scalar(v3(1), v3(0), -1.0, 1.0, ALU.mult, ALU.add)
                dr()
                nc.vector.tensor_tensor(v3(2), v3(2), over_e(r1[:, 3, :]), ALU.mult)
                dr()
                nc.vector.tensor_reduce(r1[:, 4, :], v3(2), AX.X, ALU.max)
                nc.vector.tensor_tensor(v3(1), v3(1), v3(2), ALU.mult)
                dr()
                nc.vector.tensor_reduce(r1[:, 5, :], v3(1), AX.X, ALU.max)
                dr()
                nc.vector.tensor_tensor(r1[:, 5, :], r1[:, 5, :], r1[:, 4, :], ALU.add)
                dr()
                nc.vector.tensor_scalar(r1[:, 5, :], r1[:, 5, :], GATE_EPS, None, ALU.add)
                dr()
                nc.vector.reciprocal(r1[:, 6, :], r1[:, 5, :])
                dr()
                chunks = hT[:, NC * g:NC * g + NC, :, :].rearrange("p c t f -> p (c t) f")
                nc.vector.tensor_tensor(hC[:, g, D:D + 1], r1[:, 4, 0:1], r1[:, 6, 0:1], ALU.mult)
                nc.vector.tensor_tensor(chunks[:, :, D], r1[:, 4, 1:NT], r1[:, 6, 1:NT], ALU.mult)
                nc.vector.tensor_scalar(hC[:, g, D + 1:D + 2].bitcast(I32), cst[:, C_TOK:C_TOK + 1], float(g * GB * L), None, ALU.add)
                nc.vector.tensor_scalar(chunks[:, :, D + 1].bitcast(I32), cst[:, C_TOK + 1:C_TOK + NT], float(g * GB * L), None, ALU.add)
                dve.wait_ge(s_rank, g + 1)
                nc.vector.tensor_copy(rt[:, 3, :], psM[1][:, 0:NT * E])
                dr()
                for e in range(E):
                    nc.vector.tensor_tensor_scan(rt[:, 4, e * NT:(e + 1) * NT], ones_sq[:, 0:NT], v3(3)[:, :, e],
                                                 0.0, ALU.mult, ALU.add)
                dr()
                cum = rt[:, 4, :].rearrange("p (e t) -> p e t", e=E)
                nc.vector.tensor_tensor(rt[:, 5, :].rearrange("p (e t) -> p e t", e=E),
                                        cum[:, :, NT - 1:NT].broadcast_to([128, E, NT]),
                                        cst[:, C_K128:C_K128 + NT].rearrange("p (o t) -> p o t", o=1).broadcast_to([128, E, NT]),
                                        ALU.is_gt)
                dr()
                nc.vector.tensor_reduce(tiles[:, 0, :], rt[:, 5, :].rearrange("p (e t) -> p e t", e=E), AX.X, ALU.add)
                dr()
                nc.vector.tensor_tensor_scan(tiles[:, 1, :], ones_sq[:, 0:E], tiles[:, 0, :], 0.0, ALU.mult, ALU.add)
                dr()
                nc.vector.tensor_tensor(tiles[:, 2, :], tiles[:, 1, :], tiles[:, 0, :], ALU.subtract)
                nc.vector.tensor_tensor(v3(3), rt[:, 4, :].rearrange("p (e t) -> p t e", e=E), v3(3), ALU.subtract)
                jv = cst[0:1, C_J:C_J + NX].rearrange("p (j o) -> p j o", o=1).broadcast_to([1, NX, E])
                tv = tiles[0:1, 1, :].rearrange("p (o e) -> p o e", o=1).broadcast_to([1, NX, E])
                nc.vector.tensor_tensor(tcmp[:, :].rearrange("p (j e) -> p j e", e=E), tv, jv, ALU.is_le)
                dr()
                nc.vector.tensor_reduce(tsum[:, :], tcmp[:, :].rearrange("p (j e) -> p j e", e=E), AX.X, ALU.add)
                nc.vector.scalar_tensor_tensor(out=v3(5), in0=tiles[:, 2, :].rearrange("p (o e) -> p o e", o=1).broadcast_to([128, NT, E]),
                                               scalar=128.0, in1=v3(3), op0=ALU.mult, op1=ALU.add)
                dr()
                nc.vector.tensor_scalar(texp[:, g, :], tsum[:, :], float(E - 1), float(H), ALU.min, ALU.mult)
                nc.vector.tensor_tensor(v3(5), v3(5), psM[0][:, 0:NT * E].rearrange("p (t e) -> p t e", e=E), ALU.add)
                dr()
                nc.vector.tensor_tensor(v3(5), v3(5), v3(0), ALU.mult)
                dr()
                nc.vector.tensor_reduce(r1[:, 7, :], v3(5), AX.X, ALU.add)
                dr()
                nc.vector.tensor_scalar(slot[:, g, :], r1[:, 7, :], float(g * NX * 128), None, ALU.add).then_inc(s_route, 1)

            def expert_step(g, s, k, do, ht):
                a = s + g * NX
                if ht and do[0]:
                    dve.wait_ge(s_ht, a - 1)
                    nc.vector.tensor_copy(hidT[k % 2], ps[4 + k % 2][:, :]).then_inc(s_ht_out, 1)
                if do[1]:
                    j = (k - 3) % NU
                    dve.wait_ge(s_dn, a - 2)
                    nc.vector.tensor_scalar(ys_sb[:, j, :], ps[6 + (k + 1) % 2][:, 0:D], xs_sb[:, j, D:D + 1], None,
                                            ALU.mult).then_inc(s_dn_out, 1)

            for g in range(G):
                for i in range(12):
                    out_step(g, i)
                route(g)
                if g == 0:
                    conv(1)
                    prep_xd(1)
                    scan_prep(1)
                scans = (lambda i, h: [scan(i * 4 + (NSC + 2 * h + q), q, i * (4 * SD) + (2 * h + q) * SD) for q in range(2)]
                         ) if g == 0 else (lambda i, h: None)

                def half(s0, k0, flags):
                    for k in range(k0, k0 + NU // 2):
                        expert_step(g, s0 + (k - k0), k, flags(k), g == 1)

                for h in range(2):
                    scans(0, h)
                    half(h * (NU // 2), h * (NU // 2), lambda k: (k >= 2, k >= 3))
                with dve.Fori(1, NX // NU) as i:
                    for h in range(2):
                        scans(i, h)
                        half(i * NU + h * (NU // 2), h * (NU // 2), lambda k: (1, 1))
                for k in range(3):
                    expert_step(g, NX + k, k, (k < 2, 1), g == 1)
                if g == 0:
                    scan_end(1)

        @block.gpsimd
        def _(pool):
            def norm(n, nt, second, q=0):
                pool.wait_ge(s_stat, n + 1)
                v = slice(0, nt)
                ln, mv = ln_a[:, q], mv_a[:, q]
                nc.gpsimd.tensor_tensor(ln[:, 0, v], mv[:, v, 1], epsT[:, v], ALU.add)
                nc.gpsimd.tensor_scalar(ln[:, 1, v], mv[:, v, 0], -1.0, None, ALU.mult)
                nc.gpsimd.drain()
                nc.gpsimd.tensor_tensor(ln[:, 2, v], ln[:, 0, v], mhalf[:, v], ALU.pow)
                nc.gpsimd.drain()
                i = nc.gpsimd.tensor_tensor(ln[:, 3, v], ln[:, 1, v], ln[:, 2, v], ALU.mult)
                if second:
                    nc.gpsimd.tensor_tensor(ln[:, 4, v], ln[:, 2, v], ln[:, 2, v], ALU.mult)
                    nc.gpsimd.drain()
                    nc.gpsimd.tensor_tensor(ln[:, 4, v], ln[:, 4, v], mv[:, v, 1], ALU.mult)
                    nc.gpsimd.drain()
                    nc.gpsimd.tensor_scalar(ln[:, 4, v], ln[:, 4, v], EPS, None, ALU.add)
                    nc.gpsimd.drain()
                    i = nc.gpsimd.tensor_tensor(ln[:, 5, v], ln[:, 4, v], mhalf[:, v], ALU.pow)
                i.then_inc(s_rstd, 1)

            dv = deltaT[:, :].rearrange("p (l d) -> p d l", d=32)
            av = atab[:, :].rearrange("p (d n) -> p d n", n=NS)

            def expo(ks, q, d0):
                pool.wait_ge(s_scan, ks + 1)
                t4 = tA[:, q, :].rearrange("p (d n l) -> p d n l", d=SD, n=NS)
                for i in range(SD):
                    d1 = dv[:, ds(d0 + i, 1), 1:L].broadcast_to([128, NS, L - 1])
                    a1 = av[:, ds(d0 + i, 1), :].rearrange("p o n -> p n o").broadcast_to([128, NS, L - 1])
                    r = nc.gpsimd.tensor_tensor(t4[:, i, :, 1:L], d1, a1, ALU.mult)
                r.then_inc(s_expo, 1)

            last_token = nc.gpsimd.to_reg(B * L - 1)
            pool.wait_ge(s_init, 1)
            norm(0, 1, False)
            norm(1, TT, False)
            with pool.Fori(2, NC) as n:
                norm(n, TT, False)
            for n in range(NC, NC + 4):
                norm(n, TT, False)
            pool.wait_ge(s_du, 1)
            pool.wait_ge(s_init_a, 1)
            expo(0, 0, 0)
            expo(1, 1, SD)
            with pool.Fori(NC // 2 + 2, NC) as i:
                for k in range(2):
                    norm(i * 2 + k, TT, False)
                    for j in range(NSP * k + 2, NSP * k + NSP + 2):
                        o1 = j - (NC // 2 + 2) * 2 * NSP
                        expo(i * (2 * NSP) + o1, j % 2, i * (2 * NSP * SD) + o1 * SD)
            norm(2 * NC, TT, False)
            for ks in range(4 * NSP + 2, NSC):
                expo(ks, ks % 2, ks * SD)

            for g in range(G):
                for j in range(9):
                    m = 9 * g + j
                    norm(17 + m, len(widths_of(j)), True, m % 2)
                pool.wait_ge(s_route, g + 1)
                pool.wait_ge(s_zero, 16 * NZ)
                for t in range(NT):
                    src = hC[0:GB, g, :] if t == 0 else hT[:, NC * g + (t - 1) // TT, (t - 1) % TT, :]
                    idx = slot[0:GB, g, 0:1] if t == 0 else slot[:, g, t:t + 1]
                    nc.gpsimd.indirect_dma_start(out=xsd, out_offset=bass.IndirectOffsetOnAxis(ap=idx, axis=0),
                                                 in_=src, in_offset=None).then_inc(s_scat, 16)
                for q in range(2):
                    pool.wait_ge(s_h2_st[q], 32 * ((9 * (g + 1) - q + 1) // 2))

                def add(a, k):
                    pool.wait_ge(s_dn_out, a + 1)
                    nc.gpsimd.nop(nofuse=True)
                    nc.gpsimd.indirect_dma_start(out=out.rearrange("b l d -> (b l) d"),
                                                 out_offset=bass.IndirectOffsetOnAxis(ap=xs_sb[:, k, D + 1:D + 2].bitcast(I32), axis=0),
                                                 in_=ys_sb[:, k, :], in_offset=None, bounds_check=last_token,
                                                 oob_is_err=False, compute_op=ALU.add).then_inc(s_add[k // 2], 16)

                if g == 0:
                    pool.wait_ge(s_du, 2)
                def expos(i, h):
                    if g == 0:
                        for q in range(2):
                            expo(i * 4 + (NSC + 2 * h + q), q, i * (4 * SD) + (2 * h + q) * SD)

                expos(0, 0)
                expos(0, 1)
                for a in range(2):
                    add(g * NX + a, a)
                with pool.Fori(1, NX // NU) as i:
                    for h in range(2):
                        expos(i, h)
                        for k in range(5 * h - 8, 5 * h - 3):
                            add(i * NU + (g * NX + k), k % NU)
                for a in range(NX - 8, NX):
                    add(g * NX + a, a % NU)


def kernel(**inputs):
    import numpy as np
    import concourse.bacc as bacc
    from concourse.bass_utils import run_bass_kernel_spmd as run

    a = {k: np.asarray(v) for k, v in inputs.items()}

    def cc(v):
        return np.ascontiguousarray(v)

    x = a["x"].reshape(G, GB, C, NP, PATCH, NP, PATCH).transpose(2, 4, 6, 0, 3, 5, 1).reshape(K, B * (L - 1))
    top = (KT - 1) * 128
    x_main = x[:top].reshape(SLOTS, SK, 128, G * NC, CW).transpose(3, 0, 2, 1, 4).reshape(G * NC, SLOTS, 128, SK * CW)
    x_rem = x[top:].reshape(KR, G * NC, CW).transpose(1, 0, 2)
    w = a["L0_tok_W"].T
    consts = np.zeros((128, C_N), np.float32)
    consts[:, C_ID:C_ID + 128] = np.eye(128)
    consts[:, C_TRI:C_TRI + 128] = np.triu(np.ones((128, 128)), 1)
    consts[:, C_ONE:C_ONE + 128] = 1.0
    consts[:, C_E8:C_E8 + E] = np.arange(E)
    consts[:, C_K128:C_K128 + NT] = np.arange(NT) * 128.0
    consts[:, C_J:C_J + NX] = np.arange(NX)
    p, t = np.arange(128)[:, None], np.arange(NT)[None, :]
    consts[:, C_TOK:C_TOK + NT] = p % GB * L + np.where(t == 0, 0, 2 * t - 1 + p // GB)
    arrays = {
        "x_main": cc(x_main), "x_rem": cc(x_rem),
        "w_main": cc(w[:top].reshape(KT - 1, 128, D).transpose(1, 0, 2)), "w_rem": cc(w[top:]),
        "tok_b": cc(a["L0_tok_b"].reshape(D, 1)), "cls": cc(a["L0_tok_class_token"].reshape(D, 1)),
        "pos": cc(a["L0_tok_pos_embed"].T), "w_in": cc(a["L0_attn_in_proj_w"].T),
        "cw_v": cc(a["L0_attn_conv_v_w"].reshape(CH, 3)), "cw_h": cc(a["L0_attn_conv_hs_w"].reshape(CH, 3)),
        "w_hs": cc(a["L0_attn_hs_proj_w"].T), "w_dt": cc(a["L0_attn_dt_proj_w"].T),
        "b_dt": cc(a["L0_attn_dt_proj_b"].reshape(CH, 1)), "a_log": cc(a["L0_attn_A_log"].reshape(2, 32 * NS)),
        "d_par": cc(a["L0_attn_D_param"].reshape(CH, 1)), "w_out": cc(a["L0_attn_out_proj_w"].T),
        "w_gate": cc(a["L0_ffn_w_gating"]), "gamma": cc(a["L0_ffn_gamma"].reshape(D, 1)),
        "w1": cc(a["L0_ffn_w1"].transpose(1, 0, 2)),
        "w2": cc(a["L0_ffn_w2"].reshape(E * (H // 128), 128, D).transpose(1, 0, 2)),
        "consts": consts,
    }
    nc = bacc.Bacc("TRN2", target_bir_lowering=False, num_devices=1)
    args = [nc.dram_tensor(n, v.shape, mybir.dt.from_np(v.dtype), kind="ExternalInput").ap() for n, v in arrays.items()]
    res = nc.dram_tensor("tokens_out", (B, L, D), F32, kind="ExternalOutput").ap()
    tower(nc, *args, res)
    r = run(nc, [arrays], core_ids=[0])
    return r.results[0]["tokens_out"]
```

```python
import concourse.bass as bass
from concourse import mybir
from concourse.alu_op_type import AluOpType as ALU
from contextlib import ExitStack

F32 = mybir.dt.float32
I32 = mybir.dt.int32
F32R = mybir.dt.float32r
ACT = mybir.ActivationFunctionType
AX = mybir.AxisListType
ds = bass.ds

B, C = 128, 3
NP, PATCH = 8, 28
K = C * PATCH * PATCH
D = 128
L = NP * NP + 1
G = 2
GB = B // G
HB = GB // 2
NS = 8
CH = D // 2
E = 6
H = 512
CL = 8
CW = CL * GB
NC = (L - 1) // CL
KT = -(-K // 128)
KR = K - (KT - 1) * 128
SK = 3
SLOTS = (KT - 1) // SK
TT = 4
NT = 1 + NC * TT
BATCH = [(0, 0, NT), (1, 0, 13), (1, 13, NT)]


def tokens_of(b):
    g, t0, t1 = BATCH[b]
    return (t1 - t0) * 128 - (64 if t0 == 0 else 0)


NXB = [(tokens_of(b) + E * 127) // 128 for b in range(3)]
BASE = [0, NXB[0], NXB[0] + NXB[1]]
NX = NXB[0]
NXG = [NXB[0], NXB[1] + NXB[2]]
NXS = NXG[0] + NXG[1] + NXG[1] % 2
LW = L * HB
XW = LW // 5
XL = L // 5
PHASE = [(0, 0, 3), (0, 3, 5), (1, 0, 5)]
PROJ = [[(0, 0), (0, 1), (0, 2), (1, 0), (1, 1), (1, 2), (0, 3), (0, 4), (1, 3), (1, 4)],
        [(kind, i) for kind in range(2) for i in range(5)]]
SD = 2
NSC = 32 // SD
SEQ = SD * NS
EPS = 1e-5
GATE_EPS = 1e-9

C_ID, C_TRI, C_ONE, C_E8 = 0, 128, 256, 384
C_K128 = C_E8 + E
C_J = C_K128 + NT
C_TOK = C_J + NX
C_N = C_TOK + NT
RW = D + 2
NO_TOKEN = 1 << 20
NXP = 3
SPLIT_TO = NC - 2
T_TM, T_CM, T_IN = 4, 13, 17
CLS_TM = 9
NSP = 3
NU = 10


P_COL, P_POS, P_WIN = 0, 14, 14 + L
P_N = P_WIN + D
Q_XD, Q_DT, Q_WO, Q_WG = 0, D, 2 * D, 6 * D
Q_A = Q_WG + E
Q_N = Q_A + 32 * NS


def tower(nc, x_main, x_rem, w_main, w_rem, early, late, w1, w2, consts, out):
    ctx = ExitStack()
    with ctx:
        def sb(name, shape, dt=F32):
            return ctx.enter_context(nc.sbuf_tensor(name, shape, dt))

        def sem(name):
            return ctx.enter_context(nc.semaphore(name))

        ring = sb("ring", [128, SLOTS, SK * CW])
        ring_rem = sb("ring_rem", [KR, 2, CW])
        wt = sb("wt", [128, KT - 1, D])
        wt_rem = sb("wt_rem", [KR, D])
        cst = sb("cst", [128, C_N])
        par = sb("par", [128, P_N])
        col = par[:, P_COL:P_COL + 14]
        posT = par[:, P_POS:P_POS + L]
        win = par[:, P_WIN:P_WIN + D]
        par2 = sb("par2", [128, Q_N])
        lhs_xd = par2[:, Q_XD:Q_XD + D]
        lhs_dt = par2[:, Q_DT:Q_DT + D]
        wo = par2[:, Q_WO:Q_WO + 4 * D].rearrange("p (a b) -> p a b", a=4)
        wg = par2[:, Q_WG:Q_WG + E]
        atab = par2[:, Q_A:Q_A + 32 * NS]
        hT = sb("hT", [128, G * NC, TT, RW])
        hC = sb("hC", [128, G, RW])
        stage_a = sb("stage", [128, 2, CW])
        xn_a = sb("xn", [128, 2, TT, D])
        h2s_a = sb("h2s", [128, 2, TT, D])
        xnT_a = sb("xnT", [128, 2, CW])
        bst_a = sb("bst", [128, 2, TT, 6])
        mv_a = sb("mv", [128, 2, TT, 2])
        ln_a = sb("ln", [128, 2, 6, TT])
        stage, xn, h2s, xnT, bst, mv, ln = ([t[:, q] for q in range(2)] for t in (stage_a, xn_a, h2s_a, xnT_a, bst_a, mv_a, ln_a))
        mhalf = sb("mhalf", [128, TT])
        epsT = sb("epsT", [128, TT])
        vhc = sb("vhc", [128, 2, HB])
        vh = sb("vh", [128, 2, L + 2, HB])
        w1e_a = sb("w1e_a", [128, 2, H])
        hidT_a = sb("hidT_a", [128, 2, H])
        xeT_a = sb("xeT_a", [128, 2, 128])
        lg = sb("lg", [128, NT, E])
        rt = sb("rt", [128, 6, NT * E])
        r1 = sb("r1", [128, 8, NT])
        slot = sb("slot", [128, G, NT], I32)
        tiles = sb("tiles", [128, 3, E])
        tcmp = sb("tcmp", [1, NX * E])
        tsum = sb("tsum", [1, NX])
        texp = sb("texp", [1, NXG[0] + NXG[1]], I32)

        with ExitStack() as scan_ctx:
            def scan_sb(name, shape):
                return scan_ctx.enter_context(nc.sbuf_tensor(name, shape, F32))

            vz, uz, deltaT, duT, xdT, yT = (scan_sb(n, [128, LW]) for n in ("vz", "uz", "deltaT", "duT", "xdT", "yT"))
            tA = scan_sb("tA", [128, 2, SEQ * L])
            tB = scan_sb("tB", [128, 2, SEQ * L])
        wh = sb("wh", [128, KT - 1, D], F32R)
        wl = sb("wl", [128, KT - 1, D], F32R)
        xh = sb("xh", [128, NXP, SK * CW], F32R)
        xl = sb("xl", [128, NXP, SK * CW], F32R)

        ps = [ctx.enter_context(nc.psum_tensor(f"ps{i}", [128, 512], F32)) for i in range(8)]
        psT = ps[0:2]
        psA, psB, psV = ps[2], ps[3], ps[4]
        psM = ps[5:7]
        psG = ps[7]

        xsd = nc.dram_tensor("expert_scratch", [NXS * 128, RW], F32).ap()

        flat_ring = ring[:, :, :].rearrange("p a b -> p (a b)")
        w1_sb = flat_ring[:, 0:E * H]
        w2_sb = flat_ring[:, E * H:2 * E * H]
        o = 2 * E * H
        assert o + NU * (RW + D) <= SLOTS * SK * CW
        xs_sb = flat_ring[:, o:o + NU * RW].rearrange("p (a b) -> p a b", a=NU)
        ys_sb = flat_ring[:, o + NU * RW:o + NU * (RW + D)].rearrange("p (a b) -> p a b", a=NU)
        w1e = [w1e_a[:, 0, :], w1e_a[:, 1, :]]
        hidT = [hidT_a[:, 0, :], hidT_a[:, 1, :]]
        xeT = [xeT_a[:, 0, :], xeT_a[:, 1, :]]
        fill = w1e_a[:, :, :].rearrange("p a b -> p (a b)").bitcast(I32)
        NZ = -(-NXS * RW // 1024)

        vz_g = [vz[:, :], vh[:, 0, 1:L + 1, :].rearrange("p l b -> p (l b)")]
        uz_g = [uz[:, :], vh[:, 1, 1:L + 1, :].rearrange("p l b -> p (l b)")]
        tA_b = [tA[:, 0, :], tA[:, 1, :], vz[:, 0:SEQ * L]]
        tB_b = [tB[:, 0, :], tB[:, 1, :], vz[:, SEQ * L:2 * SEQ * L]]
        N_OUT = 14
        FULL = [n // NU for n in NXG]
        LASTP = [n % NU for n in NXG]
        NPRE = NSC - NSP * (FULL[0] + 1)

        ident = cst[:, C_ID:C_ID + 128]
        ones_sq = cst[:, C_ONE:C_ONE + 128]
        tri = cst[:, C_TRI:C_TRI + 128]
        bcol, clscol, b2col, dcol, gcol, onecol, clsp = (col[:, i:i + 1] for i in (0, 1, 2, 3, 4, 5, 6))
        cwv, cwh = col[:, 8:11], col[:, 11:14]

        s_const = sem("s_const")
        s_const_a = sem("s_const_a")
        s_wt = [sem(f"s_wt{i}") for i in range(SLOTS + 1)]
        s_slot = [sem(f"s_slot{i}") for i in range(SLOTS)]
        s_rem = [sem(f"s_rem{i}") for i in range(2)]
        s_zero_set = sem("s_zero_set")
        s_zero = sem("s_zero")
        s_ew = sem("s_ew")
        s_set = sem("s_set")
        s_init = sem("s_init")
        s_init_a = sem("s_init_a")
        s_ring_used = sem("s_ring_used")
        s_wh = sem("s_wh")
        s_wl = sem("s_wl")
        s_xh = sem("s_xh")
        s_xl = sem("s_xl")
        s_tok_out = sem("s_tok_out")
        s_hT = sem("s_hT")
        s_tm = sem("s_tm")
        s_stat = sem("s_stat")
        s_rstd = sem("s_rstd")
        s_rstd2 = sem("s_rstd2")
        s_xn = sem("s_xn")
        s_cm = sem("s_cm")
        s_xnT = sem("s_xnT")
        s_vh = sem("s_vh")
        s_vh_out = sem("s_vh_out")
        s_conv = sem("s_conv")
        s_silu = sem("s_silu")
        s_pm = sem("s_pm")
        s_pm_out = sem("s_pm_out")
        s_sp = sem("s_sp")
        s_du = sem("s_du")
        s_expo = sem("s_expo")
        s_expo_d = sem("s_expo_d")
        s_decay = sem("s_decay")
        s_scan = sem("s_scan")
        s_y = sem("s_y")
        s_op = sem("s_op")
        s_op_out = sem("s_op_out")
        s_h2 = sem("s_h2")
        s_h2_st = [sem(f"s_h2_st{i}") for i in range(2)]
        s_lg = sem("s_lg")
        s_lg_out = sem("s_lg_out")
        s_xnn = sem("s_xnn")
        s_mask = sem("s_mask")
        s_dl = sem("s_dl")
        s_ex = sem("s_ex")
        s_rank = sem("s_rank")
        s_route = sem("s_route")
        s_rank_out = sem("s_rank_out")
        s_scat = [sem(f"s_scat{b}") for b in range(3)]
        s_xs = [sem(f"s_xs{i}") for i in range(NU // 2)]
        s_xp = sem("s_xp")
        s_xp_out = sem("s_xp_out")
        s_w1e = sem("s_w1e")
        s_up = sem("s_up")
        s_hid = sem("s_hid")
        s_dn = sem("s_dn")
        s_dn_out = sem("s_dn_out")
        s_add = [sem(f"s_add{i}") for i in range(NU // 2)]

        NCONST = 16 * 2

        block = ctx.enter_context(nc.Block())

        def over_chunks(eng, body):
            for g in range(G):
                body(NC * g, 0, g, 0)
                body(NC * g + 1, 1, g, 1)
                with eng.Fori(1, NC // 2) as i:
                    body(i * 2 + NC * g, 0, g, 2)
                    body(i * 2 + (NC * g + 1), 1, g, 2)

        MASK_AT, RANK_AT, GATE_AT, SLOT_AT = 8, 9, 9, 10
        PROJ_AT = {9: (0, 1), 10: (2, 3), 11: (4, 5), 12: (6, 7), 13: (8, 9)}

        def scan_parts(k, nk):
            return [divmod(n, 4) for n in range(4 * NSP) if n * nk // (4 * NSP) == k]

        def pairs_before(g, q):
            return 0 if g == 0 else -(-(NXG[0] // 2 - q) // (NU // 2))

        def widths_of(j):
            return [GB] if j == 0 else [128] * TT

        @block.sync
        def _(sp):
            def load(dst, src):
                sp.dma_start(dst, src).then_inc(s_const, 16)

            def constants():
                load(cst[:, :], consts)
                load(par[:, :], early)

            def chunk(c, h, g, first):
                for s in range(SLOTS):
                    if not (g == 0 and first == 0):
                        sp.wait_ge(s_ring_used, (SLOTS + 1) * (c - 1) + s + 1)
                    sp.dma_start(ring[:, s, :], x_main[ds(c, 1), s, :, :].rearrange("o p f -> (o p) f")).then_inc(s_slot[s], 16)
                    if g == 0 and first == 0 and s == 2:
                        constants()
                if not (g == 0 and first < 2):
                    sp.wait_ge(s_ring_used, (SLOTS + 1) * (c - 1))
                sp.dma_start(ring_rem[:, h, :], x_rem[ds(c, 1), :, :].rearrange("o p f -> (o p) f")).then_inc(s_rem[h], 16)

            over_chunks(sp, chunk)
            sp.wait_ge(s_ring_used, (SLOTS + 1) * G * NC)
            sp.dma_start(w1_sb.rearrange("p (e h) -> p e h", e=E), w1).then_inc(s_ew, 16)
            sp.dma_start(w2_sb.rearrange("p (e c d) -> p (e c) d", e=E, c=H // 128), w2).then_inc(s_ew, 16)

            for g in range(G):
                og = out[g * GB:(g + 1) * GB, 1:L, :].rearrange("b (j t r) d -> j r b t d", t=TT, r=2)
                for j in range(9):
                    m = 9 * g + j
                    sp.wait_ge(s_h2, m + 1)
                    if j == 0:
                        sp.dma_start(out[g * GB:(g + 1) * GB, 0, :], h2s[m % 2][0:GB, 0, :]).then_inc(s_h2_st[m % 2], 32)
                    else:
                        for r in range(2):
                            sp.dma_start(og[j - 1, r], h2s[m % 2][GB * r:GB * r + GB, :, :]).then_inc(s_h2_st[m % 2], 16)
                xs_v = xsd.rearrange("(n t p) d -> n p t d", t=2, p=128)
                for n in range(-(-NXG[g] // 2)):
                    q, first_tile = n % (NU // 2), NXG[0] * g + 2 * n
                    if first_tile in BASE:
                        b = BASE.index(first_tile)
                        sp.wait_ge(s_scat[b], 16 * (BATCH[b][2] - BATCH[b][1]))
                    uses = pairs_before(g, q) + n // (NU // 2)
                    if uses > 0:
                        sp.wait_ge(s_add[q], 32 * uses)
                    sp.dma_start(xs_sb[:, 2 * q:2 * q + 2, :], xs_v[first_tile // 2]).then_inc(s_xs[q], 16)
            for q in range(NU // 2):
                tiles_q = sum(1 for n in NXG for t in range(n) if t % NU // 2 == q)
                sp.wait_ge(s_add[q], 16 * tiles_q)

        @block.tensor
        def _(pe):
            def split_ktile(c, h, t):
                s, j = divmod(t, SK)
                n = c * SLOTS + (s - SLOTS + 1)
                if j == 0:
                    pe.wait_ge(s_xh, n)
                xs = lambda x, j: x[:, s % NXP, j * CW:(j + 1) * CW]
                pe.matmul(psT[h][:, :], wh[:, t, :], xs(xh, j), start=(t == 0), stop=False)
                pe.matmul(psT[h][:, :], wl[:, t, :], xs(xh, j), start=False, stop=False)
                if j == SK - 1:
                    pe.wait_ge(s_xl, n)
                    for jj in range(SK):
                        m = pe.matmul(psT[h][:, :], wh[:, SK * s + jj, :], xs(xl, jj), start=False, stop=False)
                    m.then_inc(s_ring_used, 1)

            def tok_ktile(c, h, t):
                if t < KT - 1:
                    if t % SK == 0:
                        if type(c) is int and c == 0:
                            pe.wait_ge(s_wt[t // SK], 16)
                        pe.wait_ge(s_slot[t // SK], 16 * (c + 1))
                    m = pe.matmul(psT[h][:, :], wt[:, t, :], ring[:, t // SK, (t % SK) * CW:(t % SK + 1) * CW],
                                  start=(t == 0), stop=False)
                    if t % SK == SK - 1:
                        m.then_inc(s_ring_used, 1)
                else:
                    if type(c) is int and c == 0:
                        pe.wait_ge(s_wt[SLOTS], 16)
                    pe.wait_ge(s_rem[h], 8 * c + (16 - 8 * h))
                    pe.matmul(psT[h][:, :], wt_rem[:, :], ring_rem[:, h, :], start=False, stop=True).then_inc(s_ring_used, 1)

            def to_tokens(src, widths):
                for t, w in enumerate(widths):
                    m = pe.transpose(psA[0:w, t * D:(t + 1) * D], src[:, t * 128:t * 128 + w], ident)
                m.then_inc(s_tm, 1)

            def to_channels(widths, q):
                for t, w in enumerate(widths):
                    m = pe.transpose(psB[:, t * 128:t * 128 + w], xn[q][0:w, t, :], ident[0:w, 0:w])
                m.then_inc(s_cm, 1)

            def in_proj(n, width):
                pe.wait_ge(s_xnT, n + 1)
                if not (type(n) is int and n == 0):
                    pe.wait_ge(s_vh_out, n)
                v = xnT[0][:, 0:width * GB].rearrange("p (l b) -> p l b", b=GB)
                for kind in range(2):
                    for half in range(2):
                        m = pe.matmul(psV[CH * half:CH * half + CH, kind * 256:kind * 256 + width * HB],
                                      win[:, CH * kind:CH * kind + CH], v[:, :, HB * half:HB * half + HB],
                                      start=True, stop=True)
                m.then_inc(s_vh, 1)

            def unit_1(n, c):
                pe.wait_ge(s_tok_out, c + 1)
                pe.wait_ge(s_xn, n)
                to_tokens(stage[0], [128] * TT)

            def unit_2(n):
                pe.wait_ge(s_xn, n + 1)
                pe.wait_ge(s_xnT, n)
                to_channels([128] * TT, 0)

            def scan_projection(g, i):
                k, (kind, blk) = 10 * g + i, PROJ[g][i]
                if k >= 2:
                    pe.wait_ge(s_pm_out, k - 1)
                src, lhs = (uz_g[g], lhs_xd) if kind == 0 else (yT, lhs_dt)
                pe.matmul(psM[k % 2][:, 0:XW], lhs[:, :], src[:, blk * XW:(blk + 1) * XW],
                          start=True, stop=True).then_inc(s_pm, 1)

            def chunk(c, h, g, first, between={}, split=False):
                if g > 0 or first >= 2:
                    pe.wait_ge(s_tok_out, c - 1)
                for t in range(KT):
                    if t == (CLS_TM if g == 0 and first == 0 else T_TM):
                        if g == 0 and first == 0:
                            pe.wait_ge(s_const, NCONST)
                            pe.wait_ge(s_init, 1)
                            to_tokens(hC[:, 0, :], [128])
                        else:
                            unit_1(c, c - 1)
                    if t == T_CM:
                        if g == 0 and first == 0:
                            pe.wait_ge(s_xn, 1)
                            to_channels([128], 0)
                        else:
                            unit_2(c)
                    if t == T_IN:
                        in_proj(c, 1 if g == 0 and first == 0 else CL)
                    if t in between:
                        scan_projection(0, between[t])
                    if split and t < KT - 1:
                        split_ktile(c, h, t)
                    else:
                        tok_ktile(c, h, t)

            chunk(0, 0, 0, 0)
            pe.wait_ge(s_wl, 2)
            chunk(1, 1, 0, 1, split=True)
            with pe.Fori(1, NC // 2 - 1) as i:
                chunk(i * 2, 0, 0, 2, split=True)
                chunk(i * 2 + 1, 1, 0, 2, split=True)
            chunk(NC - 2, 0, 0, 2, split=True)
            chunk(NC - 1, 1, 0, 2)
            pe.wait_ge(s_init_a, 1)
            pe.wait_ge(s_silu, 1)
            chunk(NC, 0, 1, 0, {k: k for k in range(6)})
            chunk(NC + 1, 1, 1, 1)
            pe.wait_ge(s_silu, 2)
            chunk(NC + 2, 0, 1, 2, {1 + k: 6 + k for k in range(4)})
            chunk(NC + 3, 1, 1, 3)
            with pe.Fori(NC // 2 + 2, NC) as i:
                chunk(i * 2, 0, 1, 4)
                chunk(i * 2 + 1, 1, 1, 4)
            unit_1(16, 15)
            unit_2(16)
            in_proj(16, CL)

            def out_step(g, i):
                m = 9 * g + i
                if i < 9:
                    nl, off = (1, 0) if i == 0 else (CL, (1 + CL * (i - 1)) * HB)
                    if m >= 2:
                        pe.wait_ge(s_op_out, m - 1)
                    dst = psT[m % 2][:, 0:nl * GB].rearrange("p (l b) -> p l b", b=GB)
                    for half in range(2):
                        for k, src in enumerate((vz_g[g], uz_g[g])):
                            mm = pe.matmul(dst[:, :, HB * half:HB * half + HB], wo[:, 2 * half + k, :],
                                           src[:, off:off + nl * HB], start=(k == 0), stop=(k == 1))
                    mm.then_inc(s_op, 1)
                if 1 <= i < 10:
                    u = m - 1
                    pe.wait_ge(s_op_out, u + 1)
                    if u >= 1:
                        pe.wait_ge(s_h2, u)
                    to_tokens(stage[u % 2], widths_of(i - 1))
                if 3 <= i < 12:
                    u = m - 3
                    pe.wait_ge(s_xn, u + 18)
                    pe.wait_ge(s_xnT, u + 17)
                    to_channels(widths_of(i - 3), u % 2)
                if 4 <= i < 13:
                    u = m - 4
                    pe.wait_ge(s_xnT, u + 18)
                    if u >= 1:
                        pe.wait_ge(s_lg_out, u)
                    for t, wd in enumerate(widths_of(i - 4)):
                        mm = pe.matmul(psG[0:wd, t * 8:t * 8 + E], xnT[u % 2][:, t * 128:t * 128 + wd], wg[:, :],
                                       start=True, stop=True)
                    mm.then_inc(s_lg, 1)

            def expert_step(g, s, k, do, p):
                a = s + g * NXG[0]
                if do[0]:
                    if k % 2 == 0:
                        pe.wait_ge(s_xs[k // 2], p * 16 + 16 * (pairs_before(g, k // 2) + 1))
                    if not (type(a) is int and a < 2):
                        pe.wait_ge(s_xp_out, a - 1)
                    pe.transpose(ps[k % 2][:, 0:128], xs_sb[:, k, 0:D], ident).then_inc(s_xp, 1)
                if do[1]:
                    b, q = a - 1, (k + 1) % 2
                    pe.wait_ge(s_w1e, b + 1)
                    pe.wait_ge(s_xp_out, b + 1)
                    if not (type(b) is int and b < 2):
                        pe.wait_ge(s_hid, b - 1)
                    for c in range(4):
                        mm = pe.matmul(ps[2 + q][:, c * 128:c * 128 + 128], w1e[q][:, c * 128:c * 128 + 128], xeT[q],
                                       start=True, stop=True)
                    mm.then_inc(s_up, 1)
                if do[2]:
                    b, q = a - 2, k % 2
                    e = pe.value_load(texp[0:1, ds(b, 1)], min_val=0, max_val=(E - 1) * H)
                    pe.wait_ge(s_hid, b + 1)
                    if not (type(b) is int and b < 2):
                        pe.wait_ge(s_dn_out, b - 1)
                    for c in range(4):
                        mm = pe.matmul(ps[4 + q][:, 0:D], hidT[q][:, c * 128:c * 128 + 128],
                                       w2_sb[:, ds(e + c * D, D)], start=(c == 0), stop=(c == 3))
                    mm.then_inc(s_dn, 1)

            def ranks(b):
                w = (BATCH[b][2] - BATCH[b][1]) * E
                pe.wait_ge(s_pm_out, 20)
                pe.wait_ge(s_mask, b + 1)
                if b > 0:
                    pe.wait_ge(s_rank_out, b)
                pe.matmul(psM[0][:, 0:w], tri, rt[:, 0, 0:w], start=True, stop=True)
                pe.matmul(psM[1][:, 0:w], ones_sq, rt[:, 0, 0:w], start=True, stop=True).then_inc(s_rank, 1)

            for g in range(G):
                if g == 1:
                    pe.wait_ge(s_dn_out, NXG[0])
                pe.wait_ge(s_y, g + 1)
                for i in range(N_OUT):
                    out_step(g, i)
                    if g == 0:
                        if i == min(PROJ_AT):
                            pe.wait_ge(s_silu, 3)
                        for k in PROJ_AT.get(i, ()):
                            scan_projection(1, k)
                    if g == 1 and i == RANK_AT:
                        ranks(1)
                ranks(2 * g)
                pe.wait_ge(s_rank_out, 2 * g + 1)
                pe.wait_ge(s_ew, 32)
                pe.wait_ge(s_route, g + 1)
                for s in range(NU):
                    expert_step(g, s, s, (1, s >= 1, s >= 2), 0)
                pe.wait_ge(s_route, 2 * g + 1)
                with pe.Fori(1, FULL[g]) as i:
                    for k in range(NU):
                        expert_step(g, i * NU + k, k, (1, 1, 1), i)
                for k in range(LASTP[g] + 2):
                    expert_step(g, NU * FULL[g] + k, k, (k < LASTP[g], k < LASTP[g] + 1, 1), FULL[g])

        @block.scalar
        def _(act):
            for t in range(SLOTS):
                act.dma_start(wt[:, SK * t:SK * t + SK, :], w_main[:, SK * t:SK * t + SK, :]).then_inc(s_wt[t], 16)
            act.dma_start(wt_rem[:, :], w_rem).then_inc(s_wt[SLOTS], 16)
            act.dma_start(par2[:, :], late).then_inc(s_const_a, 16)

            def scan_parameters():
                act.wait_ge(s_const_a, 16)
                act.wait_ge(s_const, NCONST)
                nc.scalar.activation(atab, atab, ACT.Exp)
                nc.scalar.drain()
                nc.scalar.mul(atab, atab, -1.0)
                nc.scalar.mul(b2col, b2col, 2.0).then_inc(s_init_a, 1)

            def norm(n, widths, src, q=0):
                act.wait_ge(s_rstd, n + 1)
                for t, w in enumerate(widths):
                    i = nc.scalar.activation(xn[q][0:w, t, :], src[0:w, t * D:(t + 1) * D], ACT.Identity,
                                             bias=ln[q][0:w, 3, t:t + 1], scale=ln[q][0:w, 2, t:t + 1])
                i.then_inc(s_xn, 1)

            def copy_cm(n, w, q=0):
                act.wait_ge(s_cm, n + 1)
                nc.scalar.activation(xnT[q][:, 0:w], psB[:, 0:w], ACT.Copy).then_inc(s_xnT, 1)

            def unit(n, dst, w):
                act.wait_ge(s_vh, n + 1)
                nc.scalar.activation(dst, psV[:, :].rearrange("p (k f) -> p k f", k=2)[:, :, 0:w], ACT.Copy).then_inc(s_vh_out, 1)

            def split_weights(half):
                for t in range(SLOTS // 2 * half, SLOTS // 2 * (half + 1)):
                    act.wait_ge(s_wt[t], 16)
                r = slice((KT - 1) // 2 * half, (KT - 1) // 2 * (half + 1))
                nc.scalar.activation(wh[:, r, :], wt[:, r, :], ACT.Copy).then_inc(s_wh, 1)

            def split_slot(c, s):
                act.wait_ge(s_slot[s], c * 16 + 16)
                if not (type(c) is int and c == 1 and s < NXP):
                    act.wait_ge(s_ring_used, c * (SLOTS + 1) + (s - NXP + 1 if s >= NXP else s - NXP))
                nc.scalar.activation(xh[:, s % NXP, :], ring[:, s, :], ACT.Copy).then_inc(s_xh, 1)

            def split_chunk(c, first, last):
                split_slot(c, 3)
                split_slot(c, 4)
                norm(c, [128] * TT, psA)
                split_slot(c, 5)
                copy_cm(c, CW)
                if not last:
                    split_slot(c + 1, 0)
                unit_of(c, 0, first)
                if not last:
                    split_slot(c + 1, 1)
                    split_slot(c + 1, 2)
                copy_hT(c)

            split_weights(0)
            norm(0, [128], psA)
            copy_cm(0, 128)
            split_weights(1)
            unit(0, vhc[:, :, :], HB)
            nc.scalar.drain()

            vhf = vh[:, :, :, :].rearrange("p k l b -> p k (l b)")

            def put_class():
                nc.scalar.activation(vh[:, :, 1, :], vhc[:, :, :], ACT.Copy)

            def unit_of(c, g, first):
                if first == 0:
                    pos0 = (2 + CL * (NC - 1)) * HB
                else:
                    if first == 1 and g == 1:
                        act.wait_ge(s_conv, 2)
                        put_class()
                    pos0 = (c - 1 - NC * g) * (CL * HB) + 2 * HB
                unit(c, vhf[:, :, ds(pos0, CL * HB)], CL * HB)

            def chunk(c, h, g, first):
                if not (g == 0 and first == 0):
                    norm(c, [128] * TT, psA)
                    copy_cm(c, CW)
                    unit_of(c, g, first)
                copy_hT(c)

            def copy_hT(c):
                act.wait_ge(s_tok_out, c + 1)
                nc.scalar.activation(hT[:, ds(c, 1), :, 0:D].rearrange("p o t f -> p (o t) f"),
                                     stage[0].rearrange("p (t f) -> p t f", t=TT), ACT.Copy).then_inc(s_hT, 1)

            zf = tA[:, :, :].rearrange("p a b -> p (a b)")
            ef = tB[:, :, :].rearrange("p a b -> p (a b)")

            def cols(p):
                return slice(PHASE[p][1] * XW, PHASE[p][2] * XW)

            def silus(p):
                silu_u(p)
                silu_v(p)

            def silu_u(p):
                g, sl = PHASE[p][0], cols(p)
                act.wait_ge(s_conv, p + 1)
                nc.scalar.activation(uz_g[g][:, sl], (uz[:, :], ef)[g][:, sl], ACT.Silu).then_inc(s_silu, 1)

            def silu_v(p):
                g, sl = PHASE[p][0], cols(p)
                nc.scalar.activation(vz_g[g][:, sl], (vz[:, :], zf)[g][:, sl], ACT.Silu)

            def projections(g, which):
                for i in which:
                    k, (kind, blk) = 10 * g + i, PROJ[g][i]
                    act.wait_ge(s_pm, k + 1)
                    sl = slice(blk * XW, (blk + 1) * XW)
                    if kind == 0:
                        nc.scalar.activation(yT[:, sl], psM[k % 2][:, 0:XW], ACT.Copy).then_inc(s_pm_out, 1)
                    else:
                        nc.scalar.activation(zf[:, sl], psM[k % 2][:, 0:XW], ACT.Identity, bias=b2col).then_inc(s_pm_out, 1)

            def abs_z(p):
                nc.scalar.drain()
                nc.scalar.activation(ef[:, cols(p)], zf[:, cols(p)], ACT.Abs)

            def exp_z(p):
                nc.scalar.drain()
                nc.scalar.activation(ef[:, cols(p)], ef[:, cols(p)], ACT.Exp, scale=-1.0)

            def log_z(p):
                nc.scalar.drain()
                nc.scalar.activation(deltaT[:, cols(p)], ef[:, cols(p)], ACT.Ln, bias=onecol).then_inc(s_sp, 1)

            def decay(ks, q):
                act.wait_ge(s_expo, ks + 1)
                v = tA_b[q].rearrange("p (s l) -> p s l", l=L)[:, :, 1:L]
                nc.scalar.activation(v, v, ACT.Exp).then_inc(s_decay, 1)

            def decay_beside(i, j):
                act.wait_ge(s_expo, i * NSP + (NSC + j + 1))
                v = tA_b[j].rearrange("p (s l) -> p s l", l=L)[:, :, 1:L]
                nc.scalar.activation(v, v, ACT.Exp).then_inc(s_decay, 1)

            def fill_scratch():
                act.wait_ge(s_zero_set, 1)
                zv = xsd.bitcast(I32).rearrange("(p r) d -> p (r d)", p=128)
                FW = NXS * RW
                for o1 in range(0, FW, 1024):
                    w = min(1024, FW - o1)
                    act.dma_start(zv[:, o1:o1 + w], fill[:, 0:w]).then_inc(s_zero, 16)

            nc.scalar.drain()
            put_class()
            for s in range(3):
                split_slot(1, s)
            chunk(0, 0, 0, 0)
            split_chunk(1, 1, False)
            with act.Fori(1, NC // 2 - 1) as i:
                split_chunk(i * 2, 2, False)
                split_chunk(i * 2 + 1, 2, False)
            split_chunk(NC - 2, 2, True)
            scan_parameters()
            c = NC - 1
            norm(c, [128] * TT, psA)
            copy_cm(c, CW)
            silus(0)
            unit_of(c, 0, 2)
            copy_hT(c)
            c = NC
            projections(0, range(6))
            abs_z(0)
            exp_z(0)
            norm(c, [128] * TT, psA)
            log_z(0)
            copy_cm(c, CW)
            unit_of(c, 1, 0)
            copy_hT(c)
            c = NC + 1
            norm(c, [128] * TT, psA)
            copy_cm(c, CW)
            silus(1)
            unit_of(c, 1, 1)
            copy_hT(c)
            c = NC + 2
            projections(0, range(6, 10))
            abs_z(1)
            exp_z(1)
            norm(c, [128] * TT, psA)
            copy_cm(c, CW)
            log_z(1)
            unit_of(c, 1, 2)
            copy_hT(c)
            decay(0, 0)

            def chunk_decays(c, first, ks, q):
                decay(ks + 1, 1 - q)
                norm(c, [128] * TT, psA)
                copy_cm(c, CW)
                decay(ks + 2, q)
                unit_of(c, 1, first)
                copy_hT(c)
                decay(ks + 3, 1 - q)

            chunk_decays(NC + 3, 3, 0, 0)
            with act.Fori(NC // 2 + 2, NC) as i:
                for k in range(2):
                    chunk_decays(i * 2 + k, 4, i * (2 * NSP) + (NSP * (k + 1) - (NC // 2 + 2) * 2 * NSP), (k + 1) % 2)
            fill_scratch()
            norm(16, [128] * TT, psA)
            copy_cm(16, CW)
            unit(16, vhf[:, :, (2 + CL * (NC - 1)) * HB:(2 + CL * NC) * HB], CL * HB)
            def out_step(g, i):
                m = 9 * g + i
                if 3 <= i < 12:
                    u, widths = m - 3, widths_of(i - 3)
                    if u >= 2:
                        act.wait_ge(s_xnn, u - 1)
                    norm(u + 17, widths, h2s[u % 2].rearrange("p t d -> p (t d)"), u % 2)
                if 4 <= i < 13:
                    u = m - 4
                    copy_cm(u + 17, sum(widths_of(i - 4)), u % 2)
                if 1 <= i < 10:
                    u, widths = m - 1, widths_of(i - 1)
                    act.wait_ge(s_tm, u + 18)
                    if u >= 2:
                        act.wait_ge(s_h2_st[u % 2], 32 * (u // 2))
                        nc.scalar.drain()
                    nc.scalar.activation(h2s[u % 2][0:widths[0], 0:len(widths), :],
                                         psA[0:widths[0], 0:len(widths) * D].rearrange("p (t d) -> p t d", d=D),
                                         ACT.Copy).then_inc(s_h2, 1)

            def expert_step(g, s, k, do):
                a = s + g * NXG[0]
                if do[0]:
                    if g == 0:
                        e = act.value_load(texp[0:1, ds(a, 1)], min_val=0, max_val=(E - 1) * H)
                        if not (type(a) is int and a < 2):
                            act.wait_ge(s_up, a - 1)
                        nc.scalar.activation(w1e[k % 2], w1_sb[:, ds(e, H)], ACT.Copy).then_inc(s_w1e, 1)
                    act.wait_ge(s_xp, a + 1)
                    nc.scalar.activation(xeT[k % 2], ps[k % 2][:, 0:128], ACT.Copy, scale=gcol).then_inc(s_xp_out, 1)
                if do[1]:
                    b, q = a - 1, (k + 1) % 2
                    act.wait_ge(s_up, b + 1)
                    if not (type(b) is int and b < 2):
                        act.wait_ge(s_dn, b - 1)
                    nc.scalar.activation(hidT[q], ps[2 + q][:, :], ACT.Gelu).then_inc(s_hid, 1)

            for g in range(G):
                def route_exp(b):
                    w = (BATCH[b][2] - BATCH[b][1]) * E
                    act.wait_ge(s_dl, b + 1)
                    nc.scalar.activation(rt[:, 2, 0:w], rt[:, 2, 0:w], ACT.Exp).then_inc(s_ex, 1)

                for i in range(N_OUT):
                    out_step(g, i)
                    if g == 0:
                        if i == 6:
                            silu_u(2)
                        if i == 7:
                            silu_v(2)
                        if i == min(PROJ_AT):
                            act.wait_ge(s_y, 1)
                        projections(1, PROJ_AT.get(i, ()))
                    if g == 1 and i == MASK_AT:
                        route_exp(1)
                if g == 0:
                    route_exp(0)
                    abs_z(2)
                    exp_z(2)
                    log_z(2)
                    for n in range(NPRE):
                        act.wait_ge(s_expo_d, n + 1)
                        v = tA_b[(n - NPRE) % 3].rearrange("p (s l) -> p s l", l=L)[:, :, 1:L]
                        nc.scalar.activation(v, v, ACT.Exp).then_inc(s_decay, 1)
                    decay_beside(0, 0)
                else:
                    route_exp(2)

                def expert_pass(i, nk, first=False, last=False):
                    for k in range(nk):
                        expert_step(g, i * NU + k, k, (1, not first or k >= 1))
                        if g == 0 and k == 3:
                            decay_beside(i, 1)
                            decay_beside(i, 2)
                            if not last:
                                decay_beside(i + 1, 0)

                act.wait_ge(s_ew, 32)
                act.wait_ge(s_zero, 16 * NZ)
                act.wait_ge(s_route, 2 * g + 1)
                expert_pass(0, NU, first=True)
                with act.Fori(1, FULL[g]) as i:
                    expert_pass(i, NU)
                expert_pass(FULL[g], LASTP[g], last=True)
                expert_step(g, NXG[g], LASTP[g], (0, 1))

        @block.vector
        def _(dve):
            def dr():
                nc.vector.drain()

            nc.vector.memset(epsT[:, :], EPS)
            nc.vector.memset(mhalf[:, :], -0.5).then_inc(s_set, 1)
            nc.vector.memset(fill, NO_TOKEN).then_inc(s_zero_set, 1)
            nc.vector.memset(lg[:, :, :], 0.0)
            nc.vector.memset(vh[:, :, 0, :], 0.0)
            nc.vector.memset(vh[:, :, L + 1, :], 0.0)
            dve.wait_ge(s_const, NCONST)
            nc.vector.tensor_tensor(clsp, clscol, posT[:, 0:1], ALU.mult)
            dr()
            nc.vector.tensor_copy(hC[:, :, 0:128], clsp.rearrange("p (o f) -> p o f", o=1).broadcast_to([128, G, 128])).then_inc(s_init, 1)

            def stats(n, widths, src, q=0):
                for t, w in enumerate(widths):
                    nc.vector.bn_stats(bst[q][0:w, t, :], src[0:w, t * D:(t + 1) * D])
                dr()
                for t, w in enumerate(widths):
                    i = nc.vector.bn_aggr(mv[q][0:w, t, :], bst[q][0:w, t, :])
                i.then_inc(s_stat, 1)

            def unit_stats(c):
                dve.wait_ge(s_tm, c + 1)
                stats(c, [128] * TT, psA)

            def chunk(c, h, g, first):
                if not (g == 0 and first == 0):
                    unit_stats(c)
                evacuate(c, h, g)

            def evacuate(c, h, g):
                if not (type(c) is int and c == 0):
                    dve.wait_ge(s_hT, c)
                dve.wait_ge(s_ring_used, 7 * c + 7)
                pv = posT[:, ds(c * CL + (1 - g * NC * CL), CL)].rearrange("p (l o) -> p l o", o=1).broadcast_to([128, CL, GB])
                nc.vector.scalar_tensor_tensor(
                    out=stage[0].rearrange("p (l b) -> p l b", b=GB),
                    in0=psT[h][:, :].rearrange("p (l b) -> p l b", b=GB), scalar=bcol, in1=pv,
                    op0=ALU.add, op1=ALU.mult).then_inc(s_tok_out, 1)

            zf = tA[:, :, :].rearrange("p a b -> p (a b)")
            ef = tB[:, :, :].rearrange("p a b -> p (a b)")

            def conv_part(p, n):
                tap, kind = divmod(n, 2)
                g, l0, l1 = PHASE[p][0], PHASE[p][1] * XL, PHASE[p][2] * XL
                dst, w = ((vz, uz), (zf, ef))[g][kind][:, l0 * HB:l1 * HB], (cwv, cwh)[kind]
                src = vh[:, kind, tap + l0:tap + l1, :].rearrange("p l b -> p (l b)")
                if n == 0:
                    dve.wait_ge(s_vh_out, NC * g + 1 + min(NC, -(-l1 // CL)))
                if tap == 0:
                    i = nc.vector.tensor_scalar(dst, src, w[:, 0:1], None, ALU.mult)
                else:
                    if kind == 0:
                        dr()
                    i = nc.vector.scalar_tensor_tensor(out=dst, in0=src, scalar=w[:, tap:tap + 1],
                                                       in1=dst, op0=ALU.mult, op1=ALU.add)
                if n == 5:
                    i.then_inc(s_conv, 1)

            def cols(p):
                return slice(PHASE[p][1] * XW, PHASE[p][2] * XW)

            def prep_xd(p):
                g, _, b1 = PHASE[p]
                dve.wait_ge(s_pm_out, 10 * g + PROJ[g].index((0, b1 - 1)) + 1)
                nc.vector.transpose(xdT[:, cols(p)], yT[:, cols(p)])

            def softplus(p):
                g, b0, b1 = PHASE[p]
                z, e, delta, du = (v[:, cols(p)] for v in (zf, ef, deltaT, duT))
                dve.wait_ge(s_sp, p + 1)
                nc.vector.tensor_scalar(du, e, 1.0, -1.0, ALU.add, ALU.add)
                dr()
                nc.vector.tensor_tensor(du, e, du, ALU.subtract)
                dr()
                nc.vector.tensor_tensor(du, du, delta, ALU.add)
                dr()
                nc.vector.scalar_tensor_tensor(out=z, in0=z, scalar=0.0, in1=du, op0=ALU.max, op1=ALU.add)
                dr()

            def scan_inputs(p):
                g, b0, b1 = PHASE[p]
                z, e, delta, du = (v[:, cols(p)] for v in (zf, ef, deltaT, duT))
                nc.vector.tensor_tensor(e, z, uz_g[g][:, cols(p)], ALU.mult)
                nc.vector.transpose(delta, z)
                dr()
                if b1 == 5:
                    i = nc.vector.memset(tA[:, :, :].rearrange("p a (s l) -> p (a s) l", l=L)[:, :, 0:1], 0.0)
                    if g == 0:
                        i.then_inc(s_scan, 2)
                    else:
                        nc.vector.memset(tA_b[2].rearrange("p (s l) -> p s l", l=L)[:, :, 0:1], 0.0)
                nc.vector.transpose(du, e).then_inc(s_du, 1)
                dr()

            duv = duT[:, :].rearrange("p (l d) -> p d l", d=32)
            xdv = xdT[:, :].rearrange("p (l r) -> p r l", r=32)
            yv = yT[:, :].rearrange("p (l d) -> p d l", d=32)

            def scan_part(n, ks, q, d0):
                t4 = tB_b[q].rearrange("p (d n l) -> p d n l", d=SD, n=NS)
                du4 = duv[:, ds(d0, SD), :].rearrange("p d (o l) -> p d o l", o=1).broadcast_to([128, SD, NS, L])
                b4 = xdv[:, 8:16, :].rearrange("p (o n) l -> p o n l", o=1).broadcast_to([128, SD, NS, L])
                c4 = xdv[:, 16:24, :].rearrange("p (o n) l -> p o n l", o=1).broadcast_to([128, SD, NS, L])
                if n == 0:
                    nc.vector.tensor_tensor(t4, du4, b4, ALU.mult)
                    return
                dr()
                if n == 1:
                    dve.wait_ge(s_decay, ks + 1)
                    nc.vector.tensor_tensor_scan(tB_b[q], tA_b[q], tB_b[q], 0.0, ALU.mult, ALU.add).then_inc(s_scan, 1)
                if n == 2:
                    nc.vector.tensor_tensor(t4, t4, c4, ALU.mult)
                if n == 3:
                    nc.vector.tensor_reduce(yv[:, ds(d0, SD), :], tB_b[q].rearrange("p (d n l) -> p d l n", d=SD, n=NS),
                                            AX.X, ALU.add)

            def scan(ks, q, d0):
                for n in range(4):
                    scan_part(n, ks, q, d0)

            def expo(n):
                t4 = tA_b[(n - NPRE) % 3].rearrange("p (d n l) -> p d n l", d=SD, n=NS)
                for i in range(SD):
                    d1 = deltaT[:, :].rearrange("p (l d) -> p d l", d=32)[:, SD * n + i:SD * n + i + 1, 1:L].broadcast_to([128, NS, L - 1])
                    a1 = atab[:, :].rearrange("p (d n) -> p d n", n=NS)[:, SD * n + i:SD * n + i + 1, :].rearrange(
                        "p o n -> p n o").broadcast_to([128, NS, L - 1])
                    r = nc.vector.tensor_tensor(t4[:, i, :, 1:L], d1, a1, ALU.mult)
                r.then_inc(s_expo_d, 1)

            def scan_end(g):
                dr()
                nc.vector.transpose(zf, yT[:, :])
                dr()
                nc.vector.scalar_tensor_tensor(out=uz_g[g], in0=uz_g[g], scalar=dcol, in1=zf,
                                               op0=ALU.mult, op1=ALU.add).then_inc(s_y, 1)

            dve.wait_ge(s_tm, 1)
            stats(0, [128], psA)
            def split_weights(half):
                r = slice((KT - 1) // 2 * half, (KT - 1) // 2 * (half + 1))
                dve.wait_ge(s_wh, half + 1)
                nc.vector.tensor_tensor(wl[:, r, :], wt[:, r, :], wh[:, r, :].bitcast(F32), ALU.subtract).then_inc(s_wl, 1)

            def split_slot(c, s):
                dve.wait_ge(s_xh, c * SLOTS + (s - SLOTS + 1))
                nc.vector.tensor_tensor(xl[:, s % NXP, :], ring[:, s, :], xh[:, s % NXP, :].bitcast(F32), ALU.subtract).then_inc(s_xl, 1)

            def split_chunk(c, h, last):
                split_slot(c, 2)
                unit_stats(c)
                for s in range(3, SLOTS):
                    split_slot(c, s)
                if not last:
                    split_slot(c + 1, 0)
                    split_slot(c + 1, 1)
                evacuate(c, h, 0)

            for half in range(2):
                split_weights(half)
            split_slot(1, 0)
            split_slot(1, 1)
            evacuate(0, 0, 0)
            split_chunk(1, 1, False)
            with dve.Fori(1, NC // 2 - 1) as i:
                split_chunk(i * 2, 0, False)
                split_chunk(i * 2 + 1, 1, False)
            split_chunk(NC - 2, 0, True)
            c = NC - 1
            for n in range(6):
                if n == 2:
                    unit_stats(c)
                conv_part(0, n)
            evacuate(c, 1, 0)
            c = NC
            unit_stats(c)
            dve.wait_ge(s_init_a, 1)
            prep_xd(0)
            softplus(0)
            evacuate(c, 0, 1)
            scan_inputs(0)
            c = NC + 1
            unit_stats(c)
            for n in range(6):
                conv_part(1, n)
            evacuate(c, 1, 1)
            c = NC + 2
            unit_stats(c)
            prep_xd(1)
            softplus(1)
            scan_inputs(1)
            evacuate(c, 0, 1)
            c = NC + 3
            unit_stats(c)
            for ks in range(NSP):
                scan(ks, ks % 2, ks * SD)
            evacuate(c, 1, 1)
            with dve.Fori(NC // 2 + 2, NC) as i:
                for k in range(2):
                    unit_stats(i * 2 + k)
                    for j in range(NSP * (k + 1), NSP * (k + 2)):
                        o1 = j - (NC // 2 + 2) * 2 * NSP
                        scan(i * (2 * NSP) + o1, j % 2, i * (2 * NSP * SD) + o1 * SD)
                    evacuate(i * 2 + k, k, 1)
            for ks in range(5 * NSP, NSC):
                for n in range(4):
                    if ks == 5 * NSP and n == 2:
                        dve.wait_ge(s_tm, 17)
                        stats(16, [128] * TT, psA)
                    scan_part(n, ks, ks % 2, ks * SD)
            scan_end(0)

            def out_step(g, i):
                m = 9 * g + i
                if 2 <= i < 11:
                    u = m - 2
                    dve.wait_ge(s_h2, u + 1)
                    stats(u + 17, widths_of(i - 2), h2s[u % 2].rearrange("p t d -> p (t d)"), u % 2)
                if i < 9:
                    w = sum(widths_of(i))
                    dve.wait_ge(s_op, m + 1)
                    if m >= 2:
                        dve.wait_ge(s_tm, m + 16)
                    if i == 0:
                        nc.vector.tensor_tensor(stage[m % 2][:, 0:w], psT[m % 2][:, 0:w], hC[:, g, 0:w], ALU.add).then_inc(s_op_out, 1)
                    else:
                        nc.vector.tensor_tensor(stage[m % 2].rearrange("p (t f) -> p t f", t=TT),
                                                psT[m % 2][:, :].rearrange("p (t f) -> p t f", t=TT),
                                                hT[:, NC * g + i - 1, :, 0:D], ALU.add).then_inc(s_op_out, 1)
                if 3 <= i < 12:
                    u = m - 3
                    dve.wait_ge(s_xn, u + 18)
                    dve.wait_ge(s_rstd2, u + 1)
                    for t, wd in enumerate(widths_of(i - 3)):
                        dst = hC[0:wd, g, 0:D] if i == 3 else hT[:, NC * g + i - 4, t, 0:D]
                        r = nc.vector.tensor_scalar(dst, xn[u % 2][0:wd, t, :], ln[u % 2][0:wd, 5, t:t + 1], None, ALU.mult)
                    r.then_inc(s_xnn, 1)
                if 5 <= i < 14:
                    u, wd = m - 5, widths_of(i - 5)
                    dve.wait_ge(s_lg, u + 1)
                    src = psG[0:wd[0], 0:8 * len(wd)].rearrange("p (t e) -> p t e", e=8)[:, :, 0:E]
                    t0 = 0 if i == 5 else 1 + TT * (i - 6)
                    nc.vector.tensor_copy(lg[0:wd[0], t0:t0 + len(wd), :], src).then_inc(s_lg_out, 1)

            def e_row(c, n, nt):
                return c.rearrange("p (o e) -> p o e", o=1).broadcast_to([c.shape[0], nt, n])

            def batch(b):
                g, t0, t1 = BATCH[b]
                nt = t1 - t0

                def v3(i):
                    return rt[:, i, 0:nt * E].rearrange("p (t e) -> p t e", e=E)

                def over_e(i):
                    return r1[:, i, 0:nt].rearrange("p (t o) -> p t o", o=1).broadcast_to([128, nt, E])

                return g, t0, t1, nt, v3, over_e

            def route_mask(b):
                g, t0, t1, nt, v3, over_e = batch(b)
                e8b = e_row(cst[:, C_E8:C_E8 + E], E, nt)
                dr()
                nc.vector.tensor_reduce(r1[:, 0, 0:nt], lg[:, t0:t1, :], AX.X, ALU.max)
                dr()
                nc.vector.tensor_tensor(v3(2), lg[:, t0:t1, :], over_e(0), ALU.subtract).then_inc(s_dl, 1)
                nc.vector.tensor_tensor(v3(1), lg[:, t0:t1, :], over_e(0), ALU.is_ge)
                dr()
                nc.vector.scalar_tensor_tensor(out=v3(1), in0=v3(1), scalar=-8.0, in1=e8b, op0=ALU.mult, op1=ALU.add)
                dr()
                nc.vector.tensor_reduce(r1[:, 1, 0:nt], v3(1), AX.X, ALU.min)
                dr()
                i = nc.vector.tensor_tensor(v3(0), v3(1), over_e(1), ALU.is_equal)
                if t0 == 0:
                    dr()
                    i = nc.vector.memset(rt[GB:128, 0, 0:E], 0.0)
                i.then_inc(s_mask, 1)
                dr()

            def route_gate(b):
                g, t0, t1, nt, v3, over_e = batch(b)
                nc.vector.tensor_scalar(v3(1), v3(0), -1.0, 1.0, ALU.mult, ALU.add)
                dve.wait_ge(s_ex, b + 1)
                nc.vector.tensor_reduce(r1[:, 2, 0:nt], v3(2), AX.X, ALU.add)
                dr()
                nc.vector.reciprocal(r1[:, 3, 0:nt], r1[:, 2, 0:nt])
                dr()
                nc.vector.tensor_tensor(v3(2), v3(2), over_e(3), ALU.mult)
                dr()
                nc.vector.tensor_reduce(r1[:, 4, 0:nt], v3(2), AX.X, ALU.max)
                nc.vector.tensor_tensor(v3(1), v3(1), v3(2), ALU.mult)
                dve.wait_ge(s_rank, b + 1)
                nc.vector.tensor_copy(rt[:, 3, 0:nt * E], psM[1][:, 0:nt * E])
                dr()
                nc.vector.tensor_copy(rt[:, 2, 0:nt * E], psM[0][:, 0:nt * E]).then_inc(s_rank_out, 1)
                nc.vector.tensor_reduce(r1[:, 5, 0:nt], v3(1), AX.X, ALU.max)
                for e in range(E):
                    nc.vector.tensor_tensor_scan(rt[:, 4, e * nt:(e + 1) * nt], ones_sq[:, 0:nt], v3(3)[:, :, e],
                                                 0.0, ALU.mult, ALU.add)

            def route_slots(b):
                g, t0, t1, nt, v3, over_e = batch(b)
                nx = NXB[b]
                by_e = lambda i: rt[:, i, 0:nt * E].rearrange("p (e t) -> p e t", e=E)
                dr()
                nc.vector.tensor_tensor(by_e(5), by_e(4)[:, :, nt - 1:nt].broadcast_to([128, E, nt]),
                                        cst[:, C_K128:C_K128 + nt].rearrange("p (o t) -> p o t", o=1).broadcast_to([128, E, nt]),
                                        ALU.is_gt)
                nc.vector.tensor_tensor(r1[:, 5, 0:nt], r1[:, 5, 0:nt], r1[:, 4, 0:nt], ALU.add)
                nc.vector.tensor_tensor(v3(3), rt[:, 4, 0:nt * E].rearrange("p (e t) -> p t e", e=E), v3(3), ALU.subtract)
                dr()
                nc.vector.tensor_reduce(tiles[:, 0, :], by_e(5), AX.X, ALU.add)
                nc.vector.tensor_scalar(r1[:, 5, 0:nt], r1[:, 5, 0:nt], GATE_EPS, None, ALU.add)
                nc.vector.tensor_tensor(v3(3), v3(3), v3(2), ALU.add)
                dr()
                nc.vector.tensor_tensor_scan(tiles[:, 1, :], ones_sq[:, 0:E], tiles[:, 0, :], 0.0, ALU.mult, ALU.add)
                nc.vector.reciprocal(r1[:, 6, 0:nt], r1[:, 5, 0:nt])
                dr()
                nc.vector.tensor_tensor(tiles[:, 2, :], tiles[:, 1, :], tiles[:, 0, :], ALU.subtract)
                jv = cst[0:1, C_J:C_J + nx].rearrange("p (j o) -> p j o", o=1).broadcast_to([1, nx, E])
                cmp = tcmp[:, 0:nx * E].rearrange("p (j e) -> p j e", e=E)
                nc.vector.tensor_tensor(cmp, e_row(tiles[0:1, 1, :], E, nx), jv, ALU.is_le)
                chunks = hT[:, NC * g:NC * g + NC, :, :].rearrange("p c t f -> p (c t) f")
                first = max(t0, 1)
                if t0 == 0:
                    nc.vector.tensor_tensor(hC[:, g, D:D + 1], r1[:, 4, 0:1], r1[:, 6, 0:1], ALU.mult)
                    nc.vector.tensor_scalar(hC[:, g, D + 1:D + 2].bitcast(I32), cst[:, C_TOK:C_TOK + 1], float(g * GB * L), None, ALU.add)
                nc.vector.tensor_tensor(chunks[:, first - 1:t1 - 1, D], r1[:, 4, first - t0:nt], r1[:, 6, first - t0:nt], ALU.mult)
                nc.vector.tensor_scalar(chunks[:, first - 1:t1 - 1, D + 1].bitcast(I32), cst[:, C_TOK + first:C_TOK + t1],
                                        float(g * GB * L), None, ALU.add)
                dr()
                nc.vector.tensor_reduce(tsum[:, 0:nx], cmp, AX.X, ALU.add)
                nc.vector.scalar_tensor_tensor(out=v3(5), in0=e_row(tiles[:, 2, :], E, nt),
                                               scalar=128.0, in1=v3(3), op0=ALU.mult, op1=ALU.add)
                dr()
                nc.vector.tensor_scalar(texp[:, BASE[b]:BASE[b] + nx], tsum[:, 0:nx], float(E - 1), float(H), ALU.min, ALU.mult)
                nc.vector.tensor_tensor(v3(5), v3(5), v3(0), ALU.mult)
                dr()
                nc.vector.tensor_reduce(r1[:, 7, 0:nt], v3(5), AX.X, ALU.add)
                dr()
                nc.vector.tensor_scalar(slot[:, g, t0:t1], r1[:, 7, 0:nt], float(BASE[b] * 128), None, ALU.add).then_inc(s_route, 1)

            def expert_step(g, s, k, do):
                a = s + g * NXG[0]
                if g == 1 and do[0]:
                    e = dve.value_load(texp[0:1, ds(a, 1)], min_val=0, max_val=(E - 1) * H)
                    dve.wait_ge(s_up, a - 1)
                    nc.vector.tensor_copy(w1e[k % 2], w1_sb[:, ds(e, H)]).then_inc(s_w1e, 1)
                if do[1]:
                    j = (k - 2) % NU
                    dve.wait_ge(s_dn, a - 1)
                    nc.vector.tensor_scalar(ys_sb[:, j, :], ps[4 + k % 2][:, 0:D], xs_sb[:, j, D:D + 1], None,
                                            ALU.mult).then_inc(s_dn_out, 1)

            for g in range(G):
                for i in range(N_OUT):
                    out_step(g, i)
                    if g == 0 and i < 6:
                        conv_part(2, i)
                    if g == 0 and i == 11:
                        prep_xd(2)
                    if g == 1 and i == MASK_AT:
                        route_mask(1)
                    if g == 1 and i == GATE_AT:
                        route_gate(1)
                    if g == 1 and i == SLOT_AT:
                        route_slots(1)
                route_mask(2 * g)
                route_gate(2 * g)
                route_slots(2 * g)
                if g == 0:
                    softplus(2)
                    scan_inputs(2)
                    for n in range(3):
                        expo(n)
                    for n in range(NPRE):
                        scan(NSC + n, (n - NPRE) % 3, n * SD)
                        if n + 3 < NPRE:
                            expo(n + 3)

                def expert_pass(i, nk, first=False):
                    for k in range(nk):
                        expert_step(g, i * NU + k, k, (1, not first or k >= 2))
                        if g == 0:
                            for j, n in scan_parts(k, nk):
                                scan_part(n, i * NSP + (NSC + NPRE + j), j, i * (NSP * SD) + (NPRE + j) * SD)

                dve.wait_ge(s_route, 2 * g + 1)
                dve.wait_ge(s_ew, 32)
                expert_pass(0, NU, first=True)
                with dve.Fori(1, FULL[g]) as i:
                    expert_pass(i, NU)
                expert_pass(FULL[g], LASTP[g])
                for k in range(2):
                    expert_step(g, NXG[g] + k, LASTP[g] + k, (0, 1))
                if g == 0:
                    scan_end(1)

        @block.gpsimd
        def _(pool):
            def norm(n, nt, second, q=0):
                pool.wait_ge(s_stat, n + 1)
                v = slice(0, nt)
                ln, mv = ln_a[:, q], mv_a[:, q]
                nc.gpsimd.tensor_tensor(ln[:, 0, v], mv[:, v, 1], epsT[:, v], ALU.add)
                nc.gpsimd.tensor_scalar(ln[:, 1, v], mv[:, v, 0], -1.0, None, ALU.mult)
                nc.gpsimd.drain()
                nc.gpsimd.tensor_tensor(ln[:, 2, v], ln[:, 0, v], mhalf[:, v], ALU.pow)
                nc.gpsimd.drain()
                nc.gpsimd.tensor_tensor(ln[:, 3, v], ln[:, 1, v], ln[:, 2, v], ALU.mult).then_inc(s_rstd, 1)
                if second:
                    nc.gpsimd.tensor_tensor(ln[:, 4, v], ln[:, 2, v], ln[:, 2, v], ALU.mult)
                    nc.gpsimd.drain()
                    nc.gpsimd.tensor_tensor(ln[:, 4, v], ln[:, 4, v], mv[:, v, 1], ALU.mult)
                    nc.gpsimd.drain()
                    nc.gpsimd.tensor_scalar(ln[:, 4, v], ln[:, 4, v], EPS, None, ALU.add)
                    nc.gpsimd.drain()
                    nc.gpsimd.tensor_tensor(ln[:, 5, v], ln[:, 4, v], mhalf[:, v], ALU.pow).then_inc(s_rstd2, 1)

            dv = deltaT[:, :].rearrange("p (l d) -> p d l", d=32)
            av = atab[:, :].rearrange("p (d n) -> p d n", n=NS)

            def expo(ks, q, d0):
                pool.wait_ge(s_scan, ks + 1)
                expo_into(tA_b[q], d0)

            def expo_into(buf, d0):
                t4 = buf.rearrange("p (d n l) -> p d n l", d=SD, n=NS)
                for i in range(SD):
                    d1 = dv[:, ds(d0 + i, 1), 1:L].broadcast_to([128, NS, L - 1])
                    a1 = av[:, ds(d0 + i, 1), :].rearrange("p o n -> p n o").broadcast_to([128, NS, L - 1])
                    r = nc.gpsimd.tensor_tensor(t4[:, i, :, 1:L], d1, a1, ALU.mult)
                r.then_inc(s_expo, 1)

            last_token = nc.gpsimd.to_reg(B * L - 1)
            pool.wait_ge(s_set, 1)
            norm(0, 1, False)
            norm(1, TT, False)
            with pool.Fori(2, NC) as n:
                norm(n, TT, False)
            for n in range(NC, NC + 3):
                norm(n, TT, False)
            pool.wait_ge(s_du, 2)
            pool.wait_ge(s_init_a, 1)
            expo(0, 0, 0)
            expo(1, 1, SD)
            norm(NC + 3, TT, False)
            for ks in range(2, NSP + 1):
                expo(ks, ks % 2, ks * SD)
            with pool.Fori(NC // 2 + 2, NC) as i:
                for k in range(2):
                    for j in range(1, NSP + 1):
                        if j == 2:
                            norm(i * 2 + k, TT, False)
                        o1 = NSP * (k + 1) + j - (NC // 2 + 2) * 2 * NSP
                        expo(i * (2 * NSP) + o1, (k + 1 + j) % 2, i * (2 * NSP * SD) + o1 * SD)
            norm(2 * NC, TT, False)

            for g in range(G):
                for j in range(9):
                    m = 9 * g + j
                    norm(17 + m, len(widths_of(j)), True, m % 2)
                def scatter(b, t):
                    src = hC[0:GB, g, :] if t == 0 else hT[:, NC * g + (t - 1) // TT, (t - 1) % TT, :]
                    idx = slot[0:GB, g, 0:1] if t == 0 else slot[:, g, t:t + 1]
                    nc.gpsimd.indirect_dma_start(out=xsd, out_offset=bass.IndirectOffsetOnAxis(ap=idx, axis=0),
                                                 in_=src, in_offset=None).then_inc(s_scat[b], 16)

                pool.wait_ge(s_route, g + 1)
                pool.wait_ge(s_zero, 16 * NZ)
                for t in range(BATCH[g][1], BATCH[g][2]):
                    scatter(g, t)
                for q in range(2):
                    pool.wait_ge(s_h2_st[q], 32 * ((9 * (g + 1) - q + 1) // 2))

                def add(a, k):
                    pool.wait_ge(s_dn_out, a + 1)
                    nc.gpsimd.nop(nofuse=True)
                    nc.gpsimd.indirect_dma_start(out=out.rearrange("b l d -> (b l) d"),
                                                 out_offset=bass.IndirectOffsetOnAxis(ap=xs_sb[:, k, D + 1:D + 2].bitcast(I32), axis=0),
                                                 in_=ys_sb[:, k, :], in_offset=None, bounds_check=last_token,
                                                 oob_is_err=False, compute_op=ALU.add).then_inc(s_add[k // 2], 16)

                def expo_beside(i, j):
                    pool.wait_ge(s_scan, i * NSP + (NSC + NPRE + j))
                    expo_into(tA_b[j], i * (NSP * SD) + (NPRE + j) * SD)

                if g == 0:
                    pool.wait_ge(s_du, 3)
                    for j in range(NSP):
                        expo_beside(0, j)

                LAG = 4

                def expert_pass(i, nk, first=False, last=False):
                    for k in range(nk):
                        if g == 1 and first:
                            if k == 0:
                                pool.wait_ge(s_route, 3)
                            for t in range(BATCH[2][1] + k * per, min(BATCH[2][1] + (k + 1) * per, NT)):
                                scatter(2, t)
                        if not (first and k < LAG):
                            add(i * NU + (g * NXG[0] + k - LAG), (k - LAG) % NU)
                        if g == 0 and k in (1, 5, 8) and not last:
                            expo_beside(i + 1, (1, 5, 8).index(k))

                per = -(-(BATCH[2][2] - BATCH[2][1]) // NU)
                expert_pass(0, NU, first=True)
                with pool.Fori(1, FULL[g]) as i:
                    expert_pass(i, NU)
                expert_pass(FULL[g], LASTP[g], last=True)
                for a in range(NXG[g] - LAG, NXG[g]):
                    add(g * NXG[0] + a, a % NU)


def kernel(**inputs):
    import numpy as np
    import concourse.bacc as bacc
    from concourse.bass_utils import run_bass_kernel_spmd as run

    a = {k: np.asarray(v) for k, v in inputs.items()}

    def cc(v):
        return np.ascontiguousarray(v)

    x = a["x"].reshape(G, GB, C, NP, PATCH, NP, PATCH).transpose(2, 4, 6, 0, 3, 5, 1).reshape(K, B * (L - 1))
    top = (KT - 1) * 128
    x_main = x[:top].reshape(SLOTS, SK, 128, G * NC, CW).transpose(3, 0, 2, 1, 4).reshape(G * NC, SLOTS, 128, SK * CW)
    x_rem = x[top:].reshape(KR, G * NC, CW).transpose(1, 0, 2)
    w = a["L0_tok_W"].T
    consts = np.zeros((128, C_N), np.float32)
    consts[:, C_ID:C_ID + 128] = np.eye(128)
    consts[:, C_TRI:C_TRI + 128] = np.triu(np.ones((128, 128)), 1)
    consts[:, C_ONE:C_ONE + 128] = 1.0
    consts[:, C_E8:C_E8 + E] = np.arange(E)
    consts[:, C_K128:C_K128 + NT] = np.arange(NT) * 128.0
    consts[:, C_J:C_J + NX] = np.arange(NX)
    p, t = np.arange(128)[:, None], np.arange(NT)[None, :]
    consts[:, C_TOK:C_TOK + NT] = p % GB * L + np.where(t == 0, 0, 2 * t - 1 + p // GB)
    halves = lambda v: np.concatenate([v, v]).reshape(D, -1)
    col = [np.zeros((D, 1), np.float32)] * 14
    col[0], col[1] = a["L0_tok_b"].reshape(D, 1), a["L0_tok_class_token"].reshape(D, 1)
    col[2], col[3] = halves(a["L0_attn_dt_proj_b"]), halves(a["L0_attn_D_param"])
    col[4], col[5] = a["L0_ffn_gamma"].reshape(D, 1), np.ones((D, 1), np.float32)
    cv, ch = halves(a["L0_attn_conv_v_w"].reshape(CH, 3)), halves(a["L0_attn_conv_hs_w"].reshape(CH, 3))
    early = cc(np.concatenate(col[:8] + [cv, ch, a["L0_tok_pos_embed"].T, a["L0_attn_in_proj_w"].T], axis=1))
    late = np.zeros((D, Q_N), np.float32)
    al = a["L0_attn_A_log"].reshape(2, 32 * NS)
    for half in range(2):
        r = slice(CH * half, CH * half + CH)
        for dh in range(2):
            q = CH * half + 32 * dh
            late[r, Q_XD + q:Q_XD + q + 24] = a["L0_attn_hs_proj_w"].T
            late[q:q + 32, Q_A:] = al[dh]
        late[CH * half:CH * half + 8, Q_DT + CH * half:Q_DT + CH * half + CH] = a["L0_attn_dt_proj_w"].T
        for i in range(2):
            late[r, Q_WO + (2 * half + i) * D:Q_WO + (2 * half + i + 1) * D] = a["L0_attn_out_proj_w"].T[CH * i:CH * i + CH]
    late[:, Q_WG:Q_WG + E] = a["L0_ffn_w_gating"]
    arrays = {
        "x_main": cc(x_main), "x_rem": cc(x_rem),
        "w_main": cc(w[:top].reshape(KT - 1, 128, D).transpose(1, 0, 2)), "w_rem": cc(w[top:]),
        "early": early, "late": late,
        "w1": cc(a["L0_ffn_w1"].transpose(1, 0, 2)),
        "w2": cc(a["L0_ffn_w2"].reshape(E * (H // 128), 128, D).transpose(1, 0, 2)),
        "consts": consts,
    }
    nc = bacc.Bacc("TRN2", target_bir_lowering=False, num_devices=1)
    args = [nc.dram_tensor(n, v.shape, mybir.dt.from_np(v.dtype), kind="ExternalInput").ap() for n, v in arrays.items()]
    res = nc.dram_tensor("tokens_out", (B, L, D), F32, kind="ExternalOutput").ap()
    tower(nc, *args, res)
    r = run(nc, [arrays], core_ids=[0])
    return r.results[0]["tokens_out"]
```
